# Optimizing a Trainium2 kernel written in Bass

```python
import numpy as np
import jax
import jax.numpy as jnp

def _softmax(x, axis=-1):
    return jax.nn.softmax(x, axis=axis)

def _gelu(x):
    return jax.nn.gelu(x, approximate=True)

def _silu(x):
    return jax.nn.silu(x)

def _sigmoid(x):
    return jax.nn.sigmoid(x)

def _layernorm(x, axis=-1, eps=1e-05):
    m = jnp.mean(x, axis=axis, keepdims=True)
    v = jnp.var(x, axis=axis, keepdims=True)
    return (x - m) / jnp.sqrt(v + eps)

def _scatter_add(tgt, idx, src, axis=0):
    return tgt.at[idx].add(src)

def _segment_sum(src, seg, n):
    return jax.ops.segment_sum(src, seg, n)
kernel_name = 'mk_adaln_d1_jaxref_r4_6833bc'

def setup_inputs(seed: int=0):
    np.random.seed(seed)
    _w = jnp.asarray

    def _L0_attn_setup():
        import jax, jax.numpy as jnp
        import numpy as np
        D_MODEL = 256
        D_STATE = 128
        D_CONV = 4
        HEADDIM = 64
        EXPAND = 2
        NGROUPS = 1
        CHUNK = 64
        D_INNER = EXPAND * D_MODEL
        NHEADS = D_INNER // HEADDIM
        CONV_DIM = D_INNER + 2 * NGROUPS * D_STATE
        D_IN_PROJ = 2 * D_INNER + 2 * NGROUPS * D_STATE + NHEADS
        EPS = 1e-05

        def _causal_dwconv(x, w, b):
            xp = jnp.pad(x, ((0, 0), (D_CONV - 1, 0), (0, 0))).transpose(0, 2, 1)
            y = jax.lax.conv_general_dilated(xp, w[:, None, :], window_strides=(1,), padding='VALID', dimension_numbers=('NCH', 'OIH', 'NCH'), feature_group_count=w.shape[0])
            return y.transpose(0, 2, 1) + b

        def _ssd(x, dt, A, Bm, Cm):
            b, l, h, p = x.shape
            g, n = (Bm.shape[2], Bm.shape[3])
            nc = l // CHUNK
            xc = x.reshape(b, nc, CHUNK, h, p)
            dtc = dt.reshape(b, nc, CHUNK, h)
            Bc = jnp.repeat(Bm.reshape(b, nc, CHUNK, g, n), h // g, axis=3)
            Cc = jnp.repeat(Cm.reshape(b, nc, CHUNK, g, n), h // g, axis=3)
            dA = dtc * A
            dA_cs = jnp.cumsum(dA, axis=2)
            xt = xc * dtc[..., None]
            diff = dA_cs[:, :, :, None, :] - dA_cs[:, :, None, :, :]
            causal = jnp.tril(jnp.ones((CHUNK, CHUNK), bool))[None, None, :, :, None]
            Lmat = jnp.where(causal, jnp.exp(diff), 0.0)
            scores = jnp.einsum('bcihn,bcjhn->bcijh', Cc, Bc) * Lmat
            y_diag = jnp.einsum('bcijh,bcjhp->bcihp', scores, xt)
            decay_states = jnp.exp(dA_cs[:, :, -1:, :] - dA_cs)
            states = jnp.einsum('bcjhn,bcjh,bcjhp->bchpn', Bc, decay_states, xt)
            chunk_decay = jnp.exp(dA_cs[:, :, -1, :])

            def step(s_prev, inp):
                cd, st = inp
                return (cd[:, :, None, None] * s_prev + st, s_prev)
            init = jnp.zeros((b, h, p, n), x.dtype)
            _, prev_states = jax.lax.scan(step, init, (jnp.moveaxis(chunk_decay, 1, 0), jnp.moveaxis(states, 1, 0)))
            prev_states = jnp.moveaxis(prev_states, 0, 1)
            y_off = jnp.einsum('bcihn,bcih,bchpn->bcihp', Cc, jnp.exp(dA_cs), prev_states)
            return (y_diag + y_off).reshape(b, l, h, p)
        key = jax.random.key(seed)
        ks = jax.random.split(key, 9)
        B, L = (1, 1024)
        hidden_states = jax.random.normal(ks[0], (B, L, D_MODEL), jnp.float32)
        W_in = jax.random.normal(ks[1], (D_MODEL, D_IN_PROJ), jnp.float32) * D_MODEL ** (-0.5)
        conv_w = jax.random.normal(ks[2], (CONV_DIM, D_CONV), jnp.float32) * D_CONV ** (-0.5)
        conv_b = jnp.zeros((CONV_DIM,), jnp.float32)
        dt = jnp.exp(jax.random.uniform(ks[3], (NHEADS,), jnp.float32) * (np.log(0.1) - np.log(0.001)) + np.log(0.001))
        dt_bias = dt + jnp.log(-jnp.expm1(-dt))
        A_log = jnp.log(jax.random.uniform(ks[4], (NHEADS,), jnp.float32) * 15.0 + 1.0)
        D = jax.random.normal(ks[5], (NHEADS,), jnp.float32)
        norm_w = jnp.ones((D_INNER,), jnp.float32)
        W_out = jax.random.normal(ks[6], (D_INNER, D_MODEL), jnp.float32) * D_INNER ** (-0.5)
        return {'hidden_states': hidden_states, 'W_in': W_in, 'conv_w': conv_w, 'conv_b': conv_b, 'dt_bias': dt_bias, 'A_log': A_log, 'D': D, 'norm_w': norm_w, 'W_out': W_out}
    _L0_attn_in = _L0_attn_setup()

    def _L0_ffn_setup():
        import jax, jax.numpy as jnp
        import numpy as np
        THRESHOLD = 0.1
        key = jax.random.key(seed)
        k1, k2, k3 = jax.random.split(key, 3)
        B, S, D, E = (4, 1024, 256, 8)
        inputs = jax.random.normal(k1, (B, S, D), dtype=jnp.float32)
        gate_w = jax.random.normal(k2, (D, E), dtype=jnp.float32) * 0.02
        gate_b = jnp.zeros((E,), dtype=jnp.float32)
        expert_w = jax.random.normal(k3, (E, D, D), dtype=jnp.float32) * 0.02
        expert_b = jnp.zeros((E, D), dtype=jnp.float32)
        return {'inputs': inputs, 'gate_w': gate_w, 'gate_b': gate_b, 'expert_w': expert_w, 'expert_b': expert_b}
    _L0_ffn_in = _L0_ffn_setup()
    _L0_c = _w((lambda *s: np.random.randn(*s).astype(np.float32) * 0.05)(8, 256))
    _L0_wmod = _w((lambda *s: np.random.randn(*s).astype(np.float32) * 0.05)(256, 6 * 256) * 256 ** (-0.5))
    _d = {'L0_attn_hidden_states': _L0_attn_in['hidden_states'], 'L0_attn_W_in': _L0_attn_in['W_in'], 'L0_attn_conv_w': _L0_attn_in['conv_w'], 'L0_attn_conv_b': _L0_attn_in['conv_b'], 'L0_attn_dt_bias': _L0_attn_in['dt_bias'], 'L0_attn_A_log': _L0_attn_in['A_log'], 'L0_attn_D': _L0_attn_in['D'], 'L0_attn_norm_w': _L0_attn_in['norm_w'], 'L0_attn_W_out': _L0_attn_in['W_out'], 'L0_ffn_gate_w': _L0_ffn_in['gate_w'], 'L0_ffn_gate_b': _L0_ffn_in['gate_b'], 'L0_ffn_expert_w': _L0_ffn_in['expert_w'], 'L0_ffn_expert_b': _L0_ffn_in['expert_b'], 'L0_c': _L0_c, 'L0_wmod': _L0_wmod}
    _x0 = _d['L0_attn_hidden_states']
    _d['L0_attn_hidden_states'] = jax.random.normal(jax.random.fold_in(jax.random.key(seed), 1), (8, 2048, 256), dtype=_x0.dtype)
    del _x0
    return _d

def reference(L0_attn_hidden_states, L0_attn_W_in, L0_attn_conv_w, L0_attn_conv_b, L0_attn_dt_bias, L0_attn_A_log, L0_attn_D, L0_attn_norm_w, L0_attn_W_out, L0_ffn_gate_w, L0_ffn_gate_b, L0_ffn_expert_w, L0_ffn_expert_b, L0_c, L0_wmod):

    def _L0_attn_ref(hidden_states, W_in, conv_w, conv_b, dt_bias, A_log, D, norm_w, W_out):
        import jax, jax.numpy as jnp
        import numpy as np
        D_MODEL = 256
        D_STATE = 128
        D_CONV = 4
        HEADDIM = 64
        EXPAND = 2
        NGROUPS = 1
        CHUNK = 64
        D_INNER = EXPAND * D_MODEL
        NHEADS = D_INNER // HEADDIM
        CONV_DIM = D_INNER + 2 * NGROUPS * D_STATE
        D_IN_PROJ = 2 * D_INNER + 2 * NGROUPS * D_STATE + NHEADS
        EPS = 1e-05

        def _causal_dwconv(x, w, b):
            xp = jnp.pad(x, ((0, 0), (D_CONV - 1, 0), (0, 0))).transpose(0, 2, 1)
            y = jax.lax.conv_general_dilated(xp, w[:, None, :], window_strides=(1,), padding='VALID', dimension_numbers=('NCH', 'OIH', 'NCH'), feature_group_count=w.shape[0])
            return y.transpose(0, 2, 1) + b

        def _ssd(x, dt, A, Bm, Cm):
            b, l, h, p = x.shape
            g, n = (Bm.shape[2], Bm.shape[3])
            nc = l // CHUNK
            xc = x.reshape(b, nc, CHUNK, h, p)
            dtc = dt.reshape(b, nc, CHUNK, h)
            Bc = jnp.repeat(Bm.reshape(b, nc, CHUNK, g, n), h // g, axis=3)
            Cc = jnp.repeat(Cm.reshape(b, nc, CHUNK, g, n), h // g, axis=3)
            dA = dtc * A
            dA_cs = jnp.cumsum(dA, axis=2)
            xt = xc * dtc[..., None]
            diff = dA_cs[:, :, :, None, :] - dA_cs[:, :, None, :, :]
            causal = jnp.tril(jnp.ones((CHUNK, CHUNK), bool))[None, None, :, :, None]
            Lmat = jnp.where(causal, jnp.exp(diff), 0.0)
            scores = jnp.einsum('bcihn,bcjhn->bcijh', Cc, Bc) * Lmat
            y_diag = jnp.einsum('bcijh,bcjhp->bcihp', scores, xt)
            decay_states = jnp.exp(dA_cs[:, :, -1:, :] - dA_cs)
            states = jnp.einsum('bcjhn,bcjh,bcjhp->bchpn', Bc, decay_states, xt)
            chunk_decay = jnp.exp(dA_cs[:, :, -1, :])

            def step(s_prev, inp):
                cd, st = inp
                return (cd[:, :, None, None] * s_prev + st, s_prev)
            init = jnp.zeros((b, h, p, n), x.dtype)
            _, prev_states = jax.lax.scan(step, init, (jnp.moveaxis(chunk_decay, 1, 0), jnp.moveaxis(states, 1, 0)))
            prev_states = jnp.moveaxis(prev_states, 0, 1)
            y_off = jnp.einsum('bcihn,bcih,bchpn->bcihp', Cc, jnp.exp(dA_cs), prev_states)
            return (y_diag + y_off).reshape(b, l, h, p)
        b, l, _ = hidden_states.shape
        zxbcdt = hidden_states @ W_in
        z = zxbcdt[..., :D_INNER]
        xBC = zxbcdt[..., D_INNER:D_INNER + CONV_DIM]
        dt = zxbcdt[..., D_INNER + CONV_DIM:]
        xBC = jax.nn.silu(_causal_dwconv(xBC, conv_w, conv_b))
        x = xBC[..., :D_INNER].reshape(b, l, NHEADS, HEADDIM)
        Bm = xBC[..., D_INNER:D_INNER + NGROUPS * D_STATE].reshape(b, l, NGROUPS, D_STATE)
        Cm = xBC[..., D_INNER + NGROUPS * D_STATE:].reshape(b, l, NGROUPS, D_STATE)
        dt = jax.nn.softplus(dt + dt_bias)
        A = -jnp.exp(A_log)
        y = _ssd(x, dt, A, Bm, Cm) + x * D[None, None, :, None]
        y = y.reshape(b, l, D_INNER)
        y = y * jax.nn.silu(z)
        y = y * jax.lax.rsqrt(jnp.mean(y * y, axis=-1, keepdims=True) + EPS) * norm_w
        return y @ W_out

    def _L0_ffn_ref(inputs, gate_w, gate_b, expert_w, expert_b):
        import jax, jax.numpy as jnp
        import numpy as np
        THRESHOLD = 0.1
        d = inputs.shape[-1]
        x = inputs.reshape(-1, d)
        gate_logits = jax.nn.softmax(x @ gate_w + gate_b, axis=-1)
        selected = (gate_logits >= THRESHOLD).astype(x.dtype)
        weights = gate_logits * selected
        wsum = jnp.sum(weights, axis=-1, keepdims=True)
        weights = weights / jnp.where(wsum == 0, jnp.ones_like(wsum), wsum)
        E = expert_w.shape[0]
        out = jnp.zeros((x.shape[0], expert_w.shape[-1]), dtype=x.dtype)
        for e in range(E):
            out = out + weights[:, e:e + 1] * (x @ expert_w[e] + expert_b[e])
        return out.reshape(*inputs.shape[:-1], out.shape[-1])
    x = L0_attn_hidden_states
    mod = (_silu(L0_c) @ L0_wmod).reshape(L0_c.shape[0], 6, 1, -1)
    sa, ca, ga, sb, cb, gb = (mod[:, 0], mod[:, 1], mod[:, 2], mod[:, 3], mod[:, 4], mod[:, 5])
    ga = (2 * (ga >= 0) - 1) * jnp.maximum(jnp.abs(ga), 0.25)
    gb = (2 * (gb >= 0) - 1) * jnp.maximum(jnp.abs(gb), 0.25)
    h = _layernorm(x, axis=-1) * (1 + ca) + sa
    x = x + ga * _L0_attn_ref(h, L0_attn_W_in, L0_attn_conv_w, L0_attn_conv_b, L0_attn_dt_bias, L0_attn_A_log, L0_attn_D, L0_attn_norm_w, L0_attn_W_out)
    h = _layernorm(x, axis=-1) * (1 + cb) + sb
    x = x + gb * _L0_ffn_ref(h, L0_ffn_gate_w, L0_ffn_gate_b, L0_ffn_expert_w, L0_ffn_expert_b)
    return x

_drawn_inputs = setup_inputs


def setup_inputs(seed=0):
    import zlib

    import numpy as np

    out = dict(_drawn_inputs(seed))
    spreads = {'L0_attn_conv_b': (0.0, 0.1),
     'L0_attn_norm_w': (1.0, 0.2),
     'L0_ffn_gate_b': (0.0, 0.755),
     'L0_ffn_expert_b': (0.0, 0.735)}
    factors = {'L0_ffn_gate_w': 2.794}
    for name, (base, spread) in spreads.items():
        noise = np.random.default_rng([zlib.crc32(name.encode()), seed]).standard_normal(out[name].shape)
        drawn = base * np.exp(spread * noise) if base else spread * noise
        out[name] = jnp.asarray(drawn.astype(out[name].dtype))
    for name, factor in factors.items():
        out[name] = (out[name] * factor).astype(out[name].dtype)
    return out
```

```python
from contextlib import ExitStack

import numpy as np

import concourse.bass as bass
from concourse import mybir

ALU = mybir.AluOpType
ACT = mybir.ActivationFunctionType
AX = mybir.AxisListType
F32 = mybir.dt.float32
F32R = mybir.dt.float32r
BF16 = mybir.dt.bfloat16

P = 128


class Stage:

    def __init__(self, sem, steps):
        self.sem = sem
        self.n = len(steps)
        self.at = {name: i + 1 for i, name in enumerate(steps)}
        assert len(self.at) == self.n
        self.said = 0

    def done(self, name, instruction):
        assert self.at[name] == self.said % self.n + 1, (name, self.said)
        self.said += 1
        return instruction.then_inc(self.sem, 1)

    def after(self, eng, name, run):
        value = run * self.n + self.at[name]
        if not isinstance(value, int) or value > 0:
            eng.wait_ge(self.sem, value)


def adaln_mamba_moe(nc, x_in, w_in, conv_w, conv_b, dt_bias, a_log, d_skip, norm_w, w_out,
                    gate_w, gate_b, exp_w, exp_b, c_in, w_mod, out):
    NB, L, DM = x_in.shape
    DI = w_out.shape[0]
    NH = a_log.shape[0]
    HD = DI // NH
    CD = conv_w.shape[0]
    TAPS = conv_w.shape[1]
    NS = (CD - DI) // 2
    NE = gate_w.shape[1]
    KT = DM // P
    FT = CD // P
    XT = DI // P
    T = 4
    GT = T * P
    NG = NB * L // GT
    NTILE = NG * T
    GPB = L // GT
    H = TAPS - 1
    EPS = 1e-5
    THRESHOLD = 0.1
    BIG = -1e30
    assert NS == P and DI == 512 and DM == 256 and GPB == 4 and NG % 2 == 0 and FT == 6
    ZH = DI // 2
    ZD = ZH + NH
    CX = DI + NH
    WC = CX + CD
    EC = NE + NE * DM

    x_tok = x_in.rearrange("b l d -> (b l) d")
    out_tok = out.rearrange("b l d -> (b l) d")

    with ExitStack() as ctx:
        def sb(name, shape, dt=F32):
            return ctx.enter_context(nc.sbuf_tensor(name, shape, dt))

        def bank(name):
            return ctx.enter_context(nc.psum_tensor(name, [P, 512], F32))

        def sem(name):
            return ctx.enter_context(nc.semaphore(name))

        pa = [bank("pa0"), bank("pa1")]
        pd = [bank("pd0"), bank("pd1")]
        px = bank("px")
        py = bank("py")
        pe_ = [bank("pe0"), bank("pe1")]

        ident = sb("ident", [P, P])
        identb = sb("identb", [P, P], BF16)
        tri = sb("tri", [P, P])
        ones = sb("ones", [P, P])
        negmask = sb("negmask", [P, P], BF16)
        sel = sb("sel", [3 * NH, NH, P], BF16)
        neghalf = sb("neghalf", [P, T])
        eps = sb("eps", [P, T])
        w_hi = sb("w_hi", [P, KT, WC], F32R)
        w_lo = sb("w_lo", [P, KT, WC], F32R)
        e_hi = sb("e_hi", [P, KT, EC], F32R)
        e_lo = sb("e_lo", [P, KT, EC], F32R)
        wo = sb("wo", [P, XT, DM])
        eb = sb("eb", [NE, DM])
        gb_rep = sb("gb_rep", [P, NE])
        cw = sb("cw", [P, FT, TAPS])
        cb = sb("cb", [P, FT])
        nw = sb("nw", [P, XT])
        a_rep = sb("a_rep", [P, NH])
        dtb_rep = sb("dtb_rep", [P, NH])
        d_rep = sb("d_rep", [P, NH])
        cT = sb("cT", [P, KT, NB])
        thc = sb("thc", [P, KT, NB])
        hc = sb("hc", [P, KT, NB])
        scT = sb("scT", [P, KT, NB])
        expa = sb("expa", [P, NH])
        modT = sb("modT", [P, NB, 4, KT])
        par1 = sb("par1", [P, 2, KT])
        par2 = sb("par2", [P, 2, KT])
        gates = sb("gates", [P, NB, 2, DM])

        xin = sb("xin", [P, T, DM])
        xres = sb("xres", [P, T, DM])
        st1 = sb("st1", [P, T, 6])
        mv1 = sb("mv1", [P, T, 2])
        rstd1 = sb("rstd1", [P, T])
        hf = sb("hf", [P, KT, GT])
        h_hi = sb("h_hi", [P, 2, KT, GT], F32R)
        h_lo = sb("h_lo", [P, 2, KT, GT], F32R)
        raw = sb("raw", [P, 2, H + GT])
        hist = sb("hist", [P, 2, FT, H])
        acc = sb("acc", [P, 2, GT])
        th = sb("th", [P, 2, GT])
        feat = sb("feat", [P, 2, FT, GT])
        gz = sb("gz", [P, 2, T, DI])
        v = sb("v", [P, T, NH])
        nabs = sb("nabs", [P, T, NH])
        u = sb("u", [P, T, NH])
        w1 = sb("w1", [P, T, NH])
        lnw = sb("lnw", [P, T, NH])
        nc1 = sb("nc1", [P, T, NH])
        sp1 = sb("sp1", [P, T, NH])
        dt = sb("dt", [P, 2, T, NH])
        dA = sb("dA", [P, T, NH])
        e3in = sb("e3in", [P, 3, T, NH])
        e3 = sb("e3", [P, 2, 3, T, NH])
        ncs = sb("ncs", [P, 2, T, NH])
        r1 = sb("r1", [P, T, NH])
        parts = sb("parts", [P, T, 3, NH], BF16)
        csT = sb("csT", [3 * NH, 2, T, P], BF16)

        gs = sb("gs", [P, P])
        bt = sb("bt", [P, P])
        xt = sb("xt", [P, DI])
        xdt = sb("xdt", [P, DI])
        xs = sb("xs", [P, DI])
        lm = sb("lm", [P, NH, P])
        mm = sb("mm", [P, NH, P])
        gsgn, gabs = lm[0:NB, 0:NH // 2].rearrange("p a n -> p (a n)"), lm[0:NB, NH // 2:].rearrange("p a n -> p (a n)")
        grow = mm[0:NB, 0:NH // 2].rearrange("p a n -> p (a n)")
        zero_or_s = sb("zero_or_s", [P, 2, DI])
        s_even = sb("s_even", [P, DI])
        sres = sb("sres", [P, DI])
        y4 = sb("y4", [P, 2, DI])
        ysq = sb("ysq", [P, DI], BF16)
        ssq = sb("ssq", [P, 2])
        ms = sb("ms", [P, 2])
        rs = sb("rs", [P, 2])
        ve2 = sb("ve2", [P, 1])
        yT = sb("yT", [P, XT, P])
        x2 = sb("x2", [P, 2, DM])
        st2 = sb("st2", [P, 6])
        mv2 = sb("mv2", [P, 2])
        rstd2 = sb("rstd2", [P, 2])
        xn2 = sb("xn2", [P, DM])
        h2f = sb("h2f", [P, KT, P])
        h2_hi = sb("h2_hi", [P, 2, KT, P], F32R)
        h2_lo = sb("h2_lo", [P, 2, KT, P], F32R)
        lg = sb("lg", [P, NE])
        nmax = sb("nmax", [P, 2])
        pe = sb("pe", [P, NE])
        psum_ = sb("psum_", [P, 4])
        pr = sb("pr", [P, NE])
        wsel = sb("wsel", [P, NE])
        wg = sb("wg", [P, NE])
        wgT = sb("wgT", [NE, P])
        eacc = sb("eacc", [P, 2, DM])
        outb = sb("outb", [P, 2, DM])

        s_ld = sem("s_ld")
        s_xin = sem("s_xin")
        s_xres = [sem(f"s_xres{t}") for t in range(T)]
        s_out = [sem("s_out0"), sem("s_out1")]

        FTS = [5, 4, 0, 1, 2, 3]
        PEA1 = Stage(sem("pe_a1"), ["hT"])
        PEA = Stage(sem("pe_a"), ["z0", "z1", "ft5", "z2", "z3", "ft4", "ft0", "cs", "ft1", "csT", "ft2", "ft3"])
        PEB = Stage(sem("pe_b"), ["D", "G", "xT", "yoff", "ydiag", "state"])
        PEC = Stage(sem("pe_c1"), ["yT", "wout", "h2T"])
        PEE = Stage(sem("pe_e"), ["e0", "e1", "e2", "wT", "e3", "e4"])
        ACTA1 = Stage(sem("act_a1"), ["h0", "h1"])
        ACTA = Stage(sem("act_a"),
                     ["tz0a", "tz0b", "tz1a", "tz1b", "raw5", "acc5", "th5"]
                     + ["tz2a", "tz2b", "tz3a", "tz3b", "raw4", "acc4", "u", "ln", "th4"]
                     + ["raw0", "acc0", "e3", "csT", "th0", "raw1", "acc1", "th1"]
                     + ["raw2", "acc2", "th2", "raw3", "acc3", "th3"])
        ACTB = Stage(sem("act_b"), ["gs", "bt", "xt"] + [f"L{h}" for h in range(NH)] + ["sq"])
        ACTC = Stage(sem("act_c1"), ["yT", "h0", "h1"])
        ACTE = Stage(sem("act_e"), ["exp", "wT"])
        DVEA1 = Stage(sem("dve_a1"), ["st0", "st1", "st2", "st3", "par", "mv0", "mv1", "mv2", "mv3",
                                      "xn0", "xn1", "xn2", "xn3", "hi"])
        def conv_steps(f):
            return [f"halo{f}", f"tap{f}a", f"tap{f}b", f"tap{f}c", f"hist{f}"]
        DVEA = Stage(sem("dve_a"),
                     ["gz0a", "gz0b", "dtb0", "gz1a", "gz1b", "dtb1"] + conv_steps(5) + ["silu5"]
                     + ["gz2a", "gz2b", "dtb2", "gz3a", "gz3b", "dtb3", "nabs", "w1"] + conv_steps(4)
                     + ["nc1", "sp1", "dt", "dA", "silu4"]
                     + ["cs", "dcs", "ncs", "p0", "r1", "p1", "p2"]
                     + conv_steps(0) + ["silu0"] + conv_steps(1) + ["silu1"]
                     + conv_steps(2) + ["silu2"] + conv_steps(3) + ["silu3"])
        DVEB = Stage(sem("dve_b"), ["M", "y1", "y3", "y4", "S"])
        DVES = Stage(sem("dve_s"), ["sres"])
        DVEC = Stage(sem("dve_c1"), ["o1", "x2", "st", "par", "mv", "xn", "hi"])
        DVEE = Stage(sem("dve_e"), ["lg", "max", "rsum", "pr", "wsel", "wguard", "rw", "rz", "rr", "wg"]
                     + [f"acc{e}" for e in range(NE)] + ["bias", "og", "out"])
        POOLA1 = Stage(sem("pool_a1"), ["ve", "rstd", "lo"])
        POOLB = Stage(sem("pool_b"), ["xdt", "xs", "xd", "scd", "y2"])
        POOLC = Stage(sem("pool_c1"), ["ms", "rs", "ve", "rstd", "lo"])

        POOL0 = Stage(sem("pool_0"), ["z_ident", "ident", "identb", "o_tri", "tri", "ones", "z_neg", "negmask",
                                      "z_sel", "sel0", "sel1", "sel2", "neghalf", "eps", "szero", "hist"])
        ACT0 = Stage(sem("act_0"), ["thc", "expa"] + [f"g{b}" for b in range(NB)])
        PE0 = Stage(sem("pe_0"), ["grow", "mod"] + [f"g{b}" for b in range(NB)])
        DVE0 = Stage(sem("dve_0"),
                     ["hc", "scT", "sgn", "abs", "max", "grow"] + [f"m{j}{k}" for j in range(4) for k in range(KT)]
                     + ["cw", "cb", "a_rep"] + [f"wo{k}" for k in range(XT)]
                     + [f"w{i}{x}" for i in range(4) for x in ("hi", "lo")] + ["ghi", "ehi", "glo", "elo"])

        pa0_bf = pa[0][:].bitcast(BF16)

        feat_flat = feat[:].rearrange("p a f n -> p (a f n)")
        stage_w = feat_flat[:, 0:KT * WC].rearrange("p (k n) -> p k n", k=KT)
        stage_m = feat_flat[:, KT * WC:KT * (WC + 6 * DM)].rearrange("p (k n) -> p k n", k=KT)
        stage_e = gz[:].rearrange("p a t n -> p (a t n)").rearrange("p (k n) -> p k n", k=KT)
        stage_g = hf[:, 0, 0:KT * NE].rearrange("p (k n) -> p k n", k=KT)

        def rep(ap, n, w):
            return ap[:, None, :].to_broadcast([P, n, w])

        def spread(ap, n, w):
            return ap[:, :, None].to_broadcast([P, n, w])

        block = ctx.enter_context(nc.Block())

        def run(eng, slots, pre):
            def pair(p, known):
                for q in range(2):
                    g = 2 * p + q
                    for t in range(T):
                        slots(eng, p, q, t, g, known)
            pre(eng)
            pair(0, True)
            with eng.Fori(1, NG // 2 - 1) as p:
                pair(p, False)
            pair(NG // 2 - 1, True)
            for extra in range(2):
                slots(eng, NG // 2, 0, extra, NG, True)

        def tile_of(g, t, back):
            n = t - back
            return (g, n) if n >= 0 else (g - 1, n + T)

        def exists(g, known):
            return not known or 0 <= g < NG

        def batch(p, q, t, back):
            g2 = 2 * p + q
            if isinstance(p, int):
                return tile_of(g2, t, back)[0] // GPB
            n = q * T + t - back
            return (p if n >= 0 else p - 1) // 2


        def state_before(q, t):
            if q == 0 and t == 0:
                return sres[:]
            return state_of(t - 1)

        def state_of(t):
            return zero_or_s[:, 1] if t % 2 else s_even[:]

        def state_ready(eng, p, q, t, n):
            if q == 0 and t == 0:
                DVES.after(eng, "sres", p)
            else:
                DVEB.after(eng, "S", n - 1)

        def mods_of(b, kind):
            return modT[:, bass.ds(b, 1), kind:kind + 2].rearrange("p b a k -> p (b a k)")

        def bank_of(f):
            return pa[{5: 0, 4: 0, 0: 1, 1: 1, 2: 1, 3: 0}[f]]

        def two_back(eng, f, g, name, stage):
            i = FTS.index(f)
            stage.after(eng, name(FTS[(i - 2) % FT]), g if i >= 2 else g - 1)

        def bank_e(e):
            return {0: 1, 1: 1, 2: 1, 3: 0, 4: 0, 5: 1, 6: 1, 7: 0}[e]

        def out_count(n, te):
            return 8 * (n - te % 2)

        loads = []

        def load(dst, src):
            loads.append((dst, src))

        wv = w_in.rearrange("(k p) n -> p k n", p=P)
        for k in range(KT):
            load(cT[:, k], c_in[:, k * P:(k + 1) * P].rearrange("b p -> p b"))
        load(stage_m, w_mod.rearrange("(k p) n -> p k n", p=P))
        load(stage_w[:, :, 0:ZH], wv[:, :, 0:ZH])
        load(stage_w[:, :, ZH:ZD], wv[:, :, DI + CD:])
        load(stage_w[:, :, ZD:WC], wv[:, :, ZH:DI + CD])
        for dst, src in ((gb_rep, gate_b), (a_rep, a_log), (dtb_rep, dt_bias), (d_rep, d_skip)):
            load(dst[:], src.rearrange("(o n) -> o n", o=1).to_broadcast([P, src.shape[0]]))
        load(cw[:], conv_w.rearrange("(f p) k -> p f k", p=P))
        load(cb[:], conv_b.rearrange("(f p) -> p f", p=P))
        load(nw[:], norm_w.rearrange("(f p) -> p f", p=P))
        load(wo[:], w_out.rearrange("(k p) n -> p k n", p=P))
        load(eb[:], exp_b)
        load(stage_g, gate_w.rearrange("(k p) n -> p k n", p=P))
        for k in range(KT):
            load(stage_e[:, k].rearrange("p (e n) -> p e n", e=NE), exp_w[:, k * P:(k + 1) * P, :].rearrange("e p n -> p e n"))
        LOADED = 16 * len(loads)

        @block.sync
        def _(sp):
            def load_xin(g):
                sp.dma_start(xin[:], x_tok[bass.ds(g * GT, GT), :].rearrange("(t p) d -> p t d", p=P)).then_inc(s_xin, 16)

            def load_xres(g, t):
                sp.dma_start(xres[:, t], x_tok[bass.ds(g * GT + t * P, P), :]).then_inc(s_xres[t], 16)

            def pre(sp):
                load_xin(0)
                for dst, src in loads:
                    with nc.allow_non_contiguous_dma(reason="small vectors, once"):
                        sp.dma_start(dst, src).then_inc(s_ld, 16)
                for t in range(T):
                    load_xres(0, t)
                for g in range(2):
                    PEA1.after(sp, "hT", g)
                    load_xin(g + 1)

            def slots(sp, p, q, t, g, known):
                if t == 0 and exists(g - 1, known) and exists(g + 2, known):
                    PEA1.after(sp, "hT", g + 1)
                    load_xin(g + 2)
                gc, tc = tile_of(g, t, 1)
                if exists(gc, known) and exists(gc + 1, known):
                    DVEC.after(sp, "x2", T * gc + tc)
                    load_xres(gc + 1, tc)
                ge, te = tile_of(g, t, 2)
                if exists(ge, known):
                    DVEE.after(sp, "out", T * ge + te)
                    sp.dma_start(out_tok[bass.ds((ge * T + te) * P, P), :], outb[:, te % 2]).then_inc(s_out[te % 2], 16)
            run(sp, slots, pre)
            for o in s_out:
                sp.wait_ge(o, 16 * NTILE // 2)

        @block.gpsimd
        def _(pool):
            def pre(pool):
                D0 = POOL0.done
                def own(name):
                    POOL0.after(pool, name, 0)
                D0("z_ident", pool.memset(ident[:], 0.0))
                own("z_ident")
                D0("ident", pool.affine_select(out=ident[:], in_=ident[:], compare_op=ALU.not_equal, fill=1.0,
                                               base=0, pattern=[[-1, P]], channel_multiplier=1))
                own("ident")
                D0("identb", pool.tensor_copy(identb[:], ident[:]))
                D0("o_tri", pool.memset(tri[:], 1.0))
                own("o_tri")
                D0("tri", pool.affine_select(out=tri[:], in_=tri[:], compare_op=ALU.is_ge, fill=0.0,
                                             base=0, pattern=[[1, P]], channel_multiplier=-1))
                D0("ones", pool.memset(ones[:], 1.0))
                D0("z_neg", pool.memset(negmask[:], 0.0))
                own("z_neg")
                D0("negmask", pool.affine_select(out=negmask[:], in_=negmask[:], compare_op=ALU.is_ge, fill=BIG,
                                                 base=0, pattern=[[1, P]], channel_multiplier=-1))
                D0("z_sel", pool.memset(sel[:], 0.0))
                own("z_sel")
                for part in range(3):
                    D0(f"sel{part}", pool.affine_select(out=sel[:], in_=sel[:], compare_op=ALU.not_equal, fill=1.0,
                                                        base=-part * NH, pattern=[[-1, NH], [0, P]], channel_multiplier=1))
                    own(f"sel{part}")
                D0("neghalf", pool.memset(neghalf[:], -0.5))
                D0("eps", pool.memset(eps[:], EPS))
                D0("szero", pool.memset(zero_or_s[:], 0.0))
                D0("hist", pool.memset(hist[:], 0.0))
                a1(pool, 0, 0)
                a1(pool, 1, 1)

            def a1(pool, g, q):
                DVEA1.after(pool, "mv3", g)
                DVEA1.after(pool, "xn3", g - 1)
                POOLA1.after(pool, "lo", g - 1)
                POOLA1.done("ve", pool.tensor_tensor(rstd1[:], mv1[:, :, 1], eps[:], ALU.add))
                POOLA1.after(pool, "ve", g)
                POOLA1.done("rstd", pool.tensor_tensor(rstd1[:], rstd1[:], neghalf[:, 0:T], ALU.pow))
                DVEA1.after(pool, "hi", g)
                PEA.after(pool, "ft3", g - 2)
                POOLA1.done("lo", pool.tensor_tensor(h_lo[:, q], hf[:], h_hi[:, q].bitcast(F32), ALU.subtract))

            def slots(pool, p, q, t, g, known):
                gc, tc = tile_of(g, t, 1)
                if exists(g, known):
                    b(pool, p, q, t, g)
                if exists(gc, known):
                    c(pool, gc, tc)
                if exists(g, known):
                    b2(pool, p, q, t, g)
                if exists(gc, known):
                    c2(pool, gc, tc)
                if t == T - 1 and exists(g, known) and exists(g + 2, known):
                    a1(pool, g + 2, q)

            def b(pool, p, q, t, g):
                n = T * g + t
                ACTB.after(pool, "xt", n)
                DVEA.after(pool, "dt", g)
                PEB.after(pool, "ydiag", n - 1)
                POOLB.done("xdt", pool.tensor_tensor(xdt[:], xt[:], spread(dt[:, q, t], NH, HD), ALU.mult))
                ACTA.after(pool, "e3", g)
                POOLB.after(pool, "xdt", n)
                PEB.after(pool, "state", n - 1)
                POOLB.done("xs", pool.tensor_tensor(xs[:], xdt[:], spread(e3[:, q, 1, t], NH, HD), ALU.mult))
                POOLB.done("xd", pool.tensor_tensor(xt[:], xt[:], spread(d_rep[:], NH, HD), ALU.mult))
                state_ready(pool, p, q, t, n)
                PEB.after(pool, "yoff", n - 1)
                POOLB.after(pool, "scd", n - 1)
                POOLB.done("scd", pool.tensor_tensor(state_of(t), state_before(q, t), spread(e3[:, q, 2, t], NH, HD), ALU.mult))

            def b2(pool, p, q, t, g):
                n = T * g + t
                DVEB.after(pool, "y1", n)
                POOLB.after(pool, "xd", n)
                POOLB.done("y2", pool.tensor_tensor(y4[:, t % 2], y4[:, t % 2], xt[:], ALU.add))

            def c(pool, gc, tc):
                n = T * gc + tc
                ACTB.after(pool, "sq", n)
                DVEC.after(pool, "o1", n - 2)
                POOLC.done("ms", pool.tensor_tensor(ms[:, tc % 2:tc % 2 + 1], ssq[:, tc % 2:tc % 2 + 1], eps[:, 0:1], ALU.add))
                POOLC.after(pool, "ms", n)
                POOLC.done("rs", pool.tensor_tensor(rs[:, tc % 2:tc % 2 + 1], ms[:, tc % 2:tc % 2 + 1], neghalf[:, 0:1], ALU.pow))

            def c2(pool, gc, tc):
                n = T * gc + tc
                DVEC.after(pool, "mv", n)
                POOLC.after(pool, "rs", n)
                POOLC.done("ve", pool.tensor_tensor(ve2[:], mv2[:, 1:2], eps[:, 0:1], ALU.add))
                POOLC.after(pool, "ve", n)
                DVEC.after(pool, "xn", n - 1)
                POOLC.done("rstd", pool.tensor_tensor(rstd2[:, 0:1], ve2[:], neghalf[:, 0:1], ALU.pow))
                DVEC.after(pool, "hi", n)
                PEE.after(pool, "e4", n - 2)
                POOLC.done("lo", pool.tensor_tensor(h2_lo[:, tc % 2], h2f[:], h2_hi[:, tc % 2].bitcast(F32), ALU.subtract))

            run(pool, slots, pre)

        @block.scalar
        def _(act):
            def pre(act):
                act.wait_ge(s_ld, LOADED)
                ACT0.done("thc", act.activation(thc[:], cT[:], ACT.Tanh, scale=0.5))
                ACT0.done("expa", act.activation(expa[:], a_rep[:], ACT.Exp))
                for b in range(NB):
                    PE0.after(act, f"g{b}", 0)
                    ACT0.done(f"g{b}", act.activation(gates[:, b].rearrange("p a n -> p (a n)"), pe_[b % 2][:], ACT.Copy))
                a1(act, 0)
                for t in range(T):
                    for piece in pieces(t):
                        piece(act, 0, 0, t)
                a1(act, 1)

            def a1(act, g):
                PEA1.after(act, "hT", g)
                DVEA1.after(act, "hi", g - 1)
                POOLA1.after(act, "lo", g - 1)
                for k in range(KT):
                    ACTA1.done(f"h{k}", act.activation(hf[:, k], pa[k][:], ACT.Identity,
                                                       bias=par1[:, 0, k:k + 1], scale=par1[:, 1, k:k + 1]))

            def z(i):
                def piece(act, g, q, t):
                    PEA.after(act, f"z{i}", g)
                    for x in range(2):
                        if i == 0 and x == 0:
                            DVEB.after(act, "y4", T * (g - 2) + 3)
                        ACTA.done(f"tz{i}{'ab'[x]}", act.activation(gz[:, q, i, x * ZH:(x + 1) * ZH], pa[x][:, 0:ZH], ACT.Tanh))
                return piece

            def raws(f):
                def piece(act, g, q, t):
                    o = FTS.index(f) % 2
                    PEA.after(act, f"ft{f}", g)
                    two_back(act, f, g, lambda ff: f"hist{ff}", DVEA)
                    ACTA.done(f"raw{f}", act.activation(raw[:, o, H:], bank_of(f)[:], ACT.Copy))
                    two_back(act, f, g, lambda ff: f"silu{ff}", DVEA)
                    ACTA.done(f"acc{f}", act.activation(acc[:, o], bank_of(f)[:], ACT.Identity,
                                                        bias=cb[:, f:f + 1], scale=cw[:, f, H:H + 1]))
                return piece

            def tanh(f):
                def piece(act, g, q, t):
                    o = FTS.index(f) % 2
                    DVEA.after(act, f"tap{f}c", g)
                    ACTA.done(f"th{f}", act.activation(th[:, o], acc[:, o], ACT.Tanh))
                return piece

            def softplus(act, g, q, t):
                DVEA.after(act, "nabs", g)
                DVEA.after(act, "nc1", g - 1)
                ACTA.done("u", act.activation(u[:], nabs[:], ACT.Exp))
                DVEA.after(act, "w1", g)
                DVEA.after(act, "sp1", g - 1)
                ACTA.done("ln", act.activation(lnw[:], w1[:], ACT.Ln))

            def decays(act, g, q, t):
                DVEA.after(act, "dcs", g)
                ACTA.done("e3", act.activation(e3[:, q], e3in[:], ACT.Exp))
                PEA.after(act, "csT", g)
                ACTA.done("csT", act.activation(csT[:, q].rearrange("p t n -> p (t n)"), pa0_bf[0:3 * NH, 0:GT], ACT.Copy))

            def pieces(t):
                return {0: [z(0), z(1), raws(5), tanh(5)],
                        1: [z(2), z(3), raws(4), softplus, tanh(4)],
                        2: [raws(0), decays, tanh(0), raws(1), tanh(1)],
                        3: [raws(2), tanh(2), raws(3), tanh(3)]}[t]

            def slots(act, p, q, t, g, known):
                n = T * g + t
                gc, tc = tile_of(g, t, 1)
                ge, te = tile_of(g, t, 2)
                todo = pieces(t) if exists(g, known) and exists(g + 1, known) else []
                todo = list(todo)

                def a():
                    if todo:
                        todo.pop(0)(act, g + 1, 1 - q, t)
                if exists(g, known):
                    b(act, q, t, n)
                if exists(gc, known):
                    nc_ = T * gc + tc
                    PEC.after(act, "yT", nc_)
                    PEC.after(act, "wout", nc_ - 1)
                    ACTC.done("yT", act.activation(yT[:].rearrange("p f n -> p (f n)"), pe_[0][:], ACT.Copy))
                a()
                if exists(ge, known):
                    ne = T * ge + te
                    DVEE.after(act, "max", ne)
                    DVEE.after(act, "wsel", ne - 1)
                    ACTE.done("exp", act.activation(pe[:], lg[:], ACT.Exp, bias=nmax[:, 1:2]))
                a()
                a()
                a()
                if exists(gc, known):
                    nc_ = T * gc + tc
                    PEC.after(act, "h2T", nc_)
                    DVEC.after(act, "hi", nc_ - 1)
                    POOLC.after(act, "lo", nc_ - 1)
                    for k in range(KT):
                        ACTC.done(f"h{k}", act.activation(h2f[:, k], pe_[1][:, k * P:(k + 1) * P], ACT.Identity,
                                                          bias=par2[:, 0, k:k + 1], scale=par2[:, 1, k:k + 1]))
                if exists(ge, known):
                    ne = T * ge + te
                    PEE.after(act, "wT", ne)
                    PEE.after(act, "e4", ne - 1)
                    ACTE.done("wT", act.activation(wgT[:], pe_[0][0:NE, 0:P], ACT.Copy))
                while todo:
                    a()
                if exists(g, known):
                    DVEB.after(act, "y4", n)
                    POOLC.after(act, "ms", n - 2)
                    ACTB.done("sq", act.activation(ysq[:], y4[:, t % 2], ACT.Square, scale=DI ** -0.5, accum_out=ssq[:, t % 2:t % 2 + 1]))
                if t == T - 1 and exists(g, known) and exists(g + 2, known):
                    a1(act, g + 2)

            def b(act, q, t, n):
                PEB.after(act, "G", n)
                DVEB.after(act, "M", n - 1)
                ACTB.done("gs", act.activation(gs[:], py[:, 0:P], ACT.Copy))
                PEB.after(act, "state", n - 1)
                ACTB.done("bt", act.activation(bt[:], py[:, P:2 * P], ACT.Copy))
                PEB.after(act, "xT", n)
                POOLB.after(act, "y2", n - 1)
                ACTB.done("xt", act.activation(xt[:], px[:], ACT.Copy))
                PEB.after(act, "D", n)
                DVEB.after(act, "M", n - 1)
                for h in range(NH):
                    ACTB.done(f"L{h}", act.activation(lm[:, h], pd[h // 4][:, h % 4 * P:(h % 4 + 1) * P], ACT.Exp,
                                                      bias=ncs[:, q, t, h:h + 1]))

            run(act, slots, pre)

        @block.vector
        def _(dve):
            def pre(dve):
                D0 = DVE0.done

                def own(name):
                    DVE0.after(dve, name, 0)
                dve.wait_ge(s_ld, LOADED)
                D0("hc", dve.tensor_scalar(hc[:], cT[:], 0.5, None, ALU.mult))
                own("hc")
                ACT0.after(dve, "thc", 0)
                D0("scT", dve.scalar_tensor_tensor(out=scT[:], in0=thc[:], scalar=1.0, in1=hc[:], op0=ALU.add, op1=ALU.mult))
                PE0.after(dve, "grow", 0)
                D0("sgn", dve.tensor_scalar(gsgn, pe_[0][0:NB, :], 0.0, 2.0, ALU.is_ge, ALU.mult))
                D0("abs", dve.tensor_scalar(gabs, pe_[0][0:NB, :], -1.0, None, ALU.mult))
                own("abs")
                D0("max", dve.scalar_tensor_tensor(out=gabs, in0=gabs, scalar=0.25, in1=pe_[0][0:NB, :], op0=ALU.max, op1=ALU.max))
                own("max")
                D0("grow", dve.scalar_tensor_tensor(out=grow, in0=gsgn, scalar=-1.0, in1=gabs, op0=ALU.add, op1=ALU.mult))
                PE0.after(dve, "mod", 0)
                for j in range(4):
                    for k in range(KT):
                        c0 = (j * KT + k) * NB
                        D0(f"m{j}{k}", dve.tensor_scalar(modT[:, :, j, k], pd[0][:, c0:c0 + NB], float(j % 2), None, ALU.add))
                D0("cw", dve.tensor_scalar(cw[:], cw[:], 0.5, None, ALU.mult))
                D0("cb", dve.tensor_scalar(cb[:], cb[:], 0.5, None, ALU.mult))
                ACT0.after(dve, "expa", 0)
                D0("a_rep", dve.tensor_scalar(a_rep[:], expa[:], -1.0, None, ALU.mult))
                for k in range(XT):
                    D0(f"wo{k}", dve.tensor_scalar(wo[:, k], wo[:, k], nw[:, k:k + 1], None, ALU.mult))
                for i, (a, b, f) in enumerate(((0, ZH, 0.5), (ZH, ZD, 1.0), (ZD, CX, 0.5), (CX, WC, 1.0))):
                    D0(f"w{i}hi", dve.tensor_scalar(w_hi[:, :, a:b], stage_w[:, :, a:b], f, None, ALU.mult))
                    own(f"w{i}hi")
                    D0(f"w{i}lo", dve.scalar_tensor_tensor(out=w_lo[:, :, a:b], in0=stage_w[:, :, a:b], scalar=f,
                                                           in1=w_hi[:, :, a:b].bitcast(F32), op0=ALU.mult, op1=ALU.subtract))
                D0("ghi", dve.tensor_copy(e_hi[:, :, 0:NE], stage_g))
                D0("ehi", dve.tensor_copy(e_hi[:, :, NE:EC], stage_e))
                own("ehi")
                D0("glo", dve.tensor_tensor(e_lo[:, :, 0:NE], stage_g, e_hi[:, :, 0:NE].bitcast(F32), ALU.subtract))
                D0("elo", dve.tensor_tensor(e_lo[:, :, NE:EC], stage_e, e_hi[:, :, NE:EC].bitcast(F32), ALU.subtract))
                own("elo")
                a1(dve, 0, 0, 0)
                for t in range(T):
                    for piece in pieces(t):
                        piece(dve, 0, 0, 0)
                a1(dve, 1, 1, 0)

            def a1(dve, g, q, bi):
                dve.wait_ge(s_xin, 16 * (g + 1))
                A = DVEA1.done
                POOLA1.after(dve, "rstd", g - 1)
                for t in range(T):
                    A(f"st{t}", dve.bn_stats(st1[:, t], xin[:, t]))
                DVEA1.after(dve, "st3", g)
                ACTA1.after(dve, "h1", g - 1)
                A("par", dve.tensor_scalar(par1[:].rearrange("p a k -> p (a k)"), mods_of(bi, 0), 1.0, None, ALU.mult))
                for t in range(T):
                    A(f"mv{t}", dve.bn_aggr(mv1[:, t], st1[:, t]))
                POOLA1.after(dve, "rstd", g)
                for t in range(T):
                    A(f"xn{t}", dve.tensor_scalar(xin[:, t], xin[:, t], mv1[:, t, 0:1], rstd1[:, t:t + 1], ALU.subtract, ALU.mult))
                ACTA1.after(dve, "h1", g)
                PEA.after(dve, "ft3", g - 2)
                A("hi", dve.tensor_copy(h_hi[:, q], hf[:]))

            def z(i):
                def piece(dve, g, q, sel_):
                    ACTA.after(dve, f"tz{i}a", g)
                    for x in range(2):
                        if x:
                            ACTA.after(dve, f"tz{i}b", g)
                        DVEA.done(f"gz{i}{'ab'[x]}", dve.scalar_tensor_tensor(
                            out=gz[:, q, i, x * ZH:(x + 1) * ZH], in0=gz[:, q, i, x * ZH:(x + 1) * ZH], scalar=1.0, in1=pa[x][:, 0:ZH],
                            op0=ALU.add, op1=ALU.mult))
                    DVEA.after(dve, "w1", g - 1)
                    DVEA.after(dve, "sp1", g - 1)
                    DVEA.done(f"dtb{i}", dve.tensor_tensor(v[:, i], pa[0][:, ZH:ZD], dtb_rep[:], ALU.add))
                return piece

            def conv(f):
                def piece(dve, g, q, sel_):
                    o = FTS.index(f) % 2
                    A = DVEA.done
                    ACTA.after(dve, f"acc{f}", g)
                    DVEA.after(dve, f"hist{f}", g - 1)
                    two_back(dve, f, g, lambda ff: f"hist{ff}", DVEA)
                    A(f"halo{f}", dve.tensor_copy(raw[:, o, 0:H].rearrange("p (a n) -> p a n", a=1), hist[:, bass.ds(sel_, 1), f]))
                    DVEA.after(dve, f"halo{f}", g)
                    for j, name in enumerate("abc"):
                        if j:
                            DVEA.after(dve, f"tap{f}{'abc'[j - 1]}", g)
                        A(f"tap{f}{name}", dve.scalar_tensor_tensor(
                            out=acc[:, o], in0=raw[:, o, j:j + GT], scalar=cw[:, f, j:j + 1], in1=acc[:, o],
                            op0=ALU.mult, op1=ALU.add))
                    A(f"hist{f}", dve.tensor_copy(hist[:, 1, f], raw[:, o, GT:GT + H]))
                return piece

            def silu(f):
                def piece(dve, g, q, sel_):
                    o = FTS.index(f) % 2
                    ACTA.after(dve, f"th{f}", g)
                    PEB.after(dve, "yoff", T * (g - 2) + 3)
                    DVEA.done(f"silu{f}", dve.scalar_tensor_tensor(
                        out=feat[:, q, f], in0=th[:, o], scalar=1.0, in1=acc[:, o], op0=ALU.add, op1=ALU.mult))
                return piece

            def softplus1(dve, g, q, sel_):
                DVEA.after(dve, "dtb3", g)
                ACTA.after(dve, "u", g - 1)
                DVEA.done("nabs", dve.scalar_tensor_tensor(out=nabs[:], in0=v[:], scalar=-1.0, in1=v[:], op0=ALU.mult, op1=ALU.min))
                ACTA.after(dve, "u", g)
                ACTA.after(dve, "ln", g - 1)
                DVEA.after(dve, "nc1", g - 1)
                DVEA.done("w1", dve.tensor_scalar(w1[:], u[:], 1.0, None, ALU.add))

            def softplus2(dve, g, q, sel_):
                DVEA.after(dve, "w1", g)
                DVEA.done("nc1", dve.scalar_tensor_tensor(out=nc1[:], in0=w1[:], scalar=1.0, in1=u[:], op0=ALU.subtract, op1=ALU.subtract))
                ACTA.after(dve, "ln", g)
                DVEA.done("sp1", dve.scalar_tensor_tensor(out=sp1[:], in0=v[:], scalar=0.0, in1=lnw[:], op0=ALU.max, op1=ALU.add))
                DVEA.after(dve, "sp1", g)
                POOLB.after(dve, "xdt", T * (g - 2) + 3)
                DVEA.done("dt", dve.tensor_tensor(dt[:, q], sp1[:], nc1[:], ALU.subtract))
                DVEA.after(dve, "dt", g)
                PEA.after(dve, "cs", g - 1)
                DVEA.done("dA", dve.tensor_tensor(dA[:], dt[:, q], rep(a_rep[:], T, NH), ALU.mult))

            def sums(dve, g, q, sel_):
                PEA.after(dve, "cs", g)
                ACTA.after(dve, "e3", g - 1)
                DVEA.done("cs", dve.tensor_copy(e3in[:, 0:3:2], pa[0][:, 0:2 * T * NH].rearrange("p (a t h) -> p a t h", a=2, t=T)))
                DVEA.after(dve, "cs", g)
                DVEA.done("dcs", dve.tensor_tensor(e3in[:, 1], e3in[:, 2], e3in[:, 0], ALU.subtract))
                ACTB.after(dve, f"L{NH - 1}", T * (g - 2) + 3)
                DVEA.done("ncs", dve.tensor_scalar(ncs[:, q], e3in[:, 0], -1.0, None, ALU.mult))
                PEA.after(dve, "csT", g - 1)
                DVEA.done("p0", dve.tensor_copy(parts[:, :, 0], e3in[:, 0]))
                DVEA.after(dve, "p0", g)
                DVEA.done("r1", dve.tensor_tensor(r1[:], e3in[:, 0], parts[:, :, 0], ALU.subtract))
                DVEA.after(dve, "r1", g)
                DVEA.done("p1", dve.tensor_copy(parts[:, :, 1], r1[:]))
                DVEA.after(dve, "p1", g)
                DVEA.done("p2", dve.tensor_tensor(parts[:, :, 2], r1[:], parts[:, :, 1], ALU.subtract))

            def pieces(t):
                return {0: [z(0), z(1), conv(5), silu(5)],
                        1: [z(2), z(3), softplus1, conv(4), softplus2, silu(4)],
                        2: [sums, conv(0), silu(0), conv(1), silu(1)],
                        3: [conv(2), silu(2), conv(3), silu(3)]}[t]

            def slots(dve, p, q, t, g, known):
                n = T * g + t
                gc, tc = tile_of(g, t, 1)
                ge, te = tile_of(g, t, 2)
                todo = list(pieces(t)) if exists(g, known) and exists(g + 1, known) else []
                sel_ = (p + 1) % 2 if q else 1

                def a():
                    if todo:
                        todo.pop(0)(dve, g + 1, 1 - q, sel_)
                has_b, has_c, has_e = exists(g, known), exists(gc, known), exists(ge, known)
                if has_b and t == 0 and q == 0:
                    DVEB.after(dve, "S", n - 1)
                    PEB.after(dve, "yoff", n - 2 * T)
                    POOLB.after(dve, "scd", n - 2 * T)
                    DVES.done("sres", dve.tensor_copy(sres[:].rearrange("p (a n) -> p a n", a=1), zero_or_s[:, bass.ds(p % 2, 1)]))
                a()
                if has_e:
                    soft(dve, te, T * ge + te)
                if has_b:
                    ACTB.after(dve, f"L{NH - 1}", n)
                    PEB.after(dve, "ydiag", n - 1)
                    DVEB.done("M", dve.tensor_tensor(mm[:], lm[:], rep(gs[:], NH, P), ALU.mult))
                if has_c:
                    c1(dve, gc, tc, batch(p, q, t, 1))
                if has_b:
                    PEB.after(dve, "yoff", n)
                    ACTA.after(dve, "e3", g)
                    PEC.after(dve, "yT", n - 2)
                    ACTB.after(dve, "sq", n - 2)
                    DVEB.done("y1", dve.tensor_tensor(y4[:, t % 2], px[:], spread(e3[:, q, 0, t], NH, HD), ALU.mult))
                a()
                if has_c:
                    c2(dve, tc, T * gc + tc)
                if has_e:
                    for e in range(1, 5):
                        expert(dve, e, te, T * ge + te)
                a()
                if has_b:
                    PEB.after(dve, "ydiag", n)
                    POOLB.after(dve, "y2", n)
                    DVEB.done("y3", dve.tensor_tensor(y4[:, t % 2], py[:], y4[:, t % 2], ALU.add))
                    DVEB.after(dve, "y3", n)
                    DVEA.after(dve, "gz3b", g)
                    DVEB.done("y4", dve.tensor_tensor(y4[:, t % 2], y4[:, t % 2], gz[:, q, t], ALU.mult))
                    PEB.after(dve, "state", n)
                    POOLB.after(dve, "scd", n)
                    PEB.after(dve, "yoff", n - 1)
                    DVEB.done("S", dve.tensor_tensor(state_of(t), state_of(t), px[:], ALU.add))
                if has_c:
                    ACTC.after(dve, "h1", T * gc + tc)
                    PEE.after(dve, "e4", T * gc + tc - 2)
                    DVEC.done("hi", dve.tensor_copy(h2_hi[:, tc % 2], h2f[:]))
                while todo:
                    a()
                if has_e:
                    for e in range(5, NE):
                        expert(dve, e, te, T * ge + te)
                    finish(dve, te, T * ge + te, batch(p, q, t, 2))
                if t == T - 1 and exists(g, known) and exists(g + 2, known):
                    a1(dve, g + 2, q, (p + 1) // 2)

            def c1(dve, gc, tc, bc):
                n = T * gc + tc
                PEC.after(dve, "wout", n)
                POOLC.after(dve, "rs", n)
                DVEE.after(dve, "out", n - 2)
                ACT0.after(dve, f"g{NB - 1}", 0)
                DVEC.done("o1", dve.scalar_tensor_tensor(
                    out=x2[:, tc % 2], in0=pe_[0][:, 0:DM], scalar=rs[:, tc % 2:tc % 2 + 1],
                    in1=gates[:, bass.ds(bc, 1), 0].rearrange("p a n -> p (a n)"), op0=ALU.mult, op1=ALU.mult))
                DVEC.after(dve, "o1", n)
                dve.wait_ge(s_xres[tc], 16 * (gc + 1))
                DVEC.done("x2", dve.tensor_tensor(x2[:, tc % 2], x2[:, tc % 2], xres[:, tc], ALU.add))
                DVEC.after(dve, "x2", n)
                DVEC.done("st", dve.bn_stats(st2[:], x2[:, tc % 2]))
                DVEC.after(dve, "st", n)
                ACTC.after(dve, "h1", n - 1)
                POOLC.after(dve, "ve", n - 1)
                DVEC.done("par", dve.tensor_scalar(par2[:].rearrange("p a k -> p (a k)"), mods_of(bc, 2), 1.0, None, ALU.mult))
                DVEC.done("mv", dve.bn_aggr(mv2[:], st2[:]))

            def c2(dve, tc, n):
                POOLC.after(dve, "rstd", n)
                PEC.after(dve, "h2T", n - 1)
                DVEC.done("xn", dve.tensor_scalar(xn2[:], x2[:, tc % 2], mv2[:, 0:1], rstd2[:, 0:1], ALU.subtract, ALU.mult))

            def soft(dve, te, n):
                E = DVEE.done

                def own(name):
                    DVEE.after(dve, name, n)
                PEE.after(dve, "e0", n)
                DVEE.after(dve, "out", n - 1)
                ACTE.after(dve, "exp", n - 1)
                E("lg", dve.tensor_tensor(lg[:], pe_[1][:, 0:NE], gb_rep[:], ALU.add))
                own("lg")
                E("max", dve.tensor_reduce(nmax[:, 1:2], lg[:], AX.X, ALU.max, negate=True))
                ACTE.after(dve, "exp", n)
                E("rsum", dve.tensor_reduce(psum_[:, 0:1], pe[:], AX.X, ALU.add))
                own("rsum")
                E("pr", dve.reciprocal(psum_[:, 1:2], psum_[:, 0:1]))
                own("pr")
                E("wsel", dve.tensor_scalar(pr[:], pe[:], psum_[:, 1:2], None, ALU.mult))
                own("wsel")
                E("wguard", dve.scalar_tensor_tensor(out=wsel[:], in0=pr[:], scalar=THRESHOLD, in1=pr[:], op0=ALU.is_ge, op1=ALU.mult))
                own("wguard")
                E("rw", dve.tensor_reduce(psum_[:, 2:3], wsel[:], AX.X, ALU.add))
                own("rw")
                E("rz", dve.scalar_tensor_tensor(out=psum_[:, 2:3], in0=psum_[:, 2:3], scalar=0.0, in1=psum_[:, 2:3], op0=ALU.is_equal, op1=ALU.add))
                own("rz")
                E("rr", dve.reciprocal(psum_[:, 3:4], psum_[:, 2:3]))
                own("rr")
                PEE.after(dve, "wT", n - 1)
                E("wg", dve.tensor_scalar(wg[:], wsel[:], psum_[:, 3:4], None, ALU.mult))
                own("wg")
                E("acc0", dve.tensor_scalar(eacc[:, 0], pe_[1][:, NE:NE + DM], wg[:, 0:1], None, ALU.mult))

            def expert(dve, e, te, n):
                PEE.after(dve, f"e{(e + 1) // 2}", n)
                DVEE.after(dve, f"acc{e - 1}", n)
                src = pe_[bank_e(e)][:, 0:DM] if e % 2 else pe_[bank_e(e)][:, DM:2 * DM]
                DVEE.done(f"acc{e}", dve.scalar_tensor_tensor(out=eacc[:, e % 2], in0=src, scalar=wg[:, e:e + 1],
                                                              in1=eacc[:, (e - 1) % 2], op0=ALU.mult, op1=ALU.add))

            def finish(dve, te, n, be):
                DVEE.after(dve, f"acc{NE - 1}", n)
                DVEE.done("bias", dve.tensor_tensor(eacc[:, 0], pe_[0][:, DM:2 * DM], eacc[:, 1], ALU.add))
                DVEE.after(dve, "bias", n)
                DVEE.done("og", dve.tensor_tensor(eacc[:, 1], eacc[:, 0], gates[:, bass.ds(be, 1), 1].rearrange("p a n -> p (a n)"), ALU.mult))
                DVEE.after(dve, "og", n)
                dve.wait_ge(s_out[te % 2], out_count(n, te))
                DVEE.done("out", dve.tensor_tensor(outb[:, te % 2], eacc[:, 1], x2[:, te % 2], ALU.add))

            run(dve, slots, pre)

        @block.tensor
        def _(pe_e):
            def mm_(o, l, r, start, stop):
                return pe_e.matmul(o, lhsT=l, rhs=r, start=start, stop=stop, skip_group_check=True)

            def split(o, ahi, alo, bhi, blo, cols):
                for k in range(KT):
                    for i, (l, r) in enumerate(((ahi(k), bhi), (ahi(k), blo), (alo(k), bhi))):
                        last = mm_(o, l, r[:, k, cols], k == 0 and i == 0, k == KT - 1 and i == 2)
                return last

            def pre(pe):
                pe.wait_ge(s_ld, LOADED)
                POOL0.after(pe, "hist", 0)
                DVE0.after(pe, "scT", 0)
                for j, m in enumerate((2, 5)):
                    for k in range(KT):
                        last = mm_(pe_[0][0:NB, j * DM:(j + 1) * DM], scT[:, k], stage_m[:, k, m * DM:(m + 1) * DM], k == 0, k == KT - 1)
                PE0.done("grow", last)
                for j, m in enumerate((0, 1, 3, 4)):
                    for c in range(KT):
                        o = (j * KT + c) * NB
                        for k in range(KT):
                            last = mm_(pd[0][:, o:o + NB], stage_m[:, k, m * DM + c * P:m * DM + (c + 1) * P], scT[:, k], k == 0, k == KT - 1)
                PE0.done("mod", last)
                DVE0.after(pe, "grow", 0)
                for b in range(NB):
                    if b >= 2:
                        ACT0.after(pe, f"g{b - 2}", 0)
                    PE0.done(f"g{b}", mm_(pe_[b % 2][:], ident[0:NB, b:b + 1].to_broadcast([NB, P]), grow, True, True))
                a1(pe, 0, 0)
                DVE0.after(pe, "elo", 0)
                for t in range(T):
                    for piece in pieces(t):
                        piece(pe, 0, 0)
                a1(pe, 1, 1)

            def a1(pe, g, q):
                DVEA1.after(pe, "xn3", g)
                ACTA.after(pe, "acc3", g - 1)
                ACTA.after(pe, "acc2", g - 1)
                for k in range(KT):
                    for t in range(T):
                        last = pe.transpose(pa[k][:, t * P:(t + 1) * P], xin[:, t, k * P:(k + 1) * P], ident[:])
                PEA1.done("hT", last)

            def z(i):
                def piece(pe, g, q):
                    DVEA1.after(pe, "hi", g)
                    POOLA1.after(pe, "lo", g)
                    DVEA.after(pe, "dtb%d" % (i - 1) if i else "dtb3", g if i else g - 1)
                    if i == 2:
                        ACTA.after(pe, "acc5", g)
                    tok = slice(i * P, (i + 1) * P)
                    split(pa[0][:, 0:ZD], lambda k: h_hi[:, q, k, tok], lambda k: h_lo[:, q, k, tok], w_hi, w_lo, slice(0, ZD))
                    PEA.done(f"z{i}", split(pa[1][:, 0:ZH], lambda k: h_hi[:, q, k, tok], lambda k: h_lo[:, q, k, tok],
                                            w_hi, w_lo, slice(ZD, CX)))
                return piece

            def ft(f, stage, name):
                def piece(pe, g, q):
                    stage.after(pe, name, g)
                    cols = slice(CX + f * P, CX + (f + 1) * P)
                    for k in range(KT):
                        for i, (l, r) in enumerate(((w_hi, h_hi), (w_hi, h_lo), (w_lo, h_hi))):
                            last = mm_(bank_of(f)[:], l[:, k, cols], r[:, q, k], k == 0 and i == 0, k == KT - 1 and i == 2)
                    PEA.done(f"ft{f}", last)
                return piece

            def cs(pe, g, q):
                ACTA.after(pe, "acc4", g)
                DVEA.after(pe, "dA", g)
                flat = dA[:].rearrange("p t h -> p (t h)")
                mm_(pa[0][:, 0:T * NH], tri[:], flat, True, True)
                PEA.done("cs", mm_(pa[0][:, T * NH:2 * T * NH], ones[:], flat, True, True))

            def csTt(pe, g, q):
                DVEA.after(pe, "p2", g)
                for t in range(T):
                    last = pe.transpose(pa0_bf[0:3 * NH, t * P:(t + 1) * P], parts[:, t].rearrange("p a h -> p (a h)"), identb[:])
                PEA.done("csT", last)

            def pieces(t):
                return {0: [z(0), z(1), ft(5, DVEA, "dtb1")],
                        1: [z(2), z(3), ft(4, DVEA, "dtb3")],
                        2: [lambda pe, g, q: ft(0, DVEA, "dtb3")(pe, g, q), cs, ft(1, ACTA, "acc0"), csTt],
                        3: [ft(2, ACTA, "acc1"), ft(3, ACTA, "csT")]}[t]

            def slots(pe, p, q, t, g, known):
                n = T * g + t
                gc, tc = tile_of(g, t, 1)
                ge, te = tile_of(g, t, 2)
                todo = list(pieces(t)) if exists(g, known) and exists(g + 1, known) else []
                has_b, has_c, has_e = exists(g, known), exists(gc, known), exists(ge, known)
                nc_, ne = T * gc + tc, T * ge + te

                def a():
                    if todo:
                        todo.pop(0)(pe, g + 1, 1 - q)
                tok = slice(t * P, (t + 1) * P)
                if has_b:
                    ACTA.after(pe, "csT", g)
                    ACTB.after(pe, f"L{NH - 1}", n - 1)
                    for b in range(2):
                        mm_(pd[b][:], identb[:], rep(negmask[:], 4, P), True, False)
                        for h in range(4):
                            last = mm_(pd[b][:, h * P:(h + 1) * P], sel[:, 4 * b + h], csT[:, q, t], False, h == 3)
                    PEB.done("D", last)
                    DVEA.after(pe, "silu3", g)
                    DVEB.after(pe, "y3", n - 1)
                    mm_(py[:, 0:P], feat[:, q, 4, tok], feat[:, q, 5, tok], True, True)
                    PEB.done("G", pe.transpose(py[:, P:2 * P], feat[:, q, 4, tok], ident[:]))
                    DVEB.after(pe, "S", n - 1)
                    for f in range(XT):
                        last = pe.transpose(px[:, f * P:(f + 1) * P], feat[:, q, f, tok], ident[:])
                    PEB.done("xT", last)
                if has_c:
                    DVEB.after(pe, "y4", nc_)
                    DVEE.after(pe, "bias", ne - 1)
                    for f in range(XT):
                        last = pe.transpose(pe_[0][:, f * P:(f + 1) * P], y4[:, tc % 2, f * P:(f + 1) * P], ident[:])
                    PEC.done("yT", last)
                a()
                if has_e:
                    POOLC.after(pe, "lo", ne)
                    DVEC.after(pe, "hi", ne)
                    DVEE.after(pe, "acc6", ne - 1)
                    experts(pe, 0, te, ne)
                if has_c:
                    ACTC.after(pe, "yT", nc_)
                    for k in range(XT):
                        last = mm_(pe_[0][:, 0:DM], yT[:, k], wo[:, k], k == 0, k == XT - 1)
                    PEC.done("wout", last)
                if has_b:
                    ACTB.after(pe, "xt", n)
                    state_ready(pe, p, q, t, n)
                    PEB.done("yoff", mm_(px[:], feat[:, q, 5, tok], state_before(q, t), True, True))
                a()
                if has_e:
                    DVEE.after(pe, "acc0", ne)
                    experts(pe, 1, te, ne)
                    if has_c:
                        DVEC.after(pe, "o1", nc_)
                    experts(pe, 2, te, ne)
                if has_b:
                    DVEB.after(pe, "M", n)
                    POOLB.after(pe, "xdt", n)
                    ACTB.after(pe, "bt", n)
                    for h in range(NH):
                        last = mm_(py[:, h * HD:(h + 1) * HD], mm[:, h], xdt[:, h * HD:(h + 1) * HD], True, True)
                    PEB.done("ydiag", last)
                    POOLB.after(pe, "xs", n)
                    DVEB.after(pe, "y1", n)
                    PEB.done("state", mm_(px[:], bt[:], xs[:], True, True))
                if has_c:
                    DVEC.after(pe, "xn", nc_)
                    DVEE.after(pe, "acc2", ne)
                    for k in range(KT):
                        last = pe.transpose(pe_[1][:, k * P:(k + 1) * P], xn2[:, k * P:(k + 1) * P], ident[:])
                    PEC.done("h2T", last)
                while todo:
                    a()
                if has_e:
                    DVEE.after(pe, "acc4", ne)
                    PEE.done("wT", pe.transpose(pe_[0][0:NE, 0:P], wg[:], ident[:]))
                    if has_c:
                        ACTC.after(pe, "h1", nc_)
                    experts(pe, 3, te, ne)
                    ACTE.after(pe, "wT", ne)
                    experts(pe, 4, te, ne)
                if t == T - 1 and exists(g, known) and exists(g + 2, known):
                    a1(pe, g + 2, q)

            def experts(pe, i, te, ne):
                a, b = (0, NE + DM) if i == 0 else (NE + DM * (2 * i - 1), min(EC, NE + DM * (2 * i + 1)))
                bank_ = pe_[(1, 1, 0, 1, 0)[i]]
                last = split(bank_[:, 0:b - a], lambda k: h2_hi[:, te % 2, k], lambda k: h2_lo[:, te % 2, k],
                             e_hi, e_lo, slice(a, b))
                if i == 4:
                    last = mm_(bank_[:, DM:2 * DM], wgT[:], eb[:], True, True)
                PEE.done(f"e{i}", last)

            run(pe_e, slots, pre)


_INS = ['L0_attn_hidden_states', 'L0_attn_W_in', 'L0_attn_conv_w', 'L0_attn_conv_b', 'L0_attn_dt_bias', 'L0_attn_A_log',
        'L0_attn_D', 'L0_attn_norm_w', 'L0_attn_W_out', 'L0_ffn_gate_w', 'L0_ffn_gate_b', 'L0_ffn_expert_w',
        'L0_ffn_expert_b', 'L0_c', 'L0_wmod']


def kernel(**inputs):
    import numpy as _np
    import concourse.bacc as _bacc
    from concourse import mybir as _mybir
    from concourse.bass_utils import run_bass_kernel_spmd as _run

    nc = _bacc.Bacc("TRN2", target_bir_lowering=False, num_devices=1)
    arrays, args = {}, []
    for name in _INS:
        a = _np.ascontiguousarray(inputs[name])
        arrays[f"in_{name}_dram"] = a
        args.append(nc.dram_tensor(f"in_{name}_dram", a.shape, _mybir.dt.from_np(a.dtype), kind="ExternalInput").ap())
    shape = inputs['L0_attn_hidden_states'].shape
    args.append(nc.dram_tensor("out_0_dram", shape, _mybir.dt.float32, kind="ExternalOutput").ap())
    adaln_mamba_moe(nc, *args)
    r = _run(nc, [arrays], core_ids=[0])
    return r.results[0]["out_0_dram"]
```

```python
from contextlib import ExitStack

import numpy as np

import concourse.bass as bass
from concourse import mybir

ALU = mybir.AluOpType
ACT = mybir.ActivationFunctionType
AX = mybir.AxisListType
F32 = mybir.dt.float32
F32R = mybir.dt.float32r
BF16 = mybir.dt.bfloat16

P = 128


class Stage:

    def __init__(self, sem, runs, steps):
        self.sem = sem
        self.runs = runs
        self.n = len(steps)
        self.at = {name: i + 1 for i, name in enumerate(steps)}
        assert len(self.at) == self.n
        self.said = 0

    def done(self, name, instruction):
        assert self.at[name] == self.said % self.n + 1, (name, self.said)
        self.said += 1
        return instruction.then_inc(self.sem, 1)

    def after(self, eng, name, run):
        if not isinstance(run, int) or 0 <= run < self.runs:
            eng.wait_ge(self.sem, run * self.n + self.at[name])


def adaln_mamba_moe(nc, x_in, w_in, conv_w, conv_b, dt_bias, a_log, d_skip, norm_w, w_out,
                    gate_w, gate_b, exp_w, exp_b, c_in, w_mod, out):
    NB, L, DM = x_in.shape
    DI = w_out.shape[0]
    NH = a_log.shape[0]
    HD = DI // NH
    CD = conv_w.shape[0]
    TAPS = conv_w.shape[1]
    NS = (CD - DI) // 2
    NE = gate_w.shape[1]
    KT = DM // P
    FT = CD // P
    XT = DI // P
    T = 4
    GT = T * P
    NG = NB * L // GT
    NTILE = NG * T
    GPB = L // GT
    H = TAPS - 1
    EPS = 1e-5
    THRESHOLD = 0.1
    BIG = -1e30
    assert NS == P and DI == 512 and DM == 256 and GPB == 4 and NG % 2 == 0 and FT == 6
    ZH = DI // 2
    ZD = ZH + NH
    CX = DI + NH
    WC = CX + CD
    EC = NE + NE * DM

    x_tok = x_in.rearrange("b l d -> (b l) d")
    out_tok = out.rearrange("b l d -> (b l) d")

    with ExitStack() as ctx:
        def sb(name, shape, dt=F32):
            return ctx.enter_context(nc.sbuf_tensor(name, shape, dt))

        def bank(name):
            return ctx.enter_context(nc.psum_tensor(name, [P, 512], F32))

        def sem(name):
            return ctx.enter_context(nc.semaphore(name))

        pa = [bank("pa0"), bank("pa1")]
        pd = [bank("pd0"), bank("pd1")]
        px = bank("px")
        py = bank("py")
        pe_ = [bank("pe0"), bank("pe1")]

        ident = sb("ident", [P, P])
        identb = sb("identb", [P, P], BF16)
        tri = sb("tri", [P, P])
        sel = sb("sel", [3 * NH, NH, P], BF16)
        negmask = sb("negmask", [P, P], BF16)
        neghalf = sb("neghalf", [P, T])
        eps = sb("eps", [P, T])
        w_hi = sb("w_hi", [P, KT, WC], F32R)
        w_lo = sb("w_lo", [P, KT, WC], F32R)
        e_hi = sb("e_hi", [P, KT, EC], F32R)
        e_lo = sb("e_lo", [P, KT, EC], F32R)
        wo = sb("wo", [P, XT, DM])
        eb = sb("eb", [NE, DM])
        gb_rep = sb("gb_rep", [P, NE])
        cw = sb("cw", [P, FT, TAPS])
        cb = sb("cb", [P, FT])
        nw = sb("nw", [P, XT])
        a_rep = sb("a_rep", [P, NH])
        dtb_rep = sb("dtb_rep", [P, NH])
        d_rep = sb("d_rep", [P, NH])
        cT = sb("cT", [P, KT, NB])
        hc = sb("hc", [P, KT, NB])
        scT = sb("scT", [P, KT, NB])
        expa = sb("expa", [P, NH])
        modT = sb("modT", [P, NB, 4, KT])
        par1 = sb("par1", [P, 2, KT])
        par2 = sb("par2", [P, 2, KT])
        gates = sb("gates", [P, NB, 2, DM])

        xin = sb("xin", [P, T, DM])
        xres = sb("xres", [P, T, DM])
        st1 = sb("st1", [P, 6])
        mv1 = sb("mv1", [P, 2])
        ve1 = sb("ve1", [P, 1])
        rstd1 = sb("rstd1", [P, 1])
        hf = sb("hf", [P, 2, KT, P])
        h_hi = sb("h_hi", [P, 2, KT, GT], F32R)
        h_lo = sb("h_lo", [P, 2, KT, GT], F32R)
        raw = sb("raw", [P, 2, H + GT])
        hist = sb("hist", [P, 2, FT, H])
        acc = sb("acc", [P, 2, GT])
        th = sb("th", [P, 2, GT])
        feat = sb("feat", [P, 2, FT, GT])
        gz = sb("gz", [P, 2, T, DI])
        v = sb("v", [P, T, NH])
        nabs = sb("nabs", [P, T, NH])
        u = sb("u", [P, T, NH])
        w1 = sb("w1", [P, T, NH])
        lnw = sb("lnw", [P, T, NH])
        nc1 = sb("nc1", [P, T, NH])
        sp1 = sb("sp1", [P, T, NH])
        dt = sb("dt", [P, 2, T, NH])
        dA = sb("dA", [P, T, NH])
        e3in = sb("e3in", [P, 3, T, NH])
        e3 = sb("e3", [P, 2, 3, T, NH])
        ncs = sb("ncs", [P, 2, T, NH])
        r1 = sb("r1", [P, T, NH])
        parts = sb("parts", [P, T, 3, NH], BF16)
        csT = sb("csT", [3 * NH, 2, T, P], BF16)

        gbt = sb("gbt", [P, 2, P])
        xt = sb("xt", [P, DI])
        xdt = sb("xdt", [P, DI])
        xs = sb("xs", [P, DI])
        lm = sb("lm", [P, NH, P])
        mm = sb("mm", [P, NH, P])
        gsgn, gabs = lm[0:NB, 0:NH // 2].rearrange("p a n -> p (a n)"), lm[0:NB, NH // 2:].rearrange("p a n -> p (a n)")
        grow = mm[0:NB, 0:NH // 2].rearrange("p a n -> p (a n)")
        zero_or_s = sb("zero_or_s", [P, 2, DI])
        s_even = sb("s_even", [P, DI])
        sres = sb("sres", [P, DI])
        y4 = sb("y4", [P, 2, DI])
        ysq = sb("ysq", [P, DI], BF16)
        ssq = sb("ssq", [P, 2])
        ms = sb("ms", [P, 1])
        rs = sb("rs", [P, 1])
        yT = sb("yT", [P, XT, P])
        x2 = sb("x2", [P, 2, DM])
        st2 = sb("st2", [P, 6])
        mv2 = sb("mv2", [P, 2])
        ve2 = sb("ve2", [P, 1])
        rstd2 = sb("rstd2", [P, 1])
        xn2 = sb("xn2", [P, DM])
        h2f = sb("h2f", [P, KT, P])
        h2_hi = sb("h2_hi", [P, 2, KT, P], F32R)
        h2_lo = sb("h2_lo", [P, 2, KT, P], F32R)
        lg = sb("lg", [P, NE])
        nmax = sb("nmax", [P, 1])
        pexp = sb("pexp", [P, NE])
        sums_ = sb("sums_", [P, 4])
        pr = sb("pr", [P, NE])
        wsel = sb("wsel", [P, NE])
        wg = sb("wg", [P, NE])
        wgT = sb("wgT", [NE, P])
        eacc = sb("eacc", [P, 2, DM])
        ex = sb("ex", [P, 4, DM])
        outb = sb("outb", [P, 2, DM])

        s_ld = sem("s_ld")
        s_xin = [sem(f"s_xin{t}") for t in range(T)]
        s_xres = [sem(f"s_xres{t}") for t in range(T)]
        s_out = [sem("s_out0"), sem("s_out1")]

        POOL0 = Stage(sem("pool_0"), 1, ["z_ident", "ident", "identb", "o_tri", "tri",
                                         "z_neg", "negmask", "z_sel", "sel0", "sel1", "sel2", "neghalf", "eps", "szero", "hist"])
        ACT0 = Stage(sem("act_0"), 1, ["thc", "expa"] + [f"g{b}" for b in range(NB)])
        PE0 = Stage(sem("pe_0"), 1, ["grow", "mod"] + [f"g{b}" for b in range(NB)])
        DVE0 = Stage(sem("dve_0"), 1,
                     ["hc", "scT", "sgn", "abs", "max", "grow"] + [f"m{j}{k}" for j in range(4) for k in range(KT)]
                     + ["cw", "cb", "a_rep"] + [f"w{i}{x}" for i in range(4) for x in ("hi", "lo")]
                     + [f"wo{k}" for k in range(XT)] + ["ghi", "ehi", "glo", "elo"])
        PEN = Stage(sem("pe_n"), NTILE, ["hT"])
        ACTN = Stage(sem("act_n"), NTILE, ["h0", "h1"])
        DVEN = Stage(sem("dve_n"), NTILE, ["st", "par", "mv", "xn", "hi"])
        POOLN = Stage(sem("pool_n"), NTILE, ["ve", "rstd", "lo"])
        PEA = Stage(sem("pe_a"), NG, ["z0", "z1", "ft5", "z2", "z3", "ft4", "cs", "ft0", "ft1", "csT", "ft2", "ft3"])
        ACTA = Stage(sem("act_a"), NG,
                     ["tz0a", "tz0b", "tz1a", "tz1b", "raw5", "acc5", "th5"]
                     + ["tz2a", "tz2b", "tz3a", "tz3b", "u", "ln", "raw4", "acc4", "th4"]
                     + ["raw0", "acc0", "e3", "raw1", "acc1", "csT", "th0", "th1"]
                     + ["raw2", "acc2", "raw3", "acc3", "th2", "th3"])

        def conv_steps(f):
            return [f"halo{f}", f"tap{f}a", f"tap{f}b", f"tap{f}c", f"hist{f}"]
        DVEA = Stage(sem("dve_a"), NG,
                     ["gz0a", "gz0b", "dtb0", "gz1a", "gz1b", "dtb1"] + conv_steps(5) + ["silu5"]
                     + ["gz2a", "gz2b", "dtb2", "gz3a", "gz3b", "dtb3", "nabs", "w1", "nc1", "sp1", "dt", "dA"]
                     + conv_steps(4) + ["silu4"]
                     + ["cs", "dcs", "ncs", "p0", "r1", "p1", "p2"]
                     + conv_steps(0) + ["silu0"] + conv_steps(1) + ["silu1"]
                     + conv_steps(2) + ["silu2"] + conv_steps(3) + ["silu3"])
        PEB = Stage(sem("pe_b"), NTILE, ["D", "G", "xT", "yoff", "ydiag", "state"])
        ACTB = Stage(sem("act_b"), NTILE, ["bt"] + [f"L{h}" for h in range(4)] + ["xt"] + [f"L{h}" for h in range(4, NH)] + ["sq"])
        DVEB = Stage(sem("dve_b"), NTILE, ["M", "y1", "y3", "y4", "S"])
        DVES = Stage(sem("dve_s"), NG // 2, ["sres"])
        POOLB = Stage(sem("pool_b"), NTILE, ["xdt", "xs", "scd", "xd", "y2"])
        PEC = Stage(sem("pe_c1"), NTILE, ["yT", "wout", "h2T"])
        ACTC = Stage(sem("act_c1"), NTILE, ["yT", "h0", "h1"])
        DVEC = Stage(sem("dve_c1"), NTILE, ["o1", "st", "par", "mv", "xn", "hi"])
        POOLC = Stage(sem("pool_c1"), NTILE, ["ms", "rs", "x2", "ve", "rstd", "lo"])
        PEE = Stage(sem("pe_e"), NTILE, ["e0", "e1", "e2", "wT", "e3", "e4"])
        ACTE = Stage(sem("act_e"), NTILE, ["exp", "ex3", "ex4", "wT", "ex5", "ex6"])
        DVEE = Stage(sem("dve_e"), NTILE, ["lg", "max", "rsum", "rp", "pr", "wsel", "rw", "rz", "rr", "wg",
                                           "acc0", "acc1", "acc2", "acc7", "bias"])
        POOLE = Stage(sem("pool_e"), NTILE, ["a34", "a56", "a3456", "all", "og", "out"])

        pa1_bf = pa[1][:].bitcast(BF16)

        feat_flat = feat[:].rearrange("p a f n -> p (a f n)")
        stage_w = feat_flat[:, 0:KT * WC].rearrange("p (k n) -> p k n", k=KT)
        stage_m = feat_flat[:, KT * WC:KT * (WC + 6 * DM)].rearrange("p (k n) -> p k n", k=KT)
        stage_e = gz[:].rearrange("p a t n -> p (a t n)").rearrange("p (k n) -> p k n", k=KT)
        stage_g = xres[:, 0, 0:KT * NE].rearrange("p (k n) -> p k n", k=KT)

        all_ones = tri[:, P - 1:P].to_broadcast([P, P])

        def rep(ap, n, w):
            return ap[:, None, :].to_broadcast([P, n, w])

        def spread(ap, n, w):
            return ap[:, :, None].to_broadcast([P, n, w])

        class Tile:
            def __init__(self, p, m, back):
                m -= back
                self.p, m = p + m // (2 * T), m % (2 * T)
                self.q, self.t = m // T, m % T
                self.g = 2 * self.p + self.q
                self.n = 2 * T * self.p + m
                self.batch = self.p // (GPB // 2)
                self.exists = not isinstance(p, int) or 0 <= self.p < NG // 2
                self.tok = slice(self.t * P, (self.t + 1) * P)

        def run(eng, order, steps, end=NG // 2 - 1):
            def pair(p, ms):
                for m in ms:
                    for name, back in order[m % T]:
                        x = Tile(p, m, back)
                        if x.exists:
                            steps[name](eng, x)
            pair(-1, range(2 * T))
            pair(0, range(2 * T))
            with eng.Fori(1, end) as p:
                pair(p, range(2 * T))
            for p in range(end, NG // 2):
                pair(p, range(2 * T))
            pair(NG // 2, range(T))

        def state_of(x):
            return zero_or_s[:, 1] if x.t % 2 else s_even[:]

        def state_before(x):
            if x.q == 0 and x.t == 0:
                return sres[:]
            return s_even[:] if x.t % 2 else zero_or_s[:, 1]

        def state_ready(eng, x):
            if x.q == 0 and x.t == 0:
                DVES.after(eng, "sres", x.p)
            else:
                DVEB.after(eng, "S", x.n - 1)

        def mods_of(b, kind):
            return modT[:, bass.ds(b, 1), kind:kind + 2].rearrange("p b a k -> p (b a k)")

        def gate_of(b, i):
            return gates[:, bass.ds(b, 1), i].rearrange("p a n -> p (a n)")

        BANK = {"ft5": 0, "ft4": 0, "cs": 0, "ft0": 1, "ft1": 0, "csT": 1, "ft2": 0, "ft3": 1}
        HT_BANK = [1, 1, 1, 0]
        FTS = [5, 4, 0, 1, 2, 3]

        def turn(f):
            return FTS.index(f) % 2

        def two_back(eng, stage, step, f, g):
            i = FTS.index(f)
            stage.after(eng, f"{step}{FTS[(i - 2) % FT]}", g if i >= 2 else g - 1)

        POOL_ORDER = [
            [("n_lo", -6), ("n_rstd", -7), ("lo", 3), ("rs", 2), ("a34", 4), ("a56", 4), ("xdt", 1), ("all", 4), ("xs", 1),
             ("scd", 1), ("og", 4), ("out", 4), ("xd", 1), ("x2", 2), ("y2", 1), ("rstd", 2), ("n_lo", -7), ("n_rstd", -8),
             ("a34", 3), ("lo", 2), ("rs", 1), ("a56", 3), ("all", 3), ("xdt", 0), ("xs", 0), ("scd", 0), ("og", 3),
             ("out", 3), ("xd", 0), ("x2", 1), ("rstd", 1), ("y2", 0), ("n_lo", -8)],
            [("n_rstd", -8), ("a34", 3), ("lo", 2), ("rs", 1), ("a56", 3), ("xdt", 0), ("all", 3), ("xs", 0), ("scd", 0),
             ("og", 3), ("xd", 0), ("y2", 0), ("out", 3), ("n_lo", -8), ("x2", 1)],
            [],
            [("rstd", 3), ("n_rstd", -7), ("xdt", 1), ("xs", 1), ("a34", 4), ("lo", 3), ("rs", 2), ("a56", 4), ("all", 4),
             ("scd", 1), ("og", 4), ("out", 4), ("xd", 1), ("x2", 2), ("y2", 1), ("rstd", 2)]]
        PE_ORDER = [
            [("yT", 1), ("yoff", 0), ("z1", -4), ("wout", 1), ("e1", 2), ("ydiag", 0), ("hT", -8), ("ft5", -4), ("e2", 2),
             ("h2T", 1), ("state", 0)],
            [("D", 0), ("G", 0), ("e3", 3), ("e4", 3), ("xT", 0), ("z2", -4), ("e0", 2), ("yoff", 0), ("yT", 1), ("z3", -4),
             ("wout", 1), ("ydiag", 0), ("hT", -8), ("ft4", -4), ("state", 0)],
            [("D", 0), ("G", 0), ("e1", 3), ("xT", 0), ("e2", 3), ("h2T", 2), ("cs", -4), ("yoff", 0), ("e3", 3), ("e4", 3),
             ("e0", 2), ("ft0", -4), ("yT", 1), ("ft1", -4), ("wout", 1), ("csT", -4), ("ydiag", 0), ("hT", -8), ("e1", 2),
             ("e2", 2), ("state", 0), ("h2T", 1)],
            [("D", 0), ("G", 0), ("e3", 3), ("e4", 3), ("xT", 0), ("e0", 2), ("ft2", -4), ("ft3", -4), ("yT", 1),
             ("yoff", 0), ("wout", 1), ("hT", -8), ("ydiag", 0), ("e1", 2), ("e2", 2), ("state", 0), ("h2T", 1), ("D", -1),
             ("G", -1), ("e3", 2), ("z0", -8), ("e4", 2), ("e0", 1), ("xT", -1)]]
        ACT_ORDER = [
            [("exp", 3), ("L47", 1), ("th1", 0), ("yT", 2), ("raw2", 0), ("raw3", 0), ("n_h", -7), ("ex34", 3), ("th2", 0),
             ("h2", 2), ("sq", 1), ("wT", 3), ("ex56", 3), ("bt", 0), ("th3", 0), ("tz0", -4), ("L03", 0), ("xt", 0),
             ("exp", 2), ("L47", 0), ("yT", 1), ("tz1", -4), ("n_h", -8), ("raw5", -4), ("ex34", 2), ("h2", 1), ("sq", 0),
             ("bt", -1), ("wT", 2)],
            [("L03", 0), ("ex56", 3), ("th5", -4), ("xt", 0), ("tz2", -4), ("L47", 0), ("exp", 2), ("yT", 1), ("tz3", -4),
             ("u", -4), ("n_h", -8), ("ln", -4), ("raw4", -4), ("sq", 0), ("bt", -1)],
            [("L03", 0), ("xt", 0), ("ex34", 3), ("h2", 2), ("L47", 0), ("wT", 3), ("ex56", 3), ("th4", -4), ("exp", 2),
             ("yT", 1), ("raw0", -4), ("decays", -4), ("raw1", -4), ("csT", -4), ("n_h", -8), ("ex34", 2), ("h2", 1),
             ("th0", -4), ("sq", 0), ("bt", -1), ("wT", 2), ("ex56", 2)],
            [("L03", 0), ("xt", 0)]]
        DVE_ORDER = [
            [("M", 1), ("soft3", 3), ("silu1", 0), ("t2a", 0), ("o1", 2), ("y1", 1), ("t2b", 0), ("st", 2), ("t2c", 0),
             ("mv", 2), ("n_hi", -7), ("acc12", 3), ("xn", 2), ("y3", 1), ("n_st", -8), ("y4", 1), ("silu2", 0), ("t3a", 0),
             ("hi", 2), ("t3b", 0), ("t3c", 0), ("S", 1), ("silu3", 0), ("acc7", 3), ("bias", 3), ("soft1", 2), ("sres", 0),
             ("gz0", -4), ("soft2", 2), ("n_xn", -8), ("soft3", 2), ("M", 0), ("gz1", -4), ("o1", 1), ("acc12", 2),
             ("st", 1), ("mv", 1), ("y1", 0), ("xn", 1), ("n_hi", -8)],
            [("n_st", -8), ("y3", 1), ("y4", 1), ("t5a", -4), ("S", 1), ("t5b", -4), ("hi", 2), ("t5c", -4), ("acc7", 3),
             ("n_xn", -8), ("bias", 3), ("silu5", -4), ("gz2", -4), ("soft1", 2), ("M", 0), ("soft2", 2), ("y1", 0),
             ("gz3", -4), ("nabs", -4), ("soft3", 2), ("w1", -4), ("n_hi", -8)],
            [("n_st", -8), ("y3", 1), ("o1", 2), ("y4", 1), ("S", 1), ("st", 2), ("mv", 2), ("acc12", 3), ("xn", 2),
             ("dt", -4), ("t4a", -4), ("t4b", -4), ("hi", 2), ("t4c", -4), ("n_xn", -8), ("M", 0), ("y1", 0), ("acc7", 3),
             ("bias", 3), ("soft1", 2)],
            [("silu4", -4), ("cs", -4), ("soft2", 3), ("parts", -4), ("soft3", 3), ("o1", 2), ("t0a", -4), ("t0b", -4),
             ("st", 2), ("mv", 2), ("y3", 1), ("acc12", 3), ("xn", 2), ("n_hi", -7), ("n_st", -8), ("t0c", -4), ("y4", 1),
             ("hi", 2), ("silu0", -4), ("t1a", -4), ("S", 1), ("t1b", -4), ("acc7", 3), ("n_xn", -8), ("bias", 3),
             ("soft1", 2), ("t1c", -4), ("soft2", 2)]]

        block = ctx.enter_context(nc.Block())

        loads = []

        def load(dst, src):
            loads.append((dst, src))

        wv = w_in.rearrange("(k p) n -> p k n", p=P)
        for k in range(KT):
            load(cT[:, k], c_in[:, k * P:(k + 1) * P].rearrange("b p -> p b"))
        for dst, src in ((gb_rep, gate_b), (a_rep, a_log), (dtb_rep, dt_bias), (d_rep, d_skip)):
            load(dst[:], src.rearrange("(o n) -> o n", o=1).to_broadcast([P, src.shape[0]]))
        load(stage_m, w_mod.rearrange("(k p) n -> p k n", p=P))
        load(stage_w[:, :, 0:ZH], wv[:, :, 0:ZH])
        load(stage_w[:, :, ZH:ZD], wv[:, :, DI + CD:])
        load(stage_w[:, :, ZD:WC], wv[:, :, ZH:DI + CD])
        load(cw[:], conv_w.rearrange("(f p) k -> p f k", p=P))
        load(cb[:], conv_b.rearrange("(f p) -> p f", p=P))
        load(nw[:], norm_w.rearrange("(f p) -> p f", p=P))
        load(wo[:], w_out.rearrange("(k p) n -> p k n", p=P))
        load(eb[:], exp_b)
        load(stage_g, gate_w.rearrange("(k p) n -> p k n", p=P))
        for k in range(KT):
            load(stage_e[:, k].rearrange("p (e n) -> p e n", e=NE), exp_w[:, k * P:(k + 1) * P, :].rearrange("e p n -> p e n"))
        LOADED = 16 * len(loads)

        @block.sync
        def _(sp):
            def x_of(n):
                return x_tok[bass.ds(n * P, P), :]

            for t in range(T):
                sp.dma_start(xin[:, t], x_of(t)).then_inc(s_xin[t], 16)
            for dst, src in loads:
                with nc.allow_non_contiguous_dma(reason="small vectors, once"):
                    sp.dma_start(dst, src).then_inc(s_ld, 16)

            def load_xin(sp, x):
                if x.exists and (not isinstance(x.g, int) or x.g + 1 < NG):
                    PEN.after(sp, "hT", x.n)
                    sp.dma_start(xin[:, x.t], x_of(x.n + T)).then_inc(s_xin[x.t], 16)

            def load_xres(sp, x):
                if isinstance(x.g, int) and x.g == 0:
                    DVE0.after(sp, "glo", 0)
                POOLC.after(sp, "x2", x.n - T)
                sp.dma_start(xres[:, x.t], x_of(x.n)).then_inc(s_xres[x.t], 16)

            def store(sp, x):
                POOLE.after(sp, "out", x.n)
                sp.dma_start(out_tok[bass.ds(x.n * P, P), :], outb[:, x.t % 2]).then_inc(s_out[x.t % 2], 16)

            run(sp, [[("store", 3), ("xres", -2), ("xin", -2 * T)]] * T, {"xin": load_xin, "xres": load_xres, "store": store},
                end=NG // 2 - 2)
            for o in s_out:
                sp.wait_ge(o, 16 * NTILE // 2)

        @block.gpsimd
        def _(pool):
            D0 = POOL0.done

            def own(name):
                POOL0.after(pool, name, 0)
            D0("z_ident", pool.memset(ident[:], 0.0))
            own("z_ident")
            D0("ident", pool.affine_select(out=ident[:], in_=ident[:], compare_op=ALU.not_equal, fill=1.0,
                                           base=0, pattern=[[-1, P]], channel_multiplier=1))
            own("ident")
            D0("identb", pool.tensor_copy(identb[:], ident[:]))
            D0("o_tri", pool.memset(tri[:], 1.0))
            own("o_tri")
            D0("tri", pool.affine_select(out=tri[:], in_=tri[:], compare_op=ALU.is_ge, fill=0.0,
                                         base=0, pattern=[[1, P]], channel_multiplier=-1))
            D0("z_neg", pool.memset(negmask[:], 0.0))
            own("z_neg")
            D0("negmask", pool.affine_select(out=negmask[:], in_=negmask[:], compare_op=ALU.is_ge, fill=BIG,
                                             base=0, pattern=[[1, P]], channel_multiplier=-1))
            D0("z_sel", pool.memset(sel[:], 0.0))
            own("z_sel")
            for part in range(3):
                D0(f"sel{part}", pool.affine_select(out=sel[:], in_=sel[:], compare_op=ALU.not_equal, fill=1.0,
                                                    base=-part * NH, pattern=[[-1, NH], [0, P]], channel_multiplier=1))
                own(f"sel{part}")
            D0("neghalf", pool.memset(neghalf[:], -0.5))
            D0("eps", pool.memset(eps[:], EPS))
            D0("szero", pool.memset(zero_or_s[:], 0.0))
            D0("hist", pool.memset(hist[:], 0.0))
            own("eps")

            def n_rstd(pool, x):
                DVEN.after(pool, "mv", x.n)
                POOLN.after(pool, "rstd", x.n - 1)
                POOLN.done("ve", pool.tensor_tensor(ve1[:], mv1[:, 1:2], eps[:, 0:1], ALU.add))
                POOLN.after(pool, "ve", x.n)
                DVEN.after(pool, "xn", x.n - 1)
                POOLN.done("rstd", pool.tensor_tensor(rstd1[:], ve1[:], neghalf[:, 0:1], ALU.pow))

            def n_lo(pool, x):
                DVEN.after(pool, "hi", x.n)
                PEA.after(pool, "ft3", x.g - 2)
                POOLN.done("lo", pool.tensor_tensor(h_lo[:, x.q, :, x.tok], hf[:, x.t % 2],
                                                    h_hi[:, x.q, :, x.tok].bitcast(F32), ALU.subtract))

            def xdt_(pool, x):
                ACTB.after(pool, "xt", x.n)
                DVEA.after(pool, "dt", x.g)
                PEB.after(pool, "ydiag", x.n - 1)
                POOLB.done("xdt", pool.tensor_tensor(xdt[:], xt[:], spread(dt[:, x.q, x.t], NH, HD), ALU.mult))

            def xs_(pool, x):
                ACTA.after(pool, "e3", x.g)
                POOLB.after(pool, "xdt", x.n)
                PEB.after(pool, "state", x.n - 1)
                POOLB.done("xs", pool.tensor_tensor(xs[:], xdt[:], spread(e3[:, x.q, 1, x.t], NH, HD), ALU.mult))

            def xd_(pool, x):
                POOLB.after(pool, "xdt", x.n)
                POOLB.done("xd", pool.tensor_tensor(xt[:], xt[:], spread(d_rep[:], NH, HD), ALU.mult))

            def scd_(pool, x):
                POOLE.after(pool, "all", x.n - 3)
                state_ready(pool, x)
                PEB.after(pool, "yoff", x.n - 1)
                POOLB.after(pool, "scd", x.n - 1)
                POOLB.done("scd", pool.tensor_tensor(state_of(x), state_before(x), spread(e3[:, x.q, 2, x.t], NH, HD), ALU.mult))

            def y2_(pool, x):
                DVEB.after(pool, "y1", x.n)
                POOLB.after(pool, "xd", x.n)
                POOLB.done("y2", pool.tensor_tensor(y4[:, x.t % 2], y4[:, x.t % 2], xt[:], ALU.add))

            def c_rs(pool, x):
                ACTB.after(pool, "sq", x.n)
                POOLC.after(pool, "rs", x.n - 1)
                POOLC.done("ms", pool.tensor_tensor(ms[:], ssq[:, x.t % 2:x.t % 2 + 1], eps[:, 0:1], ALU.add))
                POOLC.after(pool, "ms", x.n)
                DVEC.after(pool, "o1", x.n - 1)
                POOLC.done("rs", pool.tensor_tensor(rs[:], ms[:], neghalf[:, 0:1], ALU.pow))

            def c_x2(pool, x):
                DVEC.after(pool, "o1", x.n)
                pool.wait_ge(s_xres[x.t], 16 * (x.g + 1))
                POOLC.done("x2", pool.tensor_tensor(x2[:, x.t % 2], x2[:, x.t % 2], xres[:, x.t], ALU.add))

            def c_rstd(pool, x):
                DVEC.after(pool, "mv", x.n)
                POOLC.after(pool, "rstd", x.n - 1)
                POOLC.done("ve", pool.tensor_tensor(ve2[:], mv2[:, 1:2], eps[:, 0:1], ALU.add))
                POOLC.after(pool, "ve", x.n)
                DVEC.after(pool, "xn", x.n - 1)
                POOLC.done("rstd", pool.tensor_tensor(rstd2[:], ve2[:], neghalf[:, 0:1], ALU.pow))

            def c_lo(pool, x):
                DVEC.after(pool, "hi", x.n)
                PEE.after(pool, "e4", x.n - 2)
                POOLC.done("lo", pool.tensor_tensor(h2_lo[:, x.t % 2], h2f[:], h2_hi[:, x.t % 2].bitcast(F32), ALU.subtract))

            def e_34(pool, x):
                ACTE.after(pool, "ex4", x.n)
                POOLE.done("a34", pool.tensor_tensor(ex[:, 0], ex[:, 0], ex[:, 1], ALU.add))

            def e_56(pool, x):
                ACTE.after(pool, "ex6", x.n)
                POOLE.done("a56", pool.tensor_tensor(ex[:, 2], ex[:, 2], ex[:, 3], ALU.add))
                POOLE.after(pool, "a56", x.n)
                POOLE.done("a3456", pool.tensor_tensor(ex[:, 0], ex[:, 0], ex[:, 2], ALU.add))

            def e_all(pool, x):
                DVEE.after(pool, "bias", x.n)
                POOLE.after(pool, "a3456", x.n)
                POOLE.done("all", pool.tensor_tensor(ex[:, 0], ex[:, 0], eacc[:, 0], ALU.add))

            def e_og(pool, x):
                if isinstance(x.n, int):
                    POOLE.after(pool, "all", x.n)
                POOLE.done("og", pool.tensor_tensor(ex[:, 0], ex[:, 0], gate_of(x.batch, 1), ALU.mult))

            def e_out(pool, x):
                POOLE.after(pool, "og", x.n)
                if not isinstance(x.n, int) or x.n >= 2:
                    pool.wait_ge(s_out[x.t % 2], 8 * (x.n - x.t % 2))
                POOLE.done("out", pool.tensor_tensor(outb[:, x.t % 2], ex[:, 0], x2[:, x.t % 2], ALU.add))

            run(pool, POOL_ORDER,
                {"n_rstd": n_rstd, "n_lo": n_lo, "xdt": xdt_, "xs": xs_, "xd": xd_, "scd": scd_, "y2": y2_, "rs": c_rs,
                 "x2": c_x2, "rstd": c_rstd, "lo": c_lo, "a34": e_34, "a56": e_56, "all": e_all, "og": e_og, "out": e_out})

        @block.scalar
        def _(act):
            act.wait_ge(s_ld, LOADED)
            ACT0.done("thc", act.activation(scT[:], cT[:], ACT.Tanh, scale=0.5))
            ACT0.done("expa", act.activation(expa[:], a_rep[:], ACT.Exp))
            for b in range(NB):
                PE0.after(act, f"g{b}", 0)
                ACT0.done(f"g{b}", act.activation(gates[:, b].rearrange("p a n -> p (a n)"), pe_[b % 2][:], ACT.Copy))

            def n_h(act, x):
                PEN.after(act, "hT", x.n)
                DVEN.after(act, "hi", x.n - 2)
                POOLN.after(act, "lo", x.n - 2)
                for k in range(KT):
                    ACTN.done(f"h{k}", act.activation(hf[:, x.t % 2, k], pa[HT_BANK[x.t]][:, k * P:(k + 1) * P], ACT.Identity,
                                                      bias=par1[:, 0, k:k + 1], scale=par1[:, 1, k:k + 1]))

            def z(i):
                def piece(act, x):
                    PEA.after(act, f"z{i}", x.g)
                    if i == 0:
                        DVEB.after(act, "y4", T * (x.g - 2) + T - 1)
                    for half in range(2):
                        ACTA.done(f"tz{i}{'ab'[half]}", act.activation(
                            gz[:, x.q, i, half * ZH:(half + 1) * ZH], pa[half][:, 0:ZH], ACT.Tanh))
                return piece

            def raws(f):
                def piece(act, x):
                    b = pa[BANK[f"ft{f}"]]
                    PEA.after(act, f"ft{f}", x.g)
                    two_back(act, DVEA, "hist", f, x.g)
                    ACTA.done(f"raw{f}", act.activation(raw[:, turn(f), H:], b[:], ACT.Copy))
                    two_back(act, DVEA, "silu", f, x.g)
                    ACTA.done(f"acc{f}", act.activation(acc[:, turn(f)], b[:], ACT.Identity,
                                                        bias=cb[:, f:f + 1], scale=cw[:, f, H:H + 1]))
                return piece

            def tanh(f):
                def piece(act, x):
                    DVEA.after(act, f"tap{f}c", x.g)
                    ACTA.done(f"th{f}", act.activation(th[:, turn(f)], acc[:, turn(f)], ACT.Tanh))
                return piece

            def exp_u(act, x):
                DVEA.after(act, "nabs", x.g)
                DVEA.after(act, "nc1", x.g - 1)
                ACTA.done("u", act.activation(u[:], nabs[:], ACT.Exp))

            def ln_w(act, x):
                DVEA.after(act, "w1", x.g)
                DVEA.after(act, "sp1", x.g - 1)
                ACTA.done("ln", act.activation(lnw[:], w1[:], ACT.Ln))

            def decays(act, x):
                DVEA.after(act, "dcs", x.g)
                ACTA.done("e3", act.activation(e3[:, x.q], e3in[:], ACT.Exp))

            def cs_rows(act, x):
                PEA.after(act, "csT", x.g)
                ACTA.done("csT", act.activation(csT[:, x.q].rearrange("p t n -> p (t n)"), pa1_bf[0:3 * NH, 0:GT], ACT.Copy))

            def bt_(act, x):
                PEB.after(act, "G", x.n)
                PEB.after(act, "state", x.n - 1)
                DVEB.after(act, "M", x.n - 1)
                ACTB.done("bt", act.activation(gbt[:].rearrange("p a n -> p (a n)"), py[:, 0:2 * P], ACT.Copy))

            def decay(h0, h1):
                def step(act, x):
                    PEB.after(act, "D", x.n)
                    DVEB.after(act, "M", x.n - 1)
                    for h in range(h0, h1):
                        ACTB.done(f"L{h}", act.activation(lm[:, h], pd[h // 4][:, h % 4 * P:(h % 4 + 1) * P], ACT.Exp,
                                                          bias=ncs[:, x.q, x.t, h:h + 1]))
                return step

            def xt_(act, x):
                PEB.after(act, "xT", x.n)
                POOLB.after(act, "y2", x.n - 1)
                ACTB.done("xt", act.activation(xt[:], px[:], ACT.Copy))

            def sq_(act, x):
                DVEB.after(act, "y4", x.n)
                POOLC.after(act, "ms", x.n - 2)
                ACTB.done("sq", act.activation(ysq[:], y4[:, x.t % 2], ACT.Square, scale=DI ** -0.5,
                                               accum_out=ssq[:, x.t % 2:x.t % 2 + 1]))

            def yT_(act, x):
                PEC.after(act, "yT", x.n)
                PEC.after(act, "wout", x.n - 1)
                ACTC.done("yT", act.activation(yT[:].rearrange("p f n -> p (f n)"), pe_[0][:], ACT.Copy))

            def h2(act, x):
                PEC.after(act, "h2T", x.n)
                DVEC.after(act, "hi", x.n - 1)
                POOLC.after(act, "lo", x.n - 1)
                for k in range(KT):
                    ACTC.done(f"h{k}", act.activation(h2f[:, k], pe_[1][:, k * P:(k + 1) * P], ACT.Identity,
                                                      bias=par2[:, 0, k:k + 1], scale=par2[:, 1, k:k + 1]))

            def exp_(act, x):
                DVEE.after(act, "max", x.n)
                DVEE.after(act, "pr", x.n - 1)
                ACTE.done("exp", act.activation(pexp[:], lg[:], ACT.Exp, bias=nmax[:]))

            def expert_pair(e0, bank_, product):
                def step(act, x):
                    DVEE.after(act, "wg", x.n)
                    PEE.after(act, product, x.n)
                    POOLE.after(act, "out" if e0 == 3 else "a3456", x.n - 1)
                    for e in (e0, e0 + 1):
                        ACTE.done(f"ex{e}", act.activation(ex[:, e - 3], pe_[bank_][:, (e - e0) * DM:(e - e0 + 1) * DM],
                                                           ACT.Copy, scale=wg[:, e:e + 1]))
                return step

            def wT_(act, x):
                PEE.after(act, "wT", x.n)
                PEE.after(act, "e4", x.n - 1)
                ACTE.done("wT", act.activation(wgT[:], pe_[0][0:NE, 0:P], ACT.Copy))

            run(act, ACT_ORDER,
                {"n_h": n_h, "bt": bt_, "L03": decay(0, 4), "L47": decay(4, NH), "xt": xt_, "sq": sq_, "yT": yT_, "h2": h2,
                 "exp": exp_, "ex34": expert_pair(3, 0, "e2"), "ex56": expert_pair(5, 1, "e3"), "wT": wT_, "u": exp_u, "ln": ln_w, "decays": decays, "csT": cs_rows}
                | {f"tz{i}": z(i) for i in range(T)} | {f"raw{f}": raws(f) for f in FTS} | {f"th{f}": tanh(f) for f in FTS})

        @block.vector
        def _(dve):
            D0 = DVE0.done

            def own(name):
                DVE0.after(dve, name, 0)
            dve.wait_ge(s_ld, LOADED)
            D0("hc", dve.tensor_scalar(hc[:], cT[:], 0.5, None, ALU.mult))
            own("hc")
            ACT0.after(dve, "thc", 0)
            D0("scT", dve.scalar_tensor_tensor(out=scT[:], in0=scT[:], scalar=1.0, in1=hc[:], op0=ALU.add, op1=ALU.mult))
            PE0.after(dve, "grow", 0)
            D0("sgn", dve.tensor_scalar(gsgn, pe_[0][0:NB, :], 0.0, 2.0, ALU.is_ge, ALU.mult))
            D0("abs", dve.tensor_scalar(gabs, pe_[0][0:NB, :], -1.0, None, ALU.mult))
            own("abs")
            D0("max", dve.scalar_tensor_tensor(out=gabs, in0=gabs, scalar=0.25, in1=pe_[0][0:NB, :], op0=ALU.max, op1=ALU.max))
            own("max")
            D0("grow", dve.scalar_tensor_tensor(out=grow, in0=gsgn, scalar=-1.0, in1=gabs, op0=ALU.add, op1=ALU.mult))
            PE0.after(dve, "mod", 0)
            for j in range(4):
                for k in range(KT):
                    c0 = (j * KT + k) * NB
                    D0(f"m{j}{k}", dve.tensor_scalar(modT[:, :, j, k], pd[0][:, c0:c0 + NB], float(j % 2), None, ALU.add))
            D0("cw", dve.tensor_scalar(cw[:], cw[:], 0.5, None, ALU.mult))
            D0("cb", dve.tensor_scalar(cb[:], cb[:], 0.5, None, ALU.mult))
            ACT0.after(dve, "expa", 0)
            D0("a_rep", dve.tensor_scalar(a_rep[:], expa[:], -1.0, None, ALU.mult))
            for i, (a, b, f) in enumerate(((0, ZH, 0.5), (ZH, ZD, 1.0), (ZD, CX, 0.5), (CX, WC, 1.0))):
                D0(f"w{i}hi", dve.tensor_scalar(w_hi[:, :, a:b], stage_w[:, :, a:b], f, None, ALU.mult))
                own(f"w{i}hi")
                D0(f"w{i}lo", dve.scalar_tensor_tensor(out=w_lo[:, :, a:b], in0=stage_w[:, :, a:b], scalar=f,
                                                       in1=w_hi[:, :, a:b].bitcast(F32), op0=ALU.mult, op1=ALU.subtract))
            for k in range(XT):
                D0(f"wo{k}", dve.tensor_scalar(wo[:, k], wo[:, k], nw[:, k:k + 1], None, ALU.mult))
            D0("ghi", dve.tensor_copy(e_hi[:, :, 0:NE], stage_g))
            D0("ehi", dve.tensor_copy(e_hi[:, :, NE:EC], stage_e))
            own("ehi")
            D0("glo", dve.tensor_tensor(e_lo[:, :, 0:NE], stage_g, e_hi[:, :, 0:NE].bitcast(F32), ALU.subtract))
            D0("elo", dve.tensor_tensor(e_lo[:, :, NE:EC], stage_e, e_hi[:, :, NE:EC].bitcast(F32), ALU.subtract))
            own("elo")
            POOL0.after(dve, "hist", 0)
            ACT0.after(dve, f"g{NB - 1}", 0)

            def n_st(dve, x):
                dve.wait_ge(s_xin[x.t], 16 * (x.g + 1))
                DVEN.done("st", dve.bn_stats(st1[:], xin[:, x.t]))
                ACTN.after(dve, "h1", x.n - 1)
                POOLN.after(dve, "ve", x.n - 1)
                DVEN.after(dve, "st", x.n)
                DVEN.done("par", dve.tensor_scalar(par1[:].rearrange("p a k -> p (a k)"), mods_of(x.batch, 0), 1.0, None, ALU.mult))
                DVEN.done("mv", dve.bn_aggr(mv1[:], st1[:]))

            def n_xn(dve, x):
                POOLN.after(dve, "rstd", x.n)
                DVEN.done("xn", dve.tensor_scalar(xin[:, x.t], xin[:, x.t], mv1[:, 0:1], rstd1[:], ALU.subtract, ALU.mult))

            def n_hi(dve, x):
                ACTN.after(dve, "h1", x.n)
                PEA.after(dve, "ft3", x.g - 2)
                DVEN.done("hi", dve.tensor_copy(h_hi[:, x.q, :, x.tok], hf[:, x.t % 2]))

            def z(i):
                def piece(dve, x):
                    for half in range(2):
                        ACTA.after(dve, f"tz{i}{'ab'[half]}", x.g)
                        g_ = gz[:, x.q, i, half * ZH:(half + 1) * ZH]
                        DVEA.done(f"gz{i}{'ab'[half]}", dve.scalar_tensor_tensor(
                            out=g_, in0=g_, scalar=1.0, in1=pa[half][:, 0:ZH], op0=ALU.add, op1=ALU.mult))
                    DVEA.done(f"dtb{i}", dve.tensor_tensor(v[:, i], pa[0][:, ZH:ZD], dtb_rep[:], ALU.add))
                return piece

            def tap(f, j):
                def piece(dve, x):
                    A = DVEA.done
                    if j == 0:
                        ACTA.after(dve, f"acc{f}", x.g)
                        sel_ = (x.p % (GPB // 2)) if x.q == 0 else 1
                        A(f"halo{f}", dve.tensor_copy(raw[:, turn(f), 0:H].rearrange("p (a n) -> p a n", a=1),
                                                      hist[:, bass.ds(sel_, 1), f]))
                        DVEA.after(dve, f"halo{f}", x.g)
                    else:
                        DVEA.after(dve, f"tap{f}{'abc'[j - 1]}", x.g)
                    A(f"tap{f}{'abc'[j]}", dve.scalar_tensor_tensor(
                        out=acc[:, turn(f)], in0=raw[:, turn(f), j:j + GT], scalar=cw[:, f, j:j + 1], in1=acc[:, turn(f)],
                        op0=ALU.mult, op1=ALU.add))
                    if j == H - 1:
                        A(f"hist{f}", dve.tensor_copy(hist[:, 1, f], raw[:, turn(f), GT:GT + H]))
                return piece

            def silu(f):
                def piece(dve, x):
                    ACTA.after(dve, f"th{f}", x.g)
                    PEB.after(dve, "yoff", T * (x.g - 2) + T - 1)
                    DVEA.done(f"silu{f}", dve.scalar_tensor_tensor(
                        out=feat[:, x.q, f], in0=th[:, turn(f)], scalar=1.0, in1=acc[:, turn(f)], op0=ALU.add, op1=ALU.mult))
                return piece

            def nabs_(dve, x):
                DVEA.after(dve, "dtb3", x.g)
                DVEA.done("nabs", dve.scalar_tensor_tensor(out=nabs[:], in0=v[:], scalar=-1.0, in1=v[:], op0=ALU.mult, op1=ALU.min))

            def w1_(dve, x):
                ACTA.after(dve, "u", x.g)
                DVEA.done("w1", dve.tensor_scalar(w1[:], u[:], 1.0, None, ALU.add))
                DVEA.after(dve, "w1", x.g)
                DVEA.done("nc1", dve.scalar_tensor_tensor(out=nc1[:], in0=w1[:], scalar=1.0, in1=u[:], op0=ALU.subtract, op1=ALU.subtract))

            def dt_(dve, x):
                ACTA.after(dve, "ln", x.g)
                DVEA.done("sp1", dve.scalar_tensor_tensor(out=sp1[:], in0=v[:], scalar=0.0, in1=lnw[:], op0=ALU.max, op1=ALU.add))
                DVEA.after(dve, "sp1", x.g)
                POOLB.after(dve, "xdt", T * (x.g - 2) + T - 1)
                DVEA.done("dt", dve.tensor_tensor(dt[:, x.q], sp1[:], nc1[:], ALU.subtract))
                DVEA.after(dve, "dt", x.g)
                PEA.after(dve, "cs", x.g - 1)
                DVEA.done("dA", dve.tensor_tensor(dA[:], dt[:, x.q], rep(a_rep[:], T, NH), ALU.mult))

            def cs_(dve, x):
                PEA.after(dve, "cs", x.g)
                ACTA.after(dve, "e3", x.g - 1)
                DVEA.done("cs", dve.tensor_copy(e3in[:, 0:3:2], pa[0][:, 0:2 * T * NH].rearrange("p (a t h) -> p a t h", a=2, t=T)))
                DVEA.after(dve, "cs", x.g)
                DVEA.done("dcs", dve.tensor_tensor(e3in[:, 1], e3in[:, 2], e3in[:, 0], ALU.subtract))
                ACTB.after(dve, f"L{NH - 1}", T * (x.g - 2) + T - 1)
                DVEA.done("ncs", dve.tensor_scalar(ncs[:, x.q], e3in[:, 0], -1.0, None, ALU.mult))
                PEA.after(dve, "csT", x.g - 1)
                DVEA.done("p0", dve.tensor_copy(parts[:, :, 0], e3in[:, 0]))

            def parts_(dve, x):
                DVEA.after(dve, "p0", x.g)
                DVEA.done("r1", dve.tensor_tensor(r1[:], e3in[:, 0], parts[:, :, 0], ALU.subtract))
                DVEA.after(dve, "r1", x.g)
                DVEA.done("p1", dve.tensor_copy(parts[:, :, 1], r1[:]))
                DVEA.after(dve, "p1", x.g)
                DVEA.done("p2", dve.tensor_tensor(parts[:, :, 2], r1[:], parts[:, :, 1], ALU.subtract))

            def sres_(dve, x):
                if x.q == 0 and x.t == 0:
                    DVEB.after(dve, "S", x.n - 1)
                    PEB.after(dve, "yoff", x.n - 2 * T)
                    POOLB.after(dve, "scd", x.n - 2 * T)
                    DVES.done("sres", dve.tensor_copy(sres[:].rearrange("p (a n) -> p a n", a=1),
                                                      zero_or_s[:, bass.ds(x.p % (GPB // 2), 1)]))

            def M_(dve, x):
                ACTB.after(dve, f"L{NH - 1}", x.n)
                PEB.after(dve, "ydiag", x.n - 1)
                ACTB.after(dve, "bt", x.n)
                DVEB.done("M", dve.tensor_tensor(mm[:], lm[:], rep(gbt[:, 0], NH, P), ALU.mult))

            def y1_(dve, x):
                PEB.after(dve, "yoff", x.n)
                ACTA.after(dve, "e3", x.g)
                PEC.after(dve, "yT", x.n - 2)
                ACTB.after(dve, "sq", x.n - 2)
                DVEB.done("y1", dve.tensor_tensor(y4[:, x.t % 2], px[:], spread(e3[:, x.q, 0, x.t], NH, HD), ALU.mult))

            def y3_(dve, x):
                PEB.after(dve, "ydiag", x.n)
                POOLB.after(dve, "y2", x.n)
                DVEB.done("y3", dve.tensor_tensor(y4[:, x.t % 2], py[:], y4[:, x.t % 2], ALU.add))

            def y4_(dve, x):
                DVEB.after(dve, "y3", x.n)
                DVEA.after(dve, "gz3b", x.g)
                DVEB.done("y4", dve.tensor_tensor(y4[:, x.t % 2], y4[:, x.t % 2], gz[:, x.q, x.t], ALU.mult))

            def S_(dve, x):
                PEB.after(dve, "state", x.n)
                POOLB.after(dve, "scd", x.n)
                DVEB.done("S", dve.tensor_tensor(state_of(x), state_of(x), px[:], ALU.add))

            def o1_(dve, x):
                PEC.after(dve, "wout", x.n)
                POOLC.after(dve, "rs", x.n)
                POOLE.after(dve, "out", x.n - 2)
                DVEC.done("o1", dve.scalar_tensor_tensor(out=x2[:, x.t % 2], in0=pe_[0][:, 0:DM], scalar=rs[:],
                                                         in1=gate_of(x.batch, 0), op0=ALU.mult, op1=ALU.mult))

            def st_(dve, x):
                POOLC.after(dve, "x2", x.n)
                DVEC.done("st", dve.bn_stats(st2[:], x2[:, x.t % 2]))

            def mv_(dve, x):
                ACTC.after(dve, "h1", x.n - 1)
                POOLC.after(dve, "ve", x.n - 1)
                DVEC.after(dve, "st", x.n)
                DVEC.done("par", dve.tensor_scalar(par2[:].rearrange("p a k -> p (a k)"), mods_of(x.batch, 2), 1.0, None, ALU.mult))
                DVEC.done("mv", dve.bn_aggr(mv2[:], st2[:]))

            def xn_(dve, x):
                POOLC.after(dve, "rstd", x.n)
                PEC.after(dve, "h2T", x.n - 1)
                DVEC.done("xn", dve.tensor_scalar(xn2[:], x2[:, x.t % 2], mv2[:, 0:1], rstd2[:], ALU.subtract, ALU.mult))

            def hi_(dve, x):
                ACTC.after(dve, "h1", x.n)
                PEE.after(dve, "e4", x.n - 2)
                DVEC.done("hi", dve.tensor_copy(h2_hi[:, x.t % 2], h2f[:]))

            E = DVEE.done

            def soft1(dve, x):
                PEE.after(dve, "e0", x.n)
                ACTE.after(dve, "exp", x.n - 1)
                E("lg", dve.tensor_tensor(lg[:], pe_[1][:, 0:NE], gb_rep[:], ALU.add))
                DVEE.after(dve, "lg", x.n)
                E("max", dve.tensor_reduce(nmax[:], lg[:], AX.X, ALU.max, negate=True))

            def chain(*ops):
                def step(dve, x):
                    before = None
                    for name, op in ops:
                        if before:
                            DVEE.after(dve, before, x.n)
                        E(name, op(dve, x))
                        before = name
                return step

            def rsum(dve, x):
                ACTE.after(dve, "exp", x.n)
                return dve.tensor_reduce(sums_[:, 0:1], pexp[:], AX.X, ALU.add)

            def acc0(dve, x):
                POOLE.after(dve, "all", x.n - 1)
                return dve.tensor_scalar(eacc[:, 0], pe_[1][:, NE:NE + DM], wg[:, 0:1], None, ALU.mult)

            def wg_(dve, x):
                PEE.after(dve, "wT", x.n - 1)
                ACTE.after(dve, "ex6", x.n - 1)
                return dve.tensor_scalar(wg[:], wsel[:], sums_[:, 3:4], None, ALU.mult)

            soft2 = chain(
                ("rsum", rsum),
                ("rp", lambda dve, x: dve.reciprocal(sums_[:, 1:2], sums_[:, 0:1])),
                ("pr", lambda dve, x: dve.tensor_scalar(pr[:], pexp[:], sums_[:, 1:2], None, ALU.mult)),
                ("wsel", lambda dve, x: dve.scalar_tensor_tensor(out=wsel[:], in0=pr[:], scalar=THRESHOLD, in1=pr[:],
                                                                 op0=ALU.is_ge, op1=ALU.mult)))

            soft3 = chain(
                ("rw", lambda dve, x: dve.tensor_reduce(sums_[:, 2:3], wsel[:], AX.X, ALU.add)),
                ("rz", lambda dve, x: dve.scalar_tensor_tensor(out=sums_[:, 2:3], in0=sums_[:, 2:3], scalar=0.0,
                                                               in1=sums_[:, 2:3], op0=ALU.is_equal, op1=ALU.add)),
                ("rr", lambda dve, x: dve.reciprocal(sums_[:, 3:4], sums_[:, 2:3])),
                ("wg", wg_),
                ("acc0", acc0))

            def soft3_(dve, x):
                DVEE.after(dve, "wsel", x.n)
                soft3(dve, x)

            def add_expert(e, src, before):
                def step(dve, x):
                    PEE.after(dve, "e1" if e < 3 else "e4", x.n)
                    DVEE.after(dve, before, x.n)
                    return dve.scalar_tensor_tensor(out=eacc[:, e % 2], in0=src, scalar=wg[:, e:e + 1],
                                                    in1=eacc[:, (e + 1) % 2], op0=ALU.mult, op1=ALU.add)
                return step

            def acc12(dve, x):
                E("acc1", add_expert(1, pe_[1][:, 0:DM], "acc0")(dve, x))
                E("acc2", add_expert(2, pe_[1][:, DM:2 * DM], "acc1")(dve, x))

            def acc7(dve, x):
                E("acc7", add_expert(7, pe_[0][:, 0:DM], "acc2")(dve, x))

            def bias_(dve, x):
                DVEE.after(dve, "acc7", x.n)
                E("bias", dve.tensor_tensor(eacc[:, 0], pe_[0][:, DM:2 * DM], eacc[:, 1], ALU.add))

            run(dve, DVE_ORDER,
                {"n_st": n_st, "n_xn": n_xn, "n_hi": n_hi, "sres": sres_, "M": M_, "y1": y1_, "y3": y3_, "y4": y4_,
                 "S": S_, "o1": o1_, "st": st_, "mv": mv_, "xn": xn_, "hi": hi_, "soft1": soft1, "soft2": soft2,
                 "soft3": soft3_, "acc12": acc12, "acc7": acc7, "bias": bias_,
                 "nabs": nabs_, "w1": w1_, "dt": dt_, "cs": cs_, "parts": parts_}
                | {f"gz{i}": z(i) for i in range(T)} | {f"t{f}{'abc'[j]}": tap(f, j) for f in FTS for j in range(H)}
                | {f"silu{f}": silu(f) for f in FTS})

        @block.tensor
        def _(pe):
            def mm_(o, l, r, start, stop):
                return pe.matmul(o, lhsT=l, rhs=r, start=start, stop=stop, skip_group_check=True)

            def split(o, ahi, alo, bhi, blo, cols):
                for k in range(KT):
                    for i, (l, r) in enumerate(((ahi(k), bhi), (ahi(k), blo), (alo(k), bhi))):
                        last = mm_(o, l, r[:, k, cols], k == 0 and i == 0, k == KT - 1 and i == 2)
                return last

            pe.wait_ge(s_ld, LOADED)
            POOL0.after(pe, "hist", 0)
            DVE0.after(pe, "scT", 0)
            for j, m in enumerate((2, 5)):
                for k in range(KT):
                    last = mm_(pe_[0][0:NB, j * DM:(j + 1) * DM], scT[:, k], stage_m[:, k, m * DM:(m + 1) * DM], k == 0, k == KT - 1)
            PE0.done("grow", last)
            for j, m in enumerate((0, 1, 3, 4)):
                for c in range(KT):
                    o = (j * KT + c) * NB
                    for k in range(KT):
                        last = mm_(pd[0][:, o:o + NB], stage_m[:, k, m * DM + c * P:m * DM + (c + 1) * P], scT[:, k], k == 0, k == KT - 1)
            PE0.done("mod", last)
            DVE0.after(pe, "grow", 0)
            for b in range(NB):
                if b >= 2:
                    ACT0.after(pe, f"g{b - 2}", 0)
                PE0.done(f"g{b}", mm_(pe_[b % 2][:], ident[0:NB, b:b + 1].to_broadcast([NB, P]), grow, True, True))
            DVE0.after(pe, "elo", 0)

            def hT_(pe, x):
                DVEN.after(pe, "xn", x.n)
                ACTN.after(pe, "h1", x.n - 1)
                stage, name = ((DVEA, "dtb1"), (DVEA, "dtb3"), (ACTA, "csT"), (ACTA, "acc2"))[x.t]
                stage.after(pe, name, x.g - 1)
                for k in range(KT):
                    last = pe.transpose(pa[HT_BANK[x.t]][:, k * P:(k + 1) * P], xin[:, x.t, k * P:(k + 1) * P], ident[:])
                PEN.done("hT", last)

            def z(i):
                def piece(pe, x):
                    if i == 0:
                        for t in range(T):
                            DVEN.after(pe, "hi", T * x.g + t)
                        POOLN.after(pe, "lo", T * x.g + T - 1)
                        ACTN.after(pe, "h1", T * (x.g + 1) - 1)
                        ACTA.after(pe, "acc3", x.g - 1)
                    else:
                        DVEA.after(pe, f"dtb{i - 1}", x.g)
                    if i == 2:
                        ACTA.after(pe, "acc5", x.g)
                        ACTN.after(pe, "h1", T * (x.g + 1))
                    tok = slice(i * P, (i + 1) * P)
                    split(pa[0][:, 0:ZD], lambda k: h_hi[:, x.q, k, tok], lambda k: h_lo[:, x.q, k, tok], w_hi, w_lo, slice(0, ZD))
                    PEA.done(f"z{i}", split(pa[1][:, 0:ZH], lambda k: h_hi[:, x.q, k, tok], lambda k: h_lo[:, x.q, k, tok],
                                            w_hi, w_lo, slice(ZD, CX)))
                return piece

            def ft(f):
                stage, name = {5: (DVEA, "dtb1"), 4: (DVEA, "dtb3"), 0: (ACTN, 1), 1: (DVEA, "cs"), 2: (ACTA, "acc1"),
                               3: (ACTN, 2)}[f]

                def piece(pe, x):
                    if stage is ACTN:
                        stage.after(pe, "h1", T * (x.g + 1) + name)
                    else:
                        stage.after(pe, name, x.g)
                    cols = slice(CX + f * P, CX + (f + 1) * P)
                    for k in range(KT):
                        for i, (l, r) in enumerate(((w_hi, h_hi), (w_hi, h_lo), (w_lo, h_hi))):
                            last = mm_(pa[BANK[f"ft{f}"]][:], l[:, k, cols], r[:, x.q, k], k == 0 and i == 0, k == KT - 1 and i == 2)
                    PEA.done(f"ft{f}", last)
                return piece

            def cs(pe, x):
                ACTA.after(pe, "acc4", x.g)
                DVEA.after(pe, "dA", x.g)
                flat = dA[:].rearrange("p t h -> p (t h)")
                mm_(pa[0][:, 0:T * NH], tri[:], flat, True, True)
                PEA.done("cs", mm_(pa[0][:, T * NH:2 * T * NH], all_ones, flat, True, True))

            def csT_(pe, x):
                ACTA.after(pe, "acc0", x.g)
                DVEA.after(pe, "p2", x.g)
                for t in range(T):
                    last = pe.transpose(pa1_bf[0:3 * NH, t * P:(t + 1) * P], parts[:, t].rearrange("p a h -> p (a h)"), identb[:])
                PEA.done("csT", last)

            def D_(pe, x):
                ACTA.after(pe, "csT", x.g)
                ACTB.after(pe, f"L{NH - 1}", x.n - 1)
                for b in range(2):
                    mm_(pd[b][:], identb[:], rep(negmask[:], 4, P), True, False)
                    for h in range(4):
                        last = mm_(pd[b][:, h * P:(h + 1) * P], sel[:, 4 * b + h], csT[:, x.q, x.t], False, h == 3)
                PEB.done("D", last)

            def G_(pe, x):
                DVEA.after(pe, "silu5", x.g)
                DVEA.after(pe, "silu4", x.g)
                DVEB.after(pe, "y3", x.n - 1)
                mm_(py[:, 0:P], feat[:, x.q, XT, x.tok], feat[:, x.q, XT + 1, x.tok], True, True)
                PEB.done("G", pe.transpose(py[:, P:2 * P], feat[:, x.q, XT, x.tok], ident[:]))

            def xT_(pe, x):
                DVEA.after(pe, "silu3", x.g)
                DVEB.after(pe, "S", x.n - 1)
                for f in range(XT):
                    last = pe.transpose(px[:, f * P:(f + 1) * P], feat[:, x.q, f, x.tok], ident[:])
                PEB.done("xT", last)

            def yoff_(pe, x):
                ACTB.after(pe, "xt", x.n)
                state_ready(pe, x)
                PEB.done("yoff", mm_(px[:], feat[:, x.q, XT + 1, x.tok], state_before(x), True, True))

            def ydiag_(pe, x):
                DVEB.after(pe, "M", x.n)
                POOLB.after(pe, "xdt", x.n)
                ACTB.after(pe, "bt", x.n)
                for h in range(NH):
                    last = mm_(py[:, h * HD:(h + 1) * HD], mm[:, h], xdt[:, h * HD:(h + 1) * HD], True, True)
                PEB.done("ydiag", last)

            def state_(pe, x):
                POOLB.after(pe, "xs", x.n)
                DVEB.after(pe, "y1", x.n)
                PEB.done("state", mm_(px[:], gbt[:, 1], xs[:], True, True))

            def yT_(pe, x):
                DVEB.after(pe, "y4", x.n)
                DVEE.after(pe, "bias", x.n - 2)
                for f in range(XT):
                    last = pe.transpose(pe_[0][:, f * P:(f + 1) * P], y4[:, x.t % 2, f * P:(f + 1) * P], ident[:])
                PEC.done("yT", last)

            def wout_(pe, x):
                ACTC.after(pe, "yT", x.n)
                for k in range(XT):
                    last = mm_(pe_[0][:, 0:DM], yT[:, k], wo[:, k], k == 0, k == XT - 1)
                PEC.done("wout", last)

            def h2T_(pe, x):
                DVEC.after(pe, "xn", x.n)
                DVEE.after(pe, "acc2", x.n - 1)
                for k in range(KT):
                    last = pe.transpose(pe_[1][:, k * P:(k + 1) * P], xn2[:, k * P:(k + 1) * P], ident[:])
                PEC.done("h2T", last)

            def experts(i, free):
                def step(pe, x):
                    a, b = (0, NE + DM) if i == 0 else (NE + DM * (2 * i - 1), min(EC, NE + DM * (2 * i + 1)))
                    bank_ = pe_[(1, 1, 0, 1, 0)[i]]
                    free(x)
                    if i == 3:
                        PEE.done("wT", pe.transpose(pe_[0][0:NE, 0:P], wg[:], ident[:]))
                    last = split(bank_[:, 0:b - a], lambda k: h2_hi[:, x.t % 2, k], lambda k: h2_lo[:, x.t % 2, k],
                                 e_hi, e_lo, slice(a, b))
                    if i == 4:
                        last = mm_(bank_[:, DM:2 * DM], wgT[:], eb[:], True, True)
                    PEE.done(f"e{i}", last)
                return step

            def free0(x):
                DVEC.after(pe, "hi", x.n)
                POOLC.after(pe, "lo", x.n)
                ACTE.after(pe, "ex6", x.n - 1)
                ACTC.after(pe, "h1", x.n)

            def free1(x):
                DVEE.after(pe, "acc0", x.n)

            def free2(x):
                DVEE.after(pe, "bias", x.n - 1)
                DVEC.after(pe, "o1", x.n + 1)

            def free3(x):
                ACTE.after(pe, "ex4", x.n)
                DVEE.after(pe, "acc2", x.n)
                ACTC.after(pe, "h1", x.n + 1)

            def free4(x):
                ACTE.after(pe, "wT", x.n)

            run(pe, PE_ORDER,
                {"hT": hT_, "D": D_, "G": G_, "xT": xT_, "yoff": yoff_, "ydiag": ydiag_, "state": state_, "yT": yT_,
                 "wout": wout_, "h2T": h2T_, "e0": experts(0, free0), "e1": experts(1, free1), "e2": experts(2, free2),
                 "e3": experts(3, free3), "e4": experts(4, free4), "cs": cs, "csT": csT_}
                | {f"z{i}": z(i) for i in range(T)} | {f"ft{f}": ft(f) for f in FTS})

_INS = ['L0_attn_hidden_states', 'L0_attn_W_in', 'L0_attn_conv_w', 'L0_attn_conv_b', 'L0_attn_dt_bias', 'L0_attn_A_log',
        'L0_attn_D', 'L0_attn_norm_w', 'L0_attn_W_out', 'L0_ffn_gate_w', 'L0_ffn_gate_b', 'L0_ffn_expert_w',
        'L0_ffn_expert_b', 'L0_c', 'L0_wmod']


def kernel(**inputs):
    import numpy as _np
    import concourse.bacc as _bacc
    from concourse import mybir as _mybir
    from concourse.bass_utils import run_bass_kernel_spmd as _run

    nc = _bacc.Bacc("TRN2", target_bir_lowering=False, num_devices=1)
    arrays, args = {}, []
    for name in _INS:
        a = _np.ascontiguousarray(inputs[name])
        arrays[f"in_{name}_dram"] = a
        args.append(nc.dram_tensor(f"in_{name}_dram", a.shape, _mybir.dt.from_np(a.dtype), kind="ExternalInput").ap())
    shape = inputs['L0_attn_hidden_states'].shape
    args.append(nc.dram_tensor("out_0_dram", shape, _mybir.dt.float32, kind="ExternalOutput").ap())
    adaln_mamba_moe(nc, *args)
    r = _run(nc, [arrays], core_ids=[0])
    return r.results[0]["out_0_dram"]
```

```python
from contextlib import ExitStack

import numpy as np

import concourse.bass as bass
from concourse import mybir

ALU = mybir.AluOpType
ACT = mybir.ActivationFunctionType
AX = mybir.AxisListType
F32 = mybir.dt.float32
F32R = mybir.dt.float32r
BF16 = mybir.dt.bfloat16

P = 128


class Stage:

    def __init__(self, sem, runs, steps):
        self.sem = sem
        self.runs = runs
        self.n = len(steps)
        self.at = {name: i + 1 for i, name in enumerate(steps)}
        assert len(self.at) == self.n
        self.said = 0

    def done(self, name, instruction):
        assert self.at[name] == self.said % self.n + 1, (name, self.said)
        self.said += 1
        return instruction.then_inc(self.sem, 1)

    def after(self, eng, name, run):
        if not isinstance(run, int) or 0 <= run < self.runs:
            eng.wait_ge(self.sem, run * self.n + self.at[name])


def adaln_mamba_moe(nc, x_in, w_in, conv_w, conv_b, dt_bias, a_log, d_skip, norm_w, w_out,
                    gate_w, gate_b, exp_w, exp_b, c_in, w_mod, out):
    NB, L, DM = x_in.shape
    DI = w_out.shape[0]
    NH = a_log.shape[0]
    HD = DI // NH
    CD = conv_w.shape[0]
    TAPS = conv_w.shape[1]
    NS = (CD - DI) // 2
    NE = gate_w.shape[1]
    KT = DM // P
    FT = CD // P
    XT = DI // P
    T = 4
    GT = T * P
    NG = NB * L // GT
    NTILE = NG * T
    GPB = L // GT
    H = TAPS - 1
    EPS = 1e-5
    THRESHOLD = 0.1
    assert NS == P and DI == 512 and DM == 256 and GPB == 4 and NG % 2 == 0 and FT == 6
    ZH = DI // 2
    ZD = ZH + NH
    CX = DI + NH
    WC = CX + CD
    EC = NE + NE * DM

    x_tok = x_in.rearrange("b l d -> (b l) d")
    out_tok = out.rearrange("b l d -> (b l) d")

    with ExitStack() as ctx:
        def sb(name, shape, dt=F32):
            return ctx.enter_context(nc.sbuf_tensor(name, shape, dt))

        def bank(name):
            return ctx.enter_context(nc.psum_tensor(name, [P, 512], F32))

        def sem(name):
            return ctx.enter_context(nc.semaphore(name))

        pa = [bank("pa0"), bank("pa1")]
        pd = [bank("pd0"), bank("pd1")]
        px = bank("px")
        py = bank("py")
        pe_ = [bank("pe0"), bank("pe1")]

        ident = sb("ident", [P, P])
        identb = sb("identb", [P, P], BF16)
        tri = sb("tri", [P, P])
        sel = sb("sel", [3 * NH, NH, P], BF16)
        neghalf = sb("neghalf", [P, T])
        eps = sb("eps", [P, T])
        w_hi = sb("w_hi", [P, KT, WC], F32R)
        w_lo = sb("w_lo", [P, KT, WC], F32R)
        e_hi = sb("e_hi", [P, KT, EC], F32R)
        e_lo = sb("e_lo", [P, KT, EC], F32R)
        wo_hi = sb("wo_hi", [P, XT, DM], F32R)
        wo_lo = sb("wo_lo", [P, XT, DM], F32R)
        eb3 = sb("eb3", [3 * NE, DM], F32R)
        is_lo = sb("is_lo", [3 * NE, 2])
        gb_rep = sb("gb_rep", [P, NE])
        cw = sb("cw", [P, FT, TAPS])
        cb = sb("cb", [P, FT])
        nw = sb("nw", [P, XT])
        a_rep = sb("a_rep", [P, NH])
        dtb_rep = sb("dtb_rep", [P, NH])
        d_rep = sb("d_rep", [P, NH])
        cT = sb("cT", [P, KT, NB])
        hc = sb("hc", [P, KT, NB])
        scT = sb("scT", [P, KT, NB])
        expa = sb("expa", [P, NH])
        modT = sb("modT", [P, NB, 4, KT])
        par1 = sb("par1", [P, 2, KT])
        par2 = sb("par2", [P, 2, KT])
        gates = sb("gates", [P, NB, 2, DM])

        xin = sb("xin", [P, T, DM])
        xres = sb("xres", [P, 2, DM])
        st1 = sb("st1", [P, 6])
        mv1 = sb("mv1", [P, 2])
        ve1 = sb("ve1", [P, 1])
        rstd1 = sb("rstd1", [P, 1])
        hf = sb("hf", [P, 2, KT, P])
        h_hi = sb("h_hi", [P, 2, KT, GT], F32R)
        h_lo = sb("h_lo", [P, 2, KT, GT], F32R)
        raw = sb("raw", [P, 2, H + GT])
        hist = sb("hist", [P, 2, FT, H])
        acc = sb("acc", [P, 2, GT])
        feat = sb("feat", [P, 2, FT, GT])
        gz = sb("gz", [P, 2, T, DI])
        v = sb("v", [P, T, NH])
        nabs = sb("nabs", [P, T, NH])
        u = sb("u", [P, T, NH])
        w1 = sb("w1", [P, T, NH])
        lnw = sb("lnw", [P, T, NH])
        nc1 = sb("nc1", [P, T, NH])
        sp1 = sb("sp1", [P, T, NH])
        dt = sb("dt", [P, 2, T, NH])
        dA = sb("dA", [P, T, NH])
        e3in = sb("e3in", [P, 3, T, NH])
        e3 = sb("e3", [P, 2, 3, T, NH])
        csc = sb("csc", [P, 2, T, NH])
        r1 = sb("r1", [P, T, NH])
        parts = sb("parts", [P, T, 3, NH], BF16)
        csT = sb("csT", [3 * NH, 2, T, P], BF16)

        gs = sb("gs", [P, P])
        bt = sb("bt", [P, P])
        xt = sb("xt", [P, DI])
        xdt = sb("xdt", [P, DI])
        xs = sb("xs", [P, DI])
        lm = sb("lm", [P, NH, P])
        mm = sb("mm", [P, NH, P])
        gsgn, gabs = lm[0:NB, 0:NH // 2].rearrange("p a n -> p (a n)"), lm[0:NB, NH // 2:].rearrange("p a n -> p (a n)")
        grow = mm[0:NB, 0:NH // 2].rearrange("p a n -> p (a n)")
        zero_or_s = sb("zero_or_s", [P, 2, DI])
        s_even = sb("s_even", [P, DI])
        sres = sb("sres", [P, DI])
        y4 = sb("y4", [P, 2, DI])
        ysq = sb("ysq", [P, DI], BF16)
        ssq = sb("ssq", [P, 2])
        ms = sb("ms", [P, 1])
        rs = sb("rs", [P, 1])
        yT_hi = sb("yT_hi", [P, XT, P], F32R)
        yT_lo = sb("yT_lo", [P, XT, P], F32R)
        x2 = sb("x2", [P, 2, DM])
        st2 = sb("st2", [P, 6])
        mv2 = sb("mv2", [P, 2])
        ve2 = sb("ve2", [P, 1])
        rstd2 = sb("rstd2", [P, 1])
        xn2 = sb("xn2", [P, DM])
        h2f = sb("h2f", [P, KT, P])
        h2_hi = sb("h2_hi", [P, 2, KT, P], F32R)
        h2_lo = sb("h2_lo", [P, 2, KT, P], F32R)
        lgt = sb("lgt", [P, NE])
        nmax = sb("nmax", [P, 1])
        pexp = sb("pexp", [P, NE])
        sums_ = sb("sums_", [P, 4])
        pr = sb("pr", [P, NE])
        wsel = sb("wsel", [P, NE])
        wg = sb("wg", [P, NE])
        wg3 = sb("wg3", [P, 3, NE], F32R)
        wgT = sb("wgT", [3 * NE, P], F32R)
        eacc = sb("eacc", [P, 2, DM])
        ex = sb("ex", [P, 4, DM])
        outb = sb("outb", [P, 2, DM])

        s_small = sem("s_small")
        s_proj = sem("s_proj")
        s_exp = sem("s_exp")
        s_xin = [sem(f"s_xin{t}") for t in range(T)]
        s_xres = [sem(f"s_xres{t}") for t in range(2)]
        s_out = [sem("s_out0"), sem("s_out1")]

        POOL0 = Stage(sem("pool_0"), 1, ["z_ident", "ident", "identb", "o_tri", "tri",
                                         "z_sel", "sel0", "sel1", "sel2", "neghalf", "eps", "szero", "hist",
                                         "o_lo", "ge_lo", "is_lo", "is_hi"])
        ACT0 = Stage(sem("act_0"), 1, ["thc", "expa"] + [f"g{b}" for b in range(NB)])
        PE0 = Stage(sem("pe_0"), 1, ["grow", "mod"] + [f"g{b}" for b in range(NB)])
        DVE0 = Stage(sem("dve_0"), 1,
                     ["hc", "scT", "sgn", "abs", "max", "grow"] + [f"m{j}{k}" for j in range(4) for k in range(KT)]
                     + ["cw", "cb", "a_rep"] + [f"w{i}{x}" for i in range(4) for x in ("hi", "lo")]
                     + [f"wo{k}{x}" for k in range(XT) for x in ("hi", "lo")] + ["ghi", "ehi", "glo", "elo", "bhi", "blo", "blo0", "eb3"])
        PEN = Stage(sem("pe_n"), NTILE, ["hT"])
        ACTN = Stage(sem("act_n"), NTILE, ["h0", "h1"])
        DVEN = Stage(sem("dve_n"), NTILE, ["st", "par", "mv", "xn", "hi"])
        POOLN = Stage(sem("pool_n"), NTILE, ["ve", "rstd", "lo"])
        PEA = Stage(sem("pe_a"), NG, ["z0", "z1", "ft5", "z2", "z3", "ft4", "cs", "ft0", "ft1", "csT", "ft2", "ft3"])
        ACTA = Stage(sem("act_a"), NG,
                     ["tz0a", "tz0b", "tz1a", "tz1b", "raw5", "halo5", "acc5", "hist5", "th5"]
                     + ["tz2a", "tz2b", "tz3a", "tz3b", "u", "ln", "raw4", "halo4", "acc4", "hist4", "th4"]
                     + ["raw0", "halo0", "acc0", "hist0", "e3", "raw1", "halo1", "acc1", "hist1", "csT", "th0", "th1"]
                     + ["raw2", "halo2", "acc2", "hist2", "raw3", "halo3", "acc3", "hist3", "th2", "th3"])

        def conv_steps(f):
            return [f"tap{f}a", f"tap{f}b", f"tap{f}c"]
        DVEA = Stage(sem("dve_a"), NG,
                     ["gz0a", "gz0b", "dtb0", "gz1a", "gz1b", "dtb1"] + conv_steps(5) + ["silu5"]
                     + ["gz2a", "gz2b", "dtb2", "gz3a", "gz3b", "dtb3", "nabs", "w1", "nc1", "sp1", "dt", "dA"]
                     + conv_steps(4) + ["silu4"]
                     + ["cs", "dcs", "csc", "p0", "r1", "p1", "p2"]
                     + conv_steps(0) + ["silu0"] + conv_steps(1) + ["silu1"]
                     + conv_steps(2) + ["silu2"] + conv_steps(3) + ["silu3"])
        PEB = Stage(sem("pe_b"), NTILE, ["D", "G", "xT", "yoff", "ydiag", "state"])
        ACTB = Stage(sem("act_b"), NTILE, ["bt"] + [f"L{h}" for h in range(4)] + ["xt"] + [f"L{h}" for h in range(4, NH)] + ["L", "sq"])
        DVEB = Stage(sem("dve_b"), NTILE, ["gs", "M", "y1", "y3", "y4", "S"])
        DVES = Stage(sem("dve_s"), NG // 2, ["sres"])
        POOLB = Stage(sem("pool_b"), NTILE, ["xdt", "xs", "scd", "xd", "y2"])
        PEC = Stage(sem("pe_c1"), NTILE, ["yT", "wout", "h2T"])
        ACTC = Stage(sem("act_c1"), NTILE, ["yT", "h0", "h1"])
        DVEC = Stage(sem("dve_c1"), NTILE, ["yTlo", "o1", "st", "par", "mv", "xn", "hi"])
        POOLC = Stage(sem("pool_c1"), NTILE, ["ms", "rs", "x2", "ve", "rstd", "lo"])
        PEE = Stage(sem("pe_e"), NTILE, ["e0", "e1", "e2", "wT", "e3", "e4"])
        ACTE = Stage(sem("act_e"), NTILE, ["exp", "ex0", "ex3", "ex4", "wT", "ex5", "ex6"])
        DVEE = Stage(sem("dve_e"), NTILE, ["lg", "max", "rp", "pr", "wsel", "rw", "rz", "rr", "wg", "wghi", "wglo",
                                           "acc1", "acc2", "acc7", "bias"])
        POOLE = Stage(sem("pool_e"), NTILE, ["a34", "a56", "a3456", "all", "og", "out"])

        pa1_bf = pa[1][:].bitcast(BF16)

        feat_flat = feat[:].rearrange("p a f n -> p (a f n)")
        stage_w = feat_flat[:, 0:KT * WC].rearrange("p (k n) -> p k n", k=KT)
        stage_m = feat_flat[:, KT * WC:KT * (WC + 6 * DM)].rearrange("p (k n) -> p k n", k=KT)
        stage_e = gz[:].rearrange("p a t n -> p (a t n)").rearrange("p (k n) -> p k n", k=KT)
        stage_wo = y4[:].rearrange("p a n -> p (a n)").rearrange("p (k n) -> p k n", k=XT)
        stage_b, b_lo, b_hi = (x[0:3 * NE, 0:DM] for x in (xs, xdt, xt))
        stage_g = xres[:, 0, 0:KT * NE].rearrange("p (k n) -> p k n", k=KT)

        all_ones = tri[:, P - 1:P].to_broadcast([P, P])

        def rep(ap, n, w):
            return ap[:, None, :].to_broadcast([P, n, w])

        def spread(ap, n, w):
            return ap[:, :, None].to_broadcast([P, n, w])

        class Tile:
            def __init__(self, p, m, back):
                m -= back
                self.p, m = p + m // (2 * T), m % (2 * T)
                self.q, self.t = m // T, m % T
                self.g = 2 * self.p + self.q
                self.n = 2 * T * self.p + m
                self.batch = self.p // (GPB // 2)
                self.exists = not isinstance(p, int) or 0 <= self.p < NG // 2
                self.tok = slice(self.t * P, (self.t + 1) * P)

        def run(eng, order, steps, end=NG // 2 - 1):
            def pair(p, ms):
                for m in ms:
                    for name, back in order[m % T]:
                        x = Tile(p, m, back)
                        if x.exists:
                            steps[name](eng, x)
            pair(-1, range(2 * T))
            pair(0, range(2 * T))
            with eng.Fori(1, end) as p:
                pair(p, range(2 * T))
            for p in range(end, NG // 2):
                pair(p, range(2 * T))
            pair(NG // 2, range(T))

        def state_of(x):
            return zero_or_s[:, 1] if x.t % 2 else s_even[:]

        def state_before(x):
            if x.q == 0 and x.t == 0:
                return sres[:]
            return s_even[:] if x.t % 2 else zero_or_s[:, 1]

        def state_ready(eng, x):
            if x.q == 0 and x.t == 0:
                DVES.after(eng, "sres", x.p)
            else:
                DVEB.after(eng, "S", x.n - 1)

        def mods_of(b, kind):
            return modT[:, bass.ds(b, 1), kind:kind + 2].rearrange("p b a k -> p (b a k)")

        def gate_of(b, i):
            return gates[:, bass.ds(b, 1), i].rearrange("p a n -> p (a n)")

        BANK = {"ft5": 0, "ft4": 0, "cs": 0, "ft0": 1, "ft1": 0, "csT": 1, "ft2": 0, "ft3": 1}
        HT_BANK = [1, 1, 1, 0]
        FTS = [5, 4, 0, 1, 2, 3]

        def turn(f):
            return FTS.index(f) % 2

        def two_back(eng, stage, step, f, g):
            i = FTS.index(f)
            stage.after(eng, f"{step}{FTS[(i - 2) % FT]}", g if i >= 2 else g - 1)

        POOL_ORDER = [
            [("a56", 4), ("a3456", 4), ("xdt", 1), ("all", 4), ("xs", 1), ("scd", 1), ("og", 4), ("rs", 2), ("out", 4),
             ("xd", 1), ("x2", 2), ("n_lo", -7), ("y2", 1), ("ve", 2), ("rstd", 2), ("n_ve", -8), ("a34", 3), ("lo", 2),
             ("n_rstd", -8), ("ms", 1), ("rs", 1), ("a56", 3), ("a3456", 3), ("all", 3), ("xdt", 0), ("xs", 0), ("scd", 0),
             ("og", 3), ("out", 3), ("xd", 0), ("x2", 1), ("ve", 1), ("rstd", 1), ("y2", 0), ("a34", 2), ("n_lo", -8),
             ("lo", 1)],
            [("n_ve", -8), ("n_rstd", -8), ("ms", 1), ("rs", 1), ("a56", 3), ("a3456", 3), ("xdt", 0), ("all", 3), ("xs", 0),
             ("scd", 0), ("og", 3), ("out", 3), ("xd", 0), ("x2", 1), ("y2", 0), ("ve", 1), ("rstd", 1), ("n_lo", -8)],
            [("n_ve", -8), ("a34", 3), ("n_rstd", -8), ("lo", 2), ("ms", 1)],
            [("rs", 2), ("a56", 4), ("a3456", 4), ("xdt", 1), ("all", 4), ("xs", 1), ("scd", 1), ("og", 4), ("out", 4),
             ("xd", 1), ("x2", 2), ("y2", 1), ("ve", 2), ("rstd", 2), ("a34", 3), ("lo", 2), ("n_lo", -7), ("n_ve", -8),
             ("ms", 1), ("n_rstd", -8)]]
        PE_ORDER = [
            [("z0", -4), ("h2T", 2), ("D", 0), ("G", 0), ("e3", 3), ("e4", 3), ("xT", 0), ("e0", 2), ("yT", 1), ("z1", -4),
             ("yoff", 0), ("wout", 1), ("hT", -8), ("ft5", -4), ("e1", 2), ("ydiag", 0), ("e2", 2), ("z2", -4), ("h2T", 1),
             ("state", 0)],
            [("D", 0), ("e3", 3), ("G", 0), ("e4", 3), ("xT", 0), ("e0", 2), ("yT", 1), ("z3", -4), ("yoff", 0), ("wout", 1),
             ("hT", -8), ("e1", 2), ("ydiag", 0), ("ft4", -4), ("e2", 2), ("state", 0), ("h2T", 1), ("cs", -4)],
            [("D", 0), ("G", 0), ("e3", 3), ("xT", 0), ("e4", 3), ("e0", 2), ("yoff", 0), ("yT", 1), ("ft0", -4),
             ("ft1", -4), ("wout", 1), ("csT", -4), ("e1", 2), ("e2", 2), ("ydiag", 0), ("state", 0), ("h2T", 1)],
            [("D", 0), ("hT", -7), ("G", 0), ("e3", 3), ("e4", 3), ("xT", 0), ("e0", 2), ("ft2", -4), ("yT", 1), ("yoff", 0),
             ("ft3", -4), ("hT", -8), ("wout", 1), ("e1", 2), ("ydiag", 0), ("state", 0), ("e2", 2)]]
        ACT_ORDER = [
            [("exp", 2), ("yT", 1), ("L47", 0), ("tz1", -4), ("L", 0), ("ex0", 2), ("n_h", -8), ("raw5", -4), ("ex34", 2),
             ("h2", 1), ("th5", -4), ("tz2", -4), ("wT", 2), ("sq", 0), ("ex56", 2), ("bt", -1)],
            [("L03", 0), ("xt", 0), ("exp", 2), ("yT", 1), ("L47", 0), ("tz3", -4), ("L", 0), ("ex0", 2), ("n_h", -8),
             ("u", -4), ("ln", -4), ("raw4", -4), ("ex34", 2), ("h2", 1), ("sq", 0), ("bt", -1)],
            [("L03", 0), ("wT", 3), ("ex56", 3), ("xt", 0), ("th4", -4), ("exp", 2), ("yT", 1), ("L47", 0), ("L", 0),
             ("raw0", -4), ("ex0", 2), ("decays", -4), ("raw1", -4), ("csT", -4), ("th0", -4), ("ex34", 2), ("h2", 1),
             ("n_h", -8), ("sq", 0), ("bt", -1), ("wT", 2), ("ex56", 2)],
            [("L03", 0), ("xt", 0), ("L47", 0), ("exp", 2), ("th1", -4), ("yT", 1), ("raw2", -4), ("L", 0), ("ex0", 2),
             ("n_h", -8), ("raw3", -4), ("th2", -4), ("ex34", 2), ("h2", 1), ("sq", 0), ("wT", 2), ("bt", -1), ("th3", -4),
             ("ex56", 2), ("tz0", -8), ("L03", -1), ("xt", -1)]]
        DVE_ORDER = [
            [("t0b", 0), ("n_xn", -6), ("st", 3), ("wglo", 4), ("mv", 3), ("t0c", 0), ("acc1", 4), ("acc2", 4), ("xn", 3),
             ("y3", 2), ("silu0", 0), ("y4", 2), ("hi", 3), ("S", 2), ("n_hi", -6), ("n_st", -7), ("n_mv", -7), ("t1a", 0),
             ("t1b", 0), ("acc7", 4), ("bias", 4), ("lg", 3), ("max", 3), ("t1c", 0), ("n_xn", -7), ("rp", 3), ("pr", 3),
             ("gs", 1), ("wsel", 3), ("rw", 3), ("rz", 3), ("yTlo", 2), ("rr", 3), ("silu1", 0), ("wg", 3), ("t2a", 0),
             ("wghi", 3), ("t2b", 0), ("M", 1), ("wglo", 3), ("o1", 2), ("n_hi", -7), ("acc1", 3), ("y1", 1), ("t2c", 0),
             ("st", 2), ("n_st", -8), ("mv", 2), ("acc2", 3), ("n_mv", -8), ("silu2", 0), ("y3", 1), ("xn", 2), ("t3a", 0),
             ("y4", 1), ("t3b", 0), ("hi", 2), ("t3c", 0), ("S", 1), ("silu3", 0), ("acc7", 3), ("bias", 3), ("gz0", -4),
             ("lg", 2), ("max", 2), ("sres", 0), ("n_xn", -8), ("rp", 2), ("yTlo", 1), ("pr", 2), ("wsel", 2), ("rw", 2),
             ("gz1", -4), ("rz", 2), ("rr", 2), ("gs", 0), ("wg", 2), ("M", 0), ("y1", 0), ("wghi", 2), ("o1", 1),
             ("n_hi", -8), ("wglo", 2)],
            [("n_st", -8), ("acc1", 3), ("acc2", 3), ("st", 2), ("n_mv", -8), ("mv", 2), ("t5a", -4), ("t5b", -4), ("xn", 2),
             ("t5c", -4), ("y3", 1), ("hi", 2), ("y4", 1), ("S", 1), ("silu5", -4), ("gz2", -4), ("n_xn", -8), ("acc7", 3),
             ("bias", 3), ("lg", 2), ("max", 2), ("rp", 2), ("pr", 2), ("wsel", 2), ("rw", 2), ("yTlo", 1), ("rz", 2),
             ("gs", 0), ("rr", 2), ("wg", 2), ("wghi", 2), ("gz3", -4), ("wglo", 2), ("M", 0), ("y1", 0), ("nabs", -4),
             ("o1", 1), ("w1", -4), ("n_hi", -8), ("acc1", 2), ("nc1", -4)],
            [],
            [("n_st", -7), ("st", 3), ("mv", 3), ("sp1", -4), ("n_mv", -7), ("dt", -4), ("acc2", 4), ("y3", 2), ("xn", 3),
             ("dA", -4), ("y4", 2), ("S", 2), ("hi", 3), ("t4a", -4), ("t4b", -4), ("t4c", -4), ("gs", 1), ("acc7", 4),
             ("bias", 4), ("lg", 3), ("max", 3), ("rp", 3), ("pr", 3), ("silu4", -4), ("wsel", 3), ("cs", -4), ("rw", 3),
             ("dcs", -4), ("yTlo", 2), ("csc", -4), ("rz", 3), ("rr", 3), ("p0", -4), ("r1", -4), ("wg", 3), ("p1", -4),
             ("wghi", 3), ("p2", -4), ("M", 1), ("t0a", -4), ("o1", 2), ("y1", 1)]]

        block = ctx.enter_context(nc.Block())

        loads = {s_small: [], s_proj: [], s_exp: []}
        wv = w_in.rearrange("(k p) n -> p k n", p=P)
        for k in range(KT):
            loads[s_small].append((cT[:, k], c_in[:, k * P:(k + 1) * P].rearrange("b p -> p b")))
        loads[s_small].append((stage_m, w_mod.rearrange("(k p) n -> p k n", p=P)))
        for dst, src in ((gb_rep, gate_b), (a_rep, a_log), (dtb_rep, dt_bias), (d_rep, d_skip)):
            loads[s_small].append((dst[:], src.rearrange("(o n) -> o n", o=1).to_broadcast([P, src.shape[0]])))
        loads[s_small] += [(cw[:], conv_w.rearrange("(f p) k -> p f k", p=P)),
                           (cb[:], conv_b.rearrange("(f p) -> p f", p=P)),
                           (nw[:], norm_w.rearrange("(f p) -> p f", p=P))]
        loads[s_proj] += [(stage_w[:, :, 0:ZH], wv[:, :, 0:ZH]),
                          (stage_w[:, :, ZH:ZD], wv[:, :, DI + CD:]),
                          (stage_w[:, :, ZD:WC], wv[:, :, ZH:DI + CD]),
                          (stage_wo, w_out.rearrange("(k p) n -> p k n", p=P))]
        loads[s_exp] += [(stage_b[part * NE:(part + 1) * NE], exp_b) for part in range(3)]
        loads[s_exp].append((stage_g, gate_w.rearrange("(k p) n -> p k n", p=P)))
        for k in range(KT):
            loads[s_exp].append((stage_e[:, k].rearrange("p (e n) -> p e n", e=NE),
                                 exp_w[:, k * P:(k + 1) * P, :].rearrange("e p n -> p e n")))

        def loaded(eng, s_part):
            eng.wait_ge(s_part, 16 * len(loads[s_part]))

        @block.sync
        def _(sp):
            def x_of(n):
                return x_tok[bass.ds(n * P, P), :]

            for t in range(T):
                sp.dma_start(xin[:, t], x_of(t)).then_inc(s_xin[t], 16)
            for s_part, pairs in loads.items():
                for dst, src in pairs:
                    with nc.allow_non_contiguous_dma(reason="small vectors, once"):
                        sp.dma_start(dst, src).then_inc(s_part, 16)

            def load_xin(sp, x):
                if x.exists and (not isinstance(x.g, int) or x.g + 1 < NG):
                    PEN.after(sp, "hT", x.n)
                    sp.dma_start(xin[:, x.t], x_of(x.n + T)).then_inc(s_xin[x.t], 16)

            def load_xres(sp, x):
                if isinstance(x.g, int) and x.g == 0:
                    DVE0.after(sp, "glo", 0)
                POOLC.after(sp, "x2", x.n - 2)
                sp.dma_start(xres[:, x.t % 2], x_of(x.n)).then_inc(s_xres[x.t % 2], 16)

            def store(sp, x):
                POOLE.after(sp, "out", x.n)
                sp.dma_start(out_tok[bass.ds(x.n * P, P), :], outb[:, x.t % 2]).then_inc(s_out[x.t % 2], 16)

            run(sp, [[("store", 3), ("xres", 0), ("xin", -2 * T)]] * T, {"xin": load_xin, "xres": load_xres, "store": store},
                end=NG // 2 - 2)
            for o in s_out:
                sp.wait_ge(o, 16 * NTILE // 2)

        @block.gpsimd
        def _(pool):
            D0 = POOL0.done

            def own(name):
                POOL0.after(pool, name, 0)
            D0("z_ident", pool.memset(ident[:], 0.0))
            own("z_ident")
            D0("ident", pool.affine_select(out=ident[:], in_=ident[:], compare_op=ALU.not_equal, fill=1.0,
                                           base=0, pattern=[[-1, P]], channel_multiplier=1))
            own("ident")
            D0("identb", pool.tensor_copy(identb[:], ident[:]))
            D0("o_tri", pool.memset(tri[:], 1.0))
            own("o_tri")
            D0("tri", pool.affine_select(out=tri[:], in_=tri[:], compare_op=ALU.is_ge, fill=0.0,
                                         base=0, pattern=[[1, P]], channel_multiplier=-1))
            D0("z_sel", pool.memset(sel[:], 0.0))
            own("z_sel")
            for part in range(3):
                D0(f"sel{part}", pool.affine_select(out=sel[:], in_=sel[:], compare_op=ALU.not_equal, fill=1.0,
                                                    base=-part * NH, pattern=[[-1, NH], [0, P]], channel_multiplier=1))
                own(f"sel{part}")
            D0("neghalf", pool.memset(neghalf[:], -0.5))
            D0("eps", pool.memset(eps[:], EPS))
            D0("szero", pool.memset(zero_or_s[:], 0.0))
            D0("hist", pool.memset(hist[:], 0.0))
            D0("o_lo", pool.memset(is_lo[:, 0:1], 1.0))
            own("o_lo")
            D0("ge_lo", pool.affine_select(out=is_lo[:, 0:1], in_=is_lo[:, 0:1], compare_op=ALU.is_ge, fill=0.0,
                                           base=-NE, pattern=[[0, 1]], channel_multiplier=1))
            own("ge_lo")
            D0("is_lo", pool.affine_select(out=is_lo[:, 0:1], in_=is_lo[:, 0:1], compare_op=ALU.is_ge, fill=0.0,
                                           base=2 * NE - 1, pattern=[[0, 1]], channel_multiplier=-1))
            own("is_lo")
            D0("is_hi", pool.tensor_scalar(is_lo[:, 1:2], is_lo[:, 0:1], -1.0, 1.0, ALU.mult, ALU.add))
            own("is_hi")

            def n_ve(pool, x):
                DVEN.after(pool, "mv", x.n)
                POOLN.after(pool, "rstd", x.n - 1)
                POOLN.done("ve", pool.tensor_tensor(ve1[:], mv1[:, 1:2], eps[:, 0:1], ALU.add))

            def n_rstd(pool, x):
                POOLN.after(pool, "ve", x.n)
                DVEN.after(pool, "xn", x.n - 1)
                POOLN.done("rstd", pool.tensor_tensor(rstd1[:], ve1[:], neghalf[:, 0:1], ALU.pow))

            def n_lo(pool, x):
                DVEN.after(pool, "hi", x.n)
                PEA.after(pool, "ft3", x.g - 2)
                POOLN.done("lo", pool.tensor_tensor(h_lo[:, x.q, :, x.tok], hf[:, x.t % 2],
                                                    h_hi[:, x.q, :, x.tok].bitcast(F32), ALU.subtract))

            def xdt_(pool, x):
                ACTB.after(pool, "xt", x.n)
                DVEA.after(pool, "dt", x.g)
                PEB.after(pool, "ydiag", x.n - 1)
                POOLB.done("xdt", pool.tensor_tensor(xdt[:], xt[:], spread(dt[:, x.q, x.t], NH, HD), ALU.mult))

            def xs_(pool, x):
                ACTA.after(pool, "e3", x.g)
                POOLB.after(pool, "xdt", x.n)
                PEB.after(pool, "state", x.n - 1)
                POOLB.done("xs", pool.tensor_tensor(xs[:], xdt[:], spread(e3[:, x.q, 1, x.t], NH, HD), ALU.mult))

            def xd_(pool, x):
                POOLB.after(pool, "xdt", x.n)
                POOLB.done("xd", pool.tensor_tensor(xt[:], xt[:], spread(d_rep[:], NH, HD), ALU.mult))

            def scd_(pool, x):
                POOLE.after(pool, "all", x.n - 3)
                state_ready(pool, x)
                PEB.after(pool, "yoff", x.n - 1)
                POOLB.after(pool, "scd", x.n - 1)
                POOLB.done("scd", pool.tensor_tensor(state_of(x), state_before(x), spread(e3[:, x.q, 2, x.t], NH, HD), ALU.mult))

            def y2_(pool, x):
                DVEB.after(pool, "y1", x.n)
                POOLB.after(pool, "xd", x.n)
                POOLB.done("y2", pool.tensor_tensor(y4[:, x.t % 2], y4[:, x.t % 2], xt[:], ALU.add))

            def c_ms(pool, x):
                ACTB.after(pool, "sq", x.n)
                POOLC.after(pool, "rs", x.n - 1)
                POOLC.done("ms", pool.tensor_tensor(ms[:], ssq[:, x.t % 2:x.t % 2 + 1], eps[:, 0:1], ALU.add))

            def c_rs(pool, x):
                POOLC.after(pool, "ms", x.n)
                DVEC.after(pool, "o1", x.n - 1)
                POOLC.done("rs", pool.tensor_tensor(rs[:], ms[:], neghalf[:, 0:1], ALU.pow))

            def c_x2(pool, x):
                DVEC.after(pool, "o1", x.n)
                pool.wait_ge(s_xres[x.t % 2], 8 * (x.n - x.t % 2) + 16)
                POOLC.done("x2", pool.tensor_tensor(x2[:, x.t % 2], x2[:, x.t % 2], xres[:, x.t % 2], ALU.add))

            def c_ve(pool, x):
                DVEC.after(pool, "mv", x.n)
                POOLC.after(pool, "rstd", x.n - 1)
                POOLC.done("ve", pool.tensor_tensor(ve2[:], mv2[:, 1:2], eps[:, 0:1], ALU.add))

            def c_rstd(pool, x):
                POOLC.after(pool, "ve", x.n)
                DVEC.after(pool, "xn", x.n - 1)
                POOLC.done("rstd", pool.tensor_tensor(rstd2[:], ve2[:], neghalf[:, 0:1], ALU.pow))

            def c_lo(pool, x):
                DVEC.after(pool, "hi", x.n)
                PEE.after(pool, "e4", x.n - 2)
                POOLC.done("lo", pool.tensor_tensor(h2_lo[:, x.t % 2], h2f[:], h2_hi[:, x.t % 2].bitcast(F32), ALU.subtract))

            def e_34(pool, x):
                ACTE.after(pool, "ex4", x.n)
                POOLE.done("a34", pool.tensor_tensor(ex[:, 0], ex[:, 0], ex[:, 1], ALU.add))

            def e_56(pool, x):
                ACTE.after(pool, "ex6", x.n)
                POOLE.done("a56", pool.tensor_tensor(ex[:, 2], ex[:, 2], ex[:, 3], ALU.add))

            def e_3456(pool, x):
                POOLE.after(pool, "a56", x.n)
                POOLE.done("a3456", pool.tensor_tensor(ex[:, 0], ex[:, 0], ex[:, 2], ALU.add))

            def e_all(pool, x):
                DVEE.after(pool, "bias", x.n)
                POOLE.after(pool, "a3456", x.n)
                POOLE.done("all", pool.tensor_tensor(ex[:, 0], ex[:, 0], eacc[:, 0], ALU.add))

            def e_og(pool, x):
                if isinstance(x.n, int):
                    POOLE.after(pool, "all", x.n)
                POOLE.done("og", pool.tensor_tensor(ex[:, 0], ex[:, 0], gate_of(x.batch, 1), ALU.mult))

            def e_out(pool, x):
                POOLE.after(pool, "og", x.n)
                if not isinstance(x.n, int) or x.n >= 2:
                    pool.wait_ge(s_out[x.t % 2], 8 * (x.n - x.t % 2))
                POOLE.done("out", pool.tensor_tensor(outb[:, x.t % 2], ex[:, 0], x2[:, x.t % 2], ALU.add))

            run(pool, POOL_ORDER,
                {"n_ve": n_ve, "n_rstd": n_rstd, "n_lo": n_lo, "xdt": xdt_, "xs": xs_, "xd": xd_, "scd": scd_, "y2": y2_, "ms": c_ms, "rs": c_rs,
                 "x2": c_x2, "ve": c_ve, "rstd": c_rstd, "lo": c_lo, "a34": e_34, "a56": e_56, "a3456": e_3456, "all": e_all, "og": e_og, "out": e_out})

        @block.scalar
        def _(act):
            loaded(act, s_small)
            ACT0.done("thc", act.activation(scT[:], cT[:], ACT.Tanh, scale=0.5))
            ACT0.done("expa", act.activation(expa[:], a_rep[:], ACT.Exp))
            for b in range(NB):
                PE0.after(act, f"g{b}", 0)
                ACT0.done(f"g{b}", act.activation(gates[:, b].rearrange("p a n -> p (a n)"), pe_[b % 2][:], ACT.Copy))

            def n_h(act, x):
                PEN.after(act, "hT", x.n)
                DVEN.after(act, "hi", x.n - 2)
                POOLN.after(act, "lo", x.n - 2)
                for k in range(KT):
                    ACTN.done(f"h{k}", act.activation(hf[:, x.t % 2, k], pa[HT_BANK[x.t]][:, k * P:(k + 1) * P], ACT.Identity,
                                                      bias=par1[:, 0, k:k + 1], scale=par1[:, 1, k:k + 1]))

            def z(i):
                def piece(act, x):
                    PEA.after(act, f"z{i}", x.g)
                    if i == 0:
                        DVEB.after(act, "y4", T * (x.g - 2) + T - 1)
                    for half in range(2):
                        ACTA.done(f"tz{i}{'ab'[half]}", act.activation(
                            gz[:, x.q, i, half * ZH:(half + 1) * ZH], pa[half][:, 0:ZH], ACT.Tanh))
                return piece

            def raws(f):
                def piece(act, x):
                    b = pa[BANK[f"ft{f}"]]
                    ACTA.after(act, f"hist{f}", x.g - 1)
                    PEA.after(act, f"ft{f}", x.g)
                    two_back(act, DVEA, "silu", f, x.g)
                    ACTA.done(f"raw{f}", act.activation(raw[:, turn(f), H:], b[:], ACT.Copy))
                    which = (x.p % (GPB // 2)) if x.q == 0 else 1
                    ACTA.done(f"halo{f}", act.activation(raw[:, turn(f), 0:H].rearrange("p (a n) -> p a n", a=1),
                                                         hist[:, bass.ds(which, 1), f], ACT.Copy))
                    ACTA.done(f"acc{f}", act.activation(acc[:, turn(f)], b[:], ACT.Identity,
                                                        bias=cb[:, f:f + 1], scale=cw[:, f, H:H + 1]))
                    ACTA.after(act, f"halo{f}", x.g)
                    ACTA.done(f"hist{f}", act.activation(hist[:, 1, f], b[:, GT - H:], ACT.Copy))
                return piece

            def tanh(f):
                def piece(act, x):
                    DVEA.after(act, f"tap{f}c", x.g)
                    ACTA.done(f"th{f}", act.activation(raw[:, turn(f), H:], acc[:, turn(f)], ACT.Tanh))
                return piece

            def exp_u(act, x):
                DVEA.after(act, "nabs", x.g)
                DVEA.after(act, "nc1", x.g - 1)
                ACTA.done("u", act.activation(u[:], nabs[:], ACT.Exp))

            def ln_w(act, x):
                DVEA.after(act, "w1", x.g)
                DVEA.after(act, "sp1", x.g - 1)
                ACTA.done("ln", act.activation(lnw[:], w1[:], ACT.Ln))

            def decays(act, x):
                DVEA.after(act, "dcs", x.g)
                ACTA.done("e3", act.activation(e3[:, x.q], e3in[:], ACT.Exp))

            def cs_rows(act, x):
                PEA.after(act, "csT", x.g)
                ACTA.done("csT", act.activation(csT[:, x.q].rearrange("p t n -> p (t n)"), pa1_bf[0:3 * NH, 0:GT], ACT.Copy))

            def bt_(act, x):
                PEB.after(act, "G", x.n)
                PEB.after(act, "state", x.n - 1)
                ACTB.done("bt", act.activation(bt[:], py[:, P:2 * P], ACT.Copy))

            def decay(h0, h1):
                def step(act, x):
                    PEB.after(act, "D", x.n)
                    DVEB.after(act, "M", x.n - 1)
                    for h in range(h0, h1):
                        ACTB.done(f"L{h}", act.activation(lm[:, h], pd[h // 4][:, h % 4 * P:(h % 4 + 1) * P], ACT.Relu,
                                                          scale=-1.0, bias=csc[:, x.q, x.t, h:h + 1]))
                return step

            def decay_exp(act, x):
                ACTB.after(act, f"L{NH - 1}", x.n)
                ACTB.done("L", act.activation(lm[:].rearrange("p h n -> p (h n)"), lm[:].rearrange("p h n -> p (h n)"),
                                              ACT.Exp, scale=-1.0))

            def xt_(act, x):
                PEB.after(act, "xT", x.n)
                POOLB.after(act, "y2", x.n - 1)
                ACTB.done("xt", act.activation(xt[:], px[:], ACT.Copy))

            def sq_(act, x):
                DVEB.after(act, "y4", x.n)
                POOLC.after(act, "ms", x.n - 2)
                ACTB.done("sq", act.activation(ysq[:], y4[:, x.t % 2], ACT.Square, scale=DI ** -0.5,
                                               accum_out=ssq[:, x.t % 2:x.t % 2 + 1]))

            def yT_(act, x):
                PEC.after(act, "yT", x.n)
                PEC.after(act, "wout", x.n - 1)
                ACTC.done("yT", act.activation(yT_hi[:].rearrange("p f n -> p (f n)"), pe_[0][:], ACT.Copy))

            def h2(act, x):
                PEC.after(act, "h2T", x.n)
                DVEC.after(act, "hi", x.n - 1)
                POOLC.after(act, "lo", x.n - 1)
                for k in range(KT):
                    ACTC.done(f"h{k}", act.activation(h2f[:, k], pe_[1][:, k * P:(k + 1) * P], ACT.Identity,
                                                      bias=par2[:, 0, k:k + 1], scale=par2[:, 1, k:k + 1]))

            def exp_(act, x):
                DVEE.after(act, "max", x.n)
                DVEE.after(act, "pr", x.n - 1)
                ACTE.done("exp", act.activation(pexp[:], lgt[:], ACT.Exp, bias=nmax[:], accum_out=sums_[:, 0:1]))

            def expert_pair(e0, bank_, product):
                def step(act, x):
                    DVEE.after(act, "wg", x.n)
                    PEE.after(act, product, x.n)
                    POOLE.after(act, "out" if e0 == 3 else "a3456", x.n - 1)
                    for e in (e0, e0 + 1):
                        ACTE.done(f"ex{e}", act.activation(ex[:, e - 3], pe_[bank_][:, (e - e0) * DM:(e - e0 + 1) * DM],
                                                           ACT.Copy, scale=wg[:, e:e + 1]))
                return step

            def ex0(act, x):
                DVEE.after(act, "wg", x.n)
                POOLE.after(act, "all", x.n - 1)
                ACTE.done("ex0", act.activation(eacc[:, 0], pe_[1][:, NE:NE + DM], ACT.Copy, scale=wg[:, 0:1]))

            def wT_(act, x):
                PEE.after(act, "wT", x.n)
                PEE.after(act, "e4", x.n - 1)
                ACTE.done("wT", act.activation(wgT[:], pe_[0][0:3 * NE, 0:P], ACT.Copy))

            run(act, ACT_ORDER,
                {"n_h": n_h, "bt": bt_, "L03": decay(0, 4), "L47": decay(4, NH), "L": decay_exp, "xt": xt_, "sq": sq_, "yT": yT_, "h2": h2,
                 "exp": exp_, "ex0": ex0, "ex34": expert_pair(3, 0, "e2"), "ex56": expert_pair(5, 1, "e3"), "wT": wT_, "u": exp_u, "ln": ln_w, "decays": decays, "csT": cs_rows}
                | {f"tz{i}": z(i) for i in range(T)} | {f"raw{f}": raws(f) for f in FTS} | {f"th{f}": tanh(f) for f in FTS})

        @block.vector
        def _(dve):
            D0 = DVE0.done

            def own(name):
                DVE0.after(dve, name, 0)
            loaded(dve, s_small)
            D0("hc", dve.tensor_scalar(hc[:], cT[:], 0.5, None, ALU.mult))
            own("hc")
            ACT0.after(dve, "thc", 0)
            D0("scT", dve.scalar_tensor_tensor(out=scT[:], in0=scT[:], scalar=1.0, in1=hc[:], op0=ALU.add, op1=ALU.mult))
            PE0.after(dve, "grow", 0)
            D0("sgn", dve.tensor_scalar(gsgn, pe_[0][0:NB, :], 0.0, 2.0, ALU.is_ge, ALU.mult))
            D0("abs", dve.tensor_scalar(gabs, pe_[0][0:NB, :], -1.0, None, ALU.mult))
            own("abs")
            D0("max", dve.scalar_tensor_tensor(out=gabs, in0=gabs, scalar=0.25, in1=pe_[0][0:NB, :], op0=ALU.max, op1=ALU.max))
            own("max")
            D0("grow", dve.scalar_tensor_tensor(out=grow, in0=gsgn, scalar=-1.0, in1=gabs, op0=ALU.add, op1=ALU.mult))
            PE0.after(dve, "mod", 0)
            for j in range(4):
                for k in range(KT):
                    c0 = (j * KT + k) * NB
                    D0(f"m{j}{k}", dve.tensor_scalar(modT[:, :, j, k], pd[0][:, c0:c0 + NB], float(j % 2), None, ALU.add))
            D0("cw", dve.tensor_scalar(cw[:], cw[:], 0.5, None, ALU.mult))
            D0("cb", dve.tensor_scalar(cb[:], cb[:], 0.5, None, ALU.mult))
            ACT0.after(dve, "expa", 0)
            D0("a_rep", dve.tensor_scalar(a_rep[:], expa[:], -1.0, None, ALU.mult))
            loaded(dve, s_proj)
            for i, (a, b, f) in enumerate(((0, ZH, 0.5), (ZH, ZD, 1.0), (ZD, CX, 0.5), (CX, WC, 1.0))):
                D0(f"w{i}hi", dve.tensor_scalar(w_hi[:, :, a:b], stage_w[:, :, a:b], f, None, ALU.mult))
                own(f"w{i}hi")
                D0(f"w{i}lo", dve.scalar_tensor_tensor(out=w_lo[:, :, a:b], in0=stage_w[:, :, a:b], scalar=f,
                                                       in1=w_hi[:, :, a:b].bitcast(F32), op0=ALU.mult, op1=ALU.subtract))
            for k in range(XT):
                D0(f"wo{k}hi", dve.tensor_scalar(wo_hi[:, k], stage_wo[:, k], nw[:, k:k + 1], None, ALU.mult))
                own(f"wo{k}hi")
                D0(f"wo{k}lo", dve.scalar_tensor_tensor(out=wo_lo[:, k], in0=stage_wo[:, k], scalar=nw[:, k:k + 1],
                                                        in1=wo_hi[:, k].bitcast(F32), op0=ALU.mult, op1=ALU.subtract))
            loaded(dve, s_exp)
            D0("ghi", dve.tensor_copy(e_hi[:, :, 0:NE], stage_g))
            D0("ehi", dve.tensor_copy(e_hi[:, :, NE:EC], stage_e))
            own("ehi")
            D0("glo", dve.tensor_tensor(e_lo[:, :, 0:NE], stage_g, e_hi[:, :, 0:NE].bitcast(F32), ALU.subtract))
            D0("elo", dve.tensor_tensor(e_lo[:, :, NE:EC], stage_e, e_hi[:, :, NE:EC].bitcast(F32), ALU.subtract))
            D0("bhi", dve.tensor_copy(b_hi.bitcast(F32R), stage_b))
            own("bhi")
            D0("blo", dve.tensor_tensor(b_lo, stage_b, b_hi, ALU.subtract))
            own("blo")
            POOL0.after(dve, "is_hi", 0)
            D0("blo0", dve.tensor_scalar(b_lo, b_lo, is_lo[:, 0:1], None, ALU.mult))
            own("blo0")
            D0("eb3", dve.scalar_tensor_tensor(out=eb3[:], in0=b_hi, scalar=is_lo[:, 1:2], in1=b_lo, op0=ALU.mult, op1=ALU.add))
            own("eb3")
            POOL0.after(dve, "hist", 0)
            ACT0.after(dve, f"g{NB - 1}", 0)

            def n_st(dve, x):
                dve.wait_ge(s_xin[x.t], 16 * (x.g + 1))
                DVEN.done("st", dve.bn_stats(st1[:], xin[:, x.t]))

            def n_mv(dve, x):
                ACTN.after(dve, "h1", x.n - 1)
                POOLN.after(dve, "ve", x.n - 1)
                DVEN.after(dve, "st", x.n)
                DVEN.done("par", dve.tensor_scalar(par1[:].rearrange("p a k -> p (a k)"), mods_of(x.batch, 0), 1.0, None, ALU.mult))
                DVEN.done("mv", dve.bn_aggr(mv1[:], st1[:]))

            def n_xn(dve, x):
                POOLN.after(dve, "rstd", x.n)
                DVEN.done("xn", dve.tensor_scalar(xin[:, x.t], xin[:, x.t], mv1[:, 0:1], rstd1[:], ALU.subtract, ALU.mult))

            def n_hi(dve, x):
                ACTN.after(dve, "h1", x.n)
                PEA.after(dve, "ft3", x.g - 2)
                DVEN.done("hi", dve.tensor_copy(h_hi[:, x.q, :, x.tok], hf[:, x.t % 2]))

            def z(i):
                def piece(dve, x):
                    for half in range(2):
                        ACTA.after(dve, f"tz{i}{'ab'[half]}", x.g)
                        g_ = gz[:, x.q, i, half * ZH:(half + 1) * ZH]
                        DVEA.done(f"gz{i}{'ab'[half]}", dve.scalar_tensor_tensor(
                            out=g_, in0=g_, scalar=1.0, in1=pa[half][:, 0:ZH], op0=ALU.add, op1=ALU.mult))
                    DVEA.done(f"dtb{i}", dve.tensor_tensor(v[:, i], pa[0][:, ZH:ZD], dtb_rep[:], ALU.add))
                return piece

            def tap(f, j):
                def piece(dve, x):
                    if j:
                        DVEA.after(dve, f"tap{f}{'abc'[j - 1]}", x.g)
                    else:
                        ACTA.after(dve, f"hist{f}", x.g)
                    DVEA.done(f"tap{f}{'abc'[j]}", dve.scalar_tensor_tensor(
                        out=acc[:, turn(f)], in0=raw[:, turn(f), j:j + GT], scalar=cw[:, f, j:j + 1], in1=acc[:, turn(f)],
                        op0=ALU.mult, op1=ALU.add))
                return piece

            def silu(f):
                def piece(dve, x):
                    ACTA.after(dve, f"th{f}", x.g)
                    PEB.after(dve, "yoff", T * (x.g - 2) + T - 1)
                    DVEA.done(f"silu{f}", dve.scalar_tensor_tensor(
                        out=feat[:, x.q, f], in0=raw[:, turn(f), H:], scalar=1.0, in1=acc[:, turn(f)], op0=ALU.add, op1=ALU.mult))
                return piece

            def nabs_(dve, x):
                return dve.scalar_tensor_tensor(out=nabs[:], in0=v[:], scalar=-1.0, in1=v[:], op0=ALU.mult, op1=ALU.min)

            def w1_(dve, x):
                ACTA.after(dve, "u", x.g)
                return dve.tensor_scalar(w1[:], u[:], 1.0, None, ALU.add)

            def sp1_(dve, x):
                ACTA.after(dve, "ln", x.g)
                return dve.scalar_tensor_tensor(out=sp1[:], in0=v[:], scalar=0.0, in1=lnw[:], op0=ALU.max, op1=ALU.add)

            def dt_(dve, x):
                POOLB.after(dve, "xdt", T * (x.g - 2) + T - 1)
                return dve.tensor_tensor(dt[:, x.q], sp1[:], nc1[:], ALU.subtract)

            def dA_(dve, x):
                PEA.after(dve, "cs", x.g - 1)
                return dve.tensor_tensor(dA[:], dt[:, x.q], rep(a_rep[:], T, NH), ALU.mult)

            def cs_(dve, x):
                PEA.after(dve, "cs", x.g)
                ACTA.after(dve, "e3", x.g - 1)
                return dve.tensor_copy(e3in[:, 0:3:2], pa[0][:, 0:2 * T * NH].rearrange("p (a t h) -> p a t h", a=2, t=T))

            def csc_(dve, x):
                ACTB.after(dve, f"L{NH - 1}", T * (x.g - 2) + T - 1)
                return dve.tensor_copy(csc[:, x.q], e3in[:, 0])

            def p0_(dve, x):
                PEA.after(dve, "csT", x.g - 1)
                return dve.tensor_copy(parts[:, :, 0], e3in[:, 0])

            def a_step(name, before, op):
                def step(dve, x):
                    if before:
                        DVEA.after(dve, before, x.g)
                    DVEA.done(name, op(dve, x))
                return step

            a_steps = {name: a_step(name, before, op) for name, before, op in (
                ("nabs", "dtb3", nabs_),
                ("w1", None, w1_),
                ("nc1", "w1", lambda dve, x: dve.scalar_tensor_tensor(out=nc1[:], in0=w1[:], scalar=1.0, in1=u[:],
                                                                      op0=ALU.subtract, op1=ALU.subtract)),
                ("sp1", None, sp1_),
                ("dt", "sp1", dt_),
                ("dA", "dt", dA_),
                ("cs", None, cs_),
                ("dcs", "cs", lambda dve, x: dve.tensor_tensor(e3in[:, 1], e3in[:, 2], e3in[:, 0], ALU.subtract)),
                ("csc", "cs", csc_),
                ("p0", "cs", p0_),
                ("r1", "p0", lambda dve, x: dve.tensor_tensor(r1[:], e3in[:, 0], parts[:, :, 0], ALU.subtract)),
                ("p1", "r1", lambda dve, x: dve.tensor_copy(parts[:, :, 1], r1[:])),
                ("p2", "p1", lambda dve, x: dve.tensor_tensor(parts[:, :, 2], r1[:], parts[:, :, 1], ALU.subtract)))}

            def sres_(dve, x):
                if x.q == 0 and x.t == 0:
                    DVEB.after(dve, "S", x.n - 1)
                    PEB.after(dve, "yoff", x.n - 2 * T)
                    POOLB.after(dve, "scd", x.n - 2 * T)
                    DVES.done("sres", dve.tensor_copy(sres[:].rearrange("p (a n) -> p a n", a=1),
                                                      zero_or_s[:, bass.ds(x.p % (GPB // 2), 1)]))

            def gs_(dve, x):
                ACTB.after(dve, "bt", x.n)
                DVEB.after(dve, "M", x.n - 1)
                DVEB.done("gs", dve.tensor_tensor(gs[:], py[:, 0:P], tri[:], ALU.mult))

            def M_(dve, x):
                ACTB.after(dve, "L", x.n)
                PEB.after(dve, "ydiag", x.n - 1)
                DVEB.after(dve, "gs", x.n)
                DVEB.done("M", dve.tensor_tensor(mm[:], lm[:], rep(gs[:], NH, P), ALU.mult))

            def y1_(dve, x):
                PEB.after(dve, "yoff", x.n)
                ACTA.after(dve, "e3", x.g)
                PEC.after(dve, "yT", x.n - 2)
                ACTB.after(dve, "sq", x.n - 2)
                DVEB.done("y1", dve.tensor_tensor(y4[:, x.t % 2], px[:], spread(e3[:, x.q, 0, x.t], NH, HD), ALU.mult))

            def y3_(dve, x):
                PEB.after(dve, "ydiag", x.n)
                POOLB.after(dve, "y2", x.n)
                DVEB.done("y3", dve.tensor_tensor(y4[:, x.t % 2], py[:], y4[:, x.t % 2], ALU.add))

            def y4_(dve, x):
                DVEB.after(dve, "y3", x.n)
                DVEA.after(dve, "gz3b", x.g)
                DVEB.done("y4", dve.tensor_tensor(y4[:, x.t % 2], y4[:, x.t % 2], gz[:, x.q, x.t], ALU.mult))

            def S_(dve, x):
                PEB.after(dve, "state", x.n)
                POOLB.after(dve, "scd", x.n)
                DVEB.done("S", dve.tensor_tensor(state_of(x), state_of(x), px[:], ALU.add))

            def yTlo_(dve, x):
                ACTC.after(dve, "yT", x.n)
                PEC.after(dve, "wout", x.n - 1)
                DVEC.done("yTlo", dve.tensor_tensor(yT_lo[:].rearrange("p f n -> p (f n)"), pe_[0][:],
                                                    yT_hi[:].rearrange("p f n -> p (f n)").bitcast(F32), ALU.subtract))

            def o1_(dve, x):
                PEC.after(dve, "wout", x.n)
                POOLC.after(dve, "rs", x.n)
                POOLE.after(dve, "out", x.n - 2)
                DVEC.done("o1", dve.scalar_tensor_tensor(out=x2[:, x.t % 2], in0=pe_[0][:, 0:DM], scalar=rs[:],
                                                         in1=gate_of(x.batch, 0), op0=ALU.mult, op1=ALU.mult))

            def st_(dve, x):
                POOLC.after(dve, "x2", x.n)
                DVEC.done("st", dve.bn_stats(st2[:], x2[:, x.t % 2]))

            def mv_(dve, x):
                ACTC.after(dve, "h1", x.n - 1)
                POOLC.after(dve, "ve", x.n - 1)
                DVEC.after(dve, "st", x.n)
                DVEC.done("par", dve.tensor_scalar(par2[:].rearrange("p a k -> p (a k)"), mods_of(x.batch, 2), 1.0, None, ALU.mult))
                DVEC.done("mv", dve.bn_aggr(mv2[:], st2[:]))

            def xn_(dve, x):
                POOLC.after(dve, "rstd", x.n)
                PEC.after(dve, "h2T", x.n - 1)
                DVEC.done("xn", dve.tensor_scalar(xn2[:], x2[:, x.t % 2], mv2[:, 0:1], rstd2[:], ALU.subtract, ALU.mult))

            def hi_(dve, x):
                ACTC.after(dve, "h1", x.n)
                PEE.after(dve, "e4", x.n - 2)
                DVEC.done("hi", dve.tensor_copy(h2_hi[:, x.t % 2], h2f[:]))

            E = DVEE.done

            def e_step(name, before, op):
                def step(dve, x):
                    if before:
                        DVEE.after(dve, before, x.n)
                    E(name, op(dve, x))
                return step

            def lg(dve, x):
                PEE.after(dve, "e0", x.n)
                ACTE.after(dve, "exp", x.n - 1)
                return dve.tensor_tensor(lgt[:], pe_[1][:, 0:NE], gb_rep[:], ALU.add)

            def rp_(dve, x):
                ACTE.after(dve, "exp", x.n)
                return dve.reciprocal(sums_[:, 1:2], sums_[:, 0:1])

            def wg_(dve, x):
                ACTE.after(dve, "ex6", x.n - 1)
                return dve.tensor_scalar(wg[:], wsel[:], sums_[:, 3:4], None, ALU.mult)

            def wghi(dve, x):
                PEE.after(dve, "wT", x.n - 1)
                return dve.tensor_copy(wg3[:, 0:2], rep(wg[:], 2, NE))

            def acc_e(e, src):
                def op(dve, x):
                    PEE.after(dve, "e1" if e < 3 else "e4", x.n)
                    if e == 1:
                        ACTE.after(dve, "ex0", x.n)
                    return dve.scalar_tensor_tensor(out=eacc[:, e % 2], in0=src, scalar=wg[:, e:e + 1],
                                                    in1=eacc[:, (e + 1) % 2], op0=ALU.mult, op1=ALU.add)
                return op

            e_steps = {name: e_step(name, before, op) for name, before, op in (
                ("lg", None, lg),
                ("max", "lg", lambda dve, x: dve.tensor_reduce(nmax[:], lgt[:], AX.X, ALU.max, negate=True)),
                ("rp", None, rp_),
                ("pr", "rp", lambda dve, x: dve.tensor_scalar(pr[:], pexp[:], sums_[:, 1:2], None, ALU.mult)),
                ("wsel", "pr", lambda dve, x: dve.scalar_tensor_tensor(out=wsel[:], in0=pr[:], scalar=THRESHOLD, in1=pr[:],
                                                                       op0=ALU.is_ge, op1=ALU.mult)),
                ("rw", "wsel", lambda dve, x: dve.tensor_reduce(sums_[:, 2:3], wsel[:], AX.X, ALU.add)),
                ("rz", "rw", lambda dve, x: dve.scalar_tensor_tensor(out=sums_[:, 2:3], in0=sums_[:, 2:3], scalar=0.0,
                                                                     in1=sums_[:, 2:3], op0=ALU.is_equal, op1=ALU.add)),
                ("rr", "rz", lambda dve, x: dve.reciprocal(sums_[:, 3:4], sums_[:, 2:3])),
                ("wg", "rr", wg_),
                ("wghi", "wg", wghi),
                ("wglo", "wghi", lambda dve, x: dve.tensor_tensor(wg3[:, 2], wg[:], wg3[:, 1].bitcast(F32), ALU.subtract)),
                ("acc1", None, acc_e(1, pe_[1][:, 0:DM])),
                ("acc2", "acc1", acc_e(2, pe_[1][:, DM:2 * DM])),
                ("acc7", "acc2", acc_e(7, pe_[0][:, 0:DM])),
                ("bias", "acc7", lambda dve, x: dve.tensor_tensor(eacc[:, 0], pe_[0][:, DM:2 * DM], eacc[:, 1], ALU.add)))}

            run(dve, DVE_ORDER,
                {"n_st": n_st, "n_mv": n_mv, "n_xn": n_xn, "n_hi": n_hi, "sres": sres_, "gs": gs_, "M": M_, "y1": y1_, "y3": y3_, "y4": y4_,
                 "S": S_, "yTlo": yTlo_, "o1": o1_, "st": st_, "mv": mv_, "xn": xn_, "hi": hi_}
                | e_steps | a_steps
                | {f"gz{i}": z(i) for i in range(T)} | {f"t{f}{'abc'[j]}": tap(f, j) for f in FTS for j in range(H)}
                | {f"silu{f}": silu(f) for f in FTS})

        @block.tensor
        def _(pe):
            def mm_(o, l, r, start, stop):
                return pe.matmul(o, lhsT=l, rhs=r, start=start, stop=stop, skip_group_check=True)

            def split(o, ahi, alo, bhi, blo, cols, kt=KT):
                for k in range(kt):
                    for i, (l, r) in enumerate(((ahi(k), bhi), (ahi(k), blo), (alo(k), bhi))):
                        last = mm_(o, l, r[:, k, cols], k == 0 and i == 0, k == kt - 1 and i == 2)
                return last

            loaded(pe, s_small)
            POOL0.after(pe, "hist", 0)
            DVE0.after(pe, "scT", 0)
            for j, m in enumerate((2, 5)):
                for k in range(KT):
                    last = mm_(pe_[0][0:NB, j * DM:(j + 1) * DM], scT[:, k], stage_m[:, k, m * DM:(m + 1) * DM], k == 0, k == KT - 1)
            PE0.done("grow", last)
            for j, m in enumerate((0, 1, 3, 4)):
                for c in range(KT):
                    o = (j * KT + c) * NB
                    for k in range(KT):
                        last = mm_(pd[0][:, o:o + NB], stage_m[:, k, m * DM + c * P:m * DM + (c + 1) * P], scT[:, k], k == 0, k == KT - 1)
            PE0.done("mod", last)
            DVE0.after(pe, "grow", 0)
            for b in range(NB):
                if b >= 2:
                    ACT0.after(pe, f"g{b - 2}", 0)
                PE0.done(f"g{b}", mm_(pe_[b % 2][:], ident[0:NB, b:b + 1].to_broadcast([NB, P]), grow, True, True))
            DVE0.after(pe, "eb3", 0)

            def hT_(pe, x):
                DVEN.after(pe, "xn", x.n)
                ACTN.after(pe, "h1", x.n - 1)
                stage, name = ((DVEA, "dtb1"), (DVEA, "dtb3"), (ACTA, "csT"), (ACTA, "hist2"))[x.t]
                stage.after(pe, name, x.g - 1)
                for k in range(KT):
                    last = pe.transpose(pa[HT_BANK[x.t]][:, k * P:(k + 1) * P], xin[:, x.t, k * P:(k + 1) * P], ident[:])
                PEN.done("hT", last)

            def z(i):
                def piece(pe, x):
                    if i == 0:
                        for t in range(T):
                            DVEN.after(pe, "hi", T * x.g + t)
                        POOLN.after(pe, "lo", T * x.g + T - 1)
                        ACTN.after(pe, "h1", T * (x.g + 1) - 1)
                        ACTA.after(pe, "hist3", x.g - 1)
                    else:
                        DVEA.after(pe, f"dtb{i - 1}", x.g)
                    if i == 2:
                        ACTA.after(pe, "hist5", x.g)
                        ACTN.after(pe, "h1", T * (x.g + 1))
                    tok = slice(i * P, (i + 1) * P)
                    split(pa[0][:, 0:ZD], lambda k: h_hi[:, x.q, k, tok], lambda k: h_lo[:, x.q, k, tok], w_hi, w_lo, slice(0, ZD))
                    PEA.done(f"z{i}", split(pa[1][:, 0:ZH], lambda k: h_hi[:, x.q, k, tok], lambda k: h_lo[:, x.q, k, tok],
                                            w_hi, w_lo, slice(ZD, CX)))
                return piece

            def ft(f):
                stage, name = {5: (DVEA, "dtb1"), 4: (DVEA, "dtb3"), 0: (ACTN, 1), 1: (DVEA, "cs"), 2: (ACTA, "hist1"),
                               3: (ACTN, 2)}[f]

                def piece(pe, x):
                    if stage is ACTN:
                        stage.after(pe, "h1", T * (x.g + 1) + name)
                    else:
                        stage.after(pe, name, x.g)
                    cols = slice(CX + f * P, CX + (f + 1) * P)
                    for k in range(KT):
                        for i, (l, r) in enumerate(((w_hi, h_hi), (w_hi, h_lo), (w_lo, h_hi))):
                            last = mm_(pa[BANK[f"ft{f}"]][:], l[:, k, cols], r[:, x.q, k], k == 0 and i == 0, k == KT - 1 and i == 2)
                    PEA.done(f"ft{f}", last)
                return piece

            def cs(pe, x):
                ACTA.after(pe, "hist4", x.g)
                DVEA.after(pe, "dA", x.g)
                flat = dA[:].rearrange("p t h -> p (t h)")
                mm_(pa[0][:, 0:T * NH], tri[:], flat, True, True)
                PEA.done("cs", mm_(pa[0][:, T * NH:2 * T * NH], all_ones, flat, True, True))

            def csT_(pe, x):
                ACTA.after(pe, "hist0", x.g)
                DVEA.after(pe, "p2", x.g)
                for t in range(T):
                    last = pe.transpose(pa1_bf[0:3 * NH, t * P:(t + 1) * P], parts[:, t].rearrange("p a h -> p (a h)"), identb[:])
                PEA.done("csT", last)

            def D_(pe, x):
                ACTA.after(pe, "csT", x.g)
                ACTB.after(pe, f"L{NH - 1}", x.n - 1)
                for h in range(NH):
                    last = mm_(pd[h // 4][:, h % 4 * P:(h % 4 + 1) * P], sel[:, h], csT[:, x.q, x.t], True, True)
                PEB.done("D", last)

            def G_(pe, x):
                DVEA.after(pe, "silu5", x.g)
                DVEA.after(pe, "silu4", x.g)
                DVEB.after(pe, "y3", x.n - 1)
                mm_(py[:, 0:P], feat[:, x.q, XT, x.tok], feat[:, x.q, XT + 1, x.tok], True, True)
                PEB.done("G", pe.transpose(py[:, P:2 * P], feat[:, x.q, XT, x.tok], ident[:]))

            def xT_(pe, x):
                DVEA.after(pe, "silu3", x.g)
                DVEB.after(pe, "S", x.n - 1)
                for f in range(XT):
                    last = pe.transpose(px[:, f * P:(f + 1) * P], feat[:, x.q, f, x.tok], ident[:])
                PEB.done("xT", last)

            def yoff_(pe, x):
                ACTB.after(pe, "xt", x.n)
                state_ready(pe, x)
                PEB.done("yoff", mm_(px[:], feat[:, x.q, XT + 1, x.tok], state_before(x), True, True))

            def ydiag_(pe, x):
                DVEB.after(pe, "M", x.n)
                POOLB.after(pe, "xdt", x.n)
                ACTB.after(pe, "bt", x.n)
                for h in range(NH):
                    last = mm_(py[:, h * HD:(h + 1) * HD], mm[:, h], xdt[:, h * HD:(h + 1) * HD], True, True)
                PEB.done("ydiag", last)

            def state_(pe, x):
                POOLB.after(pe, "xs", x.n)
                DVEB.after(pe, "y1", x.n)
                PEB.done("state", mm_(px[:], bt[:], xs[:], True, True))

            def yT_(pe, x):
                DVEB.after(pe, "y4", x.n)
                DVEE.after(pe, "bias", x.n - 2)
                for f in range(XT):
                    last = pe.transpose(pe_[0][:, f * P:(f + 1) * P], y4[:, x.t % 2, f * P:(f + 1) * P], ident[:])
                PEC.done("yT", last)

            def wout_(pe, x):
                DVEC.after(pe, "yTlo", x.n)
                PEC.done("wout", split(pe_[0][:, 0:DM], lambda k: yT_hi[:, k], lambda k: yT_lo[:, k], wo_hi, wo_lo,
                                       slice(0, DM), XT))

            def h2T_(pe, x):
                DVEC.after(pe, "xn", x.n)
                DVEE.after(pe, "acc2", x.n - 1)
                for k in range(KT):
                    last = pe.transpose(pe_[1][:, k * P:(k + 1) * P], xn2[:, k * P:(k + 1) * P], ident[:])
                PEC.done("h2T", last)

            def experts(i, free):
                def step(pe, x):
                    a, b = (0, NE + DM) if i == 0 else (NE + DM * (2 * i - 1), min(EC, NE + DM * (2 * i + 1)))
                    bank_ = pe_[(1, 1, 0, 1, 0)[i]]
                    free(x)
                    if i == 3:
                        PEE.done("wT", pe.transpose(pe_[0][0:3 * NE, 0:P], wg3[:].rearrange("p a e -> p (a e)").bitcast(F32),
                                                        ident[:]))
                    last = split(bank_[:, 0:b - a], lambda k: h2_hi[:, x.t % 2, k], lambda k: h2_lo[:, x.t % 2, k],
                                 e_hi, e_lo, slice(a, b))
                    if i == 4:
                        last = mm_(bank_[:, DM:2 * DM], wgT[:], eb3[:], True, True)
                    PEE.done(f"e{i}", last)
                return step

            def free0(x):
                DVEC.after(pe, "hi", x.n)
                POOLC.after(pe, "lo", x.n)
                ACTE.after(pe, "ex6", x.n - 1)
                ACTC.after(pe, "h1", x.n)

            def free1(x):
                ACTE.after(pe, "ex0", x.n)

            def free2(x):
                DVEE.after(pe, "bias", x.n - 1)
                DVEC.after(pe, "o1", x.n + 1)

            def free3(x):
                ACTE.after(pe, "ex4", x.n)
                DVEE.after(pe, "acc2", x.n)
                ACTC.after(pe, "h1", x.n + 1)

            def free4(x):
                ACTE.after(pe, "wT", x.n)

            run(pe, PE_ORDER,
                {"hT": hT_, "D": D_, "G": G_, "xT": xT_, "yoff": yoff_, "ydiag": ydiag_, "state": state_, "yT": yT_,
                 "wout": wout_, "h2T": h2T_, "e0": experts(0, free0), "e1": experts(1, free1), "e2": experts(2, free2),
                 "e3": experts(3, free3), "e4": experts(4, free4), "cs": cs, "csT": csT_}
                | {f"z{i}": z(i) for i in range(T)} | {f"ft{f}": ft(f) for f in FTS})

_INS = ['L0_attn_hidden_states', 'L0_attn_W_in', 'L0_attn_conv_w', 'L0_attn_conv_b', 'L0_attn_dt_bias', 'L0_attn_A_log',
        'L0_attn_D', 'L0_attn_norm_w', 'L0_attn_W_out', 'L0_ffn_gate_w', 'L0_ffn_gate_b', 'L0_ffn_expert_w',
        'L0_ffn_expert_b', 'L0_c', 'L0_wmod']


def kernel(**inputs):
    import numpy as _np
    import concourse.bacc as _bacc
    from concourse import mybir as _mybir
    from concourse.bass_utils import run_bass_kernel_spmd as _run

    nc = _bacc.Bacc("TRN2", target_bir_lowering=False, num_devices=1)
    arrays, args = {}, []
    for name in _INS:
        a = _np.ascontiguousarray(inputs[name])
        arrays[f"in_{name}_dram"] = a
        args.append(nc.dram_tensor(f"in_{name}_dram", a.shape, _mybir.dt.from_np(a.dtype), kind="ExternalInput").ap())
    shape = inputs['L0_attn_hidden_states'].shape
    args.append(nc.dram_tensor("out_0_dram", shape, _mybir.dt.float32, kind="ExternalOutput").ap())
    adaln_mamba_moe(nc, *args)
    r = _run(nc, [arrays], core_ids=[0])
    return r.results[0]["out_0_dram"]
```
